# Optimizing a Trainium2 kernel written in Bass

```python
import numpy as np
import jax
import jax.numpy as jnp

def _softmax(x, axis=-1):
    return jax.nn.softmax(x, axis=axis)

def _gelu(x):
    return jax.nn.gelu(x, approximate=True)

def _silu(x):
    return jax.nn.silu(x)

def _sigmoid(x):
    return jax.nn.sigmoid(x)

def _layernorm(x, axis=-1, eps=1e-05):
    m = jnp.mean(x, axis=axis, keepdims=True)
    v = jnp.var(x, axis=axis, keepdims=True)
    return (x - m) / jnp.sqrt(v + eps)

def _scatter_add(tgt, idx, src, axis=0):
    return tgt.at[idx].add(src)

def _segment_sum(src, seg, n):
    return jax.ops.segment_sum(src, seg, n)
kernel_name = 'mk_perceiver_d1_seqx_r8_b7f3fa'

def setup_inputs(seed: int=0):
    np.random.seed(seed)
    _w = jnp.asarray

    def _rec_inputs():
        import jax
        import jax.numpy as jnp
        _rk = jax.random.key(seed)
        x = 7.22e-05 + 1 * jax.random.normal(jax.random.fold_in(_rk, 1), (16, 64, 128), jnp.float32)
        _lenS = 64 - jax.random.randint(jax.random.fold_in(_rk, 7), (16,), 0, max(1, 64 // 4) + 1, jnp.int32)
        _lenS2 = 1601 - jax.random.randint(jax.random.fold_in(_rk, 8), (16,), 0, max(1, 1601 // 4) + 1, jnp.int32)
        _ctx_1024P = jax.random.normal(jax.random.fold_in(_rk, 11), (16, 16, 128), jnp.float32)
        _ctx_1024c = jax.random.dirichlet(jax.random.fold_in(_rk, 511), 0.3 * jnp.ones((16,), jnp.float32), (16, 1601))
        _ctx_1024t = jnp.einsum('bsk,bkd->bsd', _ctx_1024c, _ctx_1024P)
        _ctx_1024t = _ctx_1024t * jax.lax.rsqrt(jnp.mean(jnp.square(_ctx_1024t)) + 1e-12) * 0.953939
        ctx_1024 = 4.13588e-05 + 0.999923 * (_ctx_1024t + 0.3 * jax.random.normal(jax.random.fold_in(_rk, 611), (16, 1601, 128), jnp.float32))
        return (x, ctx_1024)
    x, ctx_1024 = _rec_inputs()

    def _L0_xattn_setup():
        import jax, jax.numpy as jnp
        import numpy as np
        D_MODEL = 128
        NUM_HEADS = 16
        HEAD_DIM = D_MODEL // NUM_HEADS
        B, S = (4, 256)
        key = jax.random.key(seed)
        ks = jax.random.split(key, 11)
        scale = 1.0 / np.sqrt(D_MODEL)
        return {'query': jax.random.normal(ks[0], (B, S, D_MODEL), jnp.float32), 'key': jax.random.normal(ks[1], (B, S, D_MODEL), jnp.float32), 'value': jax.random.normal(ks[2], (B, S, D_MODEL), jnp.float32), 'Wq': jax.random.normal(ks[3], (D_MODEL, D_MODEL), jnp.float32) * scale, 'bq': jnp.zeros((D_MODEL,), jnp.float32), 'Wk': jax.random.normal(ks[4], (D_MODEL, D_MODEL), jnp.float32) * scale, 'bk': jnp.zeros((D_MODEL,), jnp.float32), 'Wv': jax.random.normal(ks[5], (D_MODEL, D_MODEL), jnp.float32) * scale, 'bv': jnp.zeros((D_MODEL,), jnp.float32), 'Wo': jax.random.normal(ks[6], (D_MODEL, D_MODEL), jnp.float32) * scale, 'bo': jnp.zeros((D_MODEL,), jnp.float32)}
    _L0_xattn_all = _L0_xattn_setup()
    _L0_xattn_in = {k: v for k, v in _L0_xattn_all.items() if k in ('Wq', 'bq', 'Wk', 'bk', 'Wv', 'bv', 'Wo', 'bo')}
    del _L0_xattn_all

    def _L0_attn_setup():
        import jax, jax.numpy as jnp
        import numpy as np
        from jax import lax
        D_MODEL = 128
        D_INNER = 256
        D_STATE = 64
        D_CONV = 4
        HEADDIM = 64
        NHEADS = D_INNER // HEADDIM
        CONV_DIM = D_INNER + 2 * D_STATE
        D_IN_PROJ = 2 * D_INNER + 2 * D_STATE + NHEADS
        D_FF = 4 * D_MODEL
        EPS = 1e-05

        def _layernorm(x, w, b):
            mu = jnp.mean(x, -1, keepdims=True)
            var = jnp.mean((x - mu) ** 2, -1, keepdims=True)
            return (x - mu) * lax.rsqrt(var + EPS) * w + b

        def _silu(x):
            return x * jax.nn.sigmoid(x)

        def _mamba2(x, in_proj_w, conv_w, conv_b, dt_bias, A_log, D_param, norm_w, out_proj_w):
            B, L, _ = x.shape
            zxbcdt = jnp.einsum('bld,ed->ble', x, in_proj_w)
            z = zxbcdt[..., :D_INNER]
            xBC = zxbcdt[..., D_INNER:D_INNER + CONV_DIM]
            dt_raw = zxbcdt[..., D_INNER + CONV_DIM:]
            dt = jax.nn.softplus(dt_raw + dt_bias)
            xp = jnp.pad(xBC, ((0, 0), (D_CONV - 1, 0), (0, 0)))
            xBC = sum((conv_w[:, k] * xp[:, k:k + L, :] for k in range(D_CONV))) + conv_b
            xBC = _silu(xBC)
            xs = xBC[..., :D_INNER].reshape(B, L, NHEADS, HEADDIM)
            Bm = xBC[..., D_INNER:D_INNER + D_STATE]
            Cm = xBC[..., D_INNER + D_STATE:]
            A = -jnp.exp(A_log)
            dA = jnp.exp(dt * A)
            dtx = dt[..., None] * xs

            def step(h, inp):
                dA_t, dtx_t, B_t, C_t = inp
                h = dA_t[:, :, None, None] * h + dtx_t[..., None] * B_t[:, None, None, :]
                y_t = jnp.einsum('bhpn,bn->bhp', h, C_t)
                return (h, y_t)
            h0 = jnp.zeros((B, NHEADS, HEADDIM, D_STATE), x.dtype)
            _, ys = lax.scan(step, h0, (jnp.swapaxes(dA, 0, 1), jnp.swapaxes(dtx, 0, 1), jnp.swapaxes(Bm, 0, 1), jnp.swapaxes(Cm, 0, 1)))
            y = jnp.swapaxes(ys, 0, 1) + D_param[None, None, :, None] * xs
            y = y.reshape(B, L, D_INNER)
            y = y * _silu(z)
            y = y * lax.rsqrt(jnp.mean(y * y, -1, keepdims=True) + EPS) * norm_w
            return jnp.einsum('ble,de->bld', y, out_proj_w)

        def _mlp(x, fc_w, fc_b, proj_w, proj_b):
            h = jax.nn.gelu(jnp.einsum('bld,fd->blf', x, fc_w) + fc_b, approximate=False)
            return jnp.einsum('blf,df->bld', h, proj_w) + proj_b
        key = jax.random.key(seed)
        ks = jax.random.split(key, 16)
        B, L = (4, 512)
        s = 0.02
        inp = {'x': jax.random.normal(ks[0], (B, L, D_MODEL), jnp.float32), 'ln1_w': jnp.ones((D_MODEL,), jnp.float32), 'ln1_b': jnp.zeros((D_MODEL,), jnp.float32), 'ln2_w': jnp.ones((D_MODEL,), jnp.float32), 'ln2_b': jnp.zeros((D_MODEL,), jnp.float32), 'in_proj_w': jax.random.normal(ks[1], (D_IN_PROJ, D_MODEL), jnp.float32) * s, 'conv_w': jax.random.normal(ks[2], (CONV_DIM, D_CONV), jnp.float32) * 0.1, 'conv_b': jnp.zeros((CONV_DIM,), jnp.float32), 'dt_bias': jax.random.normal(ks[3], (NHEADS,), jnp.float32) * 0.1, 'A_log': jnp.log(jax.random.uniform(ks[4], (NHEADS,), jnp.float32, 1.0, 16.0)), 'D_param': jnp.ones((NHEADS,), jnp.float32), 'norm_w': jnp.ones((D_INNER,), jnp.float32), 'out_proj_w': jax.random.normal(ks[5], (D_MODEL, D_INNER), jnp.float32) * s, 'fc_w': jax.random.normal(ks[6], (D_FF, D_MODEL), jnp.float32) * s, 'fc_b': jnp.zeros((D_FF,), jnp.float32), 'proj_w': jax.random.normal(ks[7], (D_MODEL, D_FF), jnp.float32) * s, 'proj_b': jnp.zeros((D_MODEL,), jnp.float32)}
        return inp
    _L0_attn_all = _L0_attn_setup()
    _L0_attn_in = {k: v for k, v in _L0_attn_all.items() if k in ('ln1_w', 'ln1_b', 'ln2_w', 'ln2_b', 'in_proj_w', 'conv_w', 'conv_b', 'dt_bias', 'A_log', 'D_param', 'norm_w', 'out_proj_w', 'fc_w', 'fc_b', 'proj_w', 'proj_b')}
    del _L0_attn_all

    def _L0_ffn_setup():
        import jax, jax.numpy as jnp
        import numpy as np
        E = 8
        K = 2
        D = 128
        H = 342
        B, S = (2, 256)

        def _moe_forward(x, centroid, Wg, bg, W1, b1, W2, b2):
            T = x.shape[0] * x.shape[1]
            xs = x.reshape(T, D)
            d2 = jnp.sum(xs * xs, axis=-1, keepdims=True) + jnp.sum(centroid * centroid, axis=-1)[None, :] - 2.0 * (xs @ centroid.T)
            dist = jnp.sqrt(jnp.maximum(d2, 1e-12))
            w, sel = jax.lax.top_k(dist, K)
            w = jax.nn.softmax(w.astype(jnp.float32), axis=1).astype(x.dtype)
            we = jnp.zeros((T, E), dtype=x.dtype).at[jnp.arange(T)[:, None], sel].add(w)
            out = jnp.zeros_like(xs)
            for e in range(E):
                h = jax.nn.silu(xs @ Wg[e] + bg[e]) * (xs @ W1[e] + b1[e])
                out = out + we[:, e:e + 1] * (h @ W2[e] + b2[e])
            return out.reshape(x.shape)
        key = jax.random.key(seed)
        ks = jax.random.split(key, 9)
        scale = 0.02
        return {'x': jax.random.normal(ks[0], (B, S, D), dtype=jnp.float32), 'centroid': jax.random.normal(ks[1], (E, D), dtype=jnp.float32), 'Wg': jax.random.normal(ks[2], (E, D, H), dtype=jnp.float32) * scale, 'bg': jnp.zeros((E, H), dtype=jnp.float32), 'W1': jax.random.normal(ks[3], (E, D, H), dtype=jnp.float32) * scale, 'b1': jnp.zeros((E, H), dtype=jnp.float32), 'W2': jax.random.normal(ks[4], (E, H, D), dtype=jnp.float32) * scale, 'b2': jnp.zeros((E, D), dtype=jnp.float32)}
    _L0_ffn_all = _L0_ffn_setup()
    _L0_ffn_in = {k: v for k, v in _L0_ffn_all.items() if k in ('centroid', 'Wg', 'bg', 'W1', 'b1', 'W2', 'b2')}
    del _L0_ffn_all
    return {'x': x, 'ctx_1024': ctx_1024, 'L0_xattn_Wq': _L0_xattn_in['Wq'], 'L0_xattn_bq': _L0_xattn_in['bq'], 'L0_xattn_Wk': _L0_xattn_in['Wk'], 'L0_xattn_bk': _L0_xattn_in['bk'], 'L0_xattn_Wv': _L0_xattn_in['Wv'], 'L0_xattn_bv': _L0_xattn_in['bv'], 'L0_xattn_Wo': _L0_xattn_in['Wo'], 'L0_xattn_bo': _L0_xattn_in['bo'], 'L0_attn_ln1_w': _L0_attn_in['ln1_w'], 'L0_attn_ln1_b': _L0_attn_in['ln1_b'], 'L0_attn_ln2_w': _L0_attn_in['ln2_w'], 'L0_attn_ln2_b': _L0_attn_in['ln2_b'], 'L0_attn_in_proj_w': _L0_attn_in['in_proj_w'], 'L0_attn_conv_w': _L0_attn_in['conv_w'], 'L0_attn_conv_b': _L0_attn_in['conv_b'], 'L0_attn_dt_bias': _L0_attn_in['dt_bias'], 'L0_attn_A_log': _L0_attn_in['A_log'], 'L0_attn_D_param': _L0_attn_in['D_param'], 'L0_attn_norm_w': _L0_attn_in['norm_w'], 'L0_attn_out_proj_w': _L0_attn_in['out_proj_w'], 'L0_attn_fc_w': _L0_attn_in['fc_w'], 'L0_attn_fc_b': _L0_attn_in['fc_b'], 'L0_attn_proj_w': _L0_attn_in['proj_w'], 'L0_attn_proj_b': _L0_attn_in['proj_b'], 'L0_ffn_centroid': _L0_ffn_in['centroid'], 'L0_ffn_Wg': _L0_ffn_in['Wg'], 'L0_ffn_bg': _L0_ffn_in['bg'], 'L0_ffn_W1': _L0_ffn_in['W1'], 'L0_ffn_b1': _L0_ffn_in['b1'], 'L0_ffn_W2': _L0_ffn_in['W2'], 'L0_ffn_b2': _L0_ffn_in['b2']}

def reference(x, ctx_1024, L0_xattn_Wq, L0_xattn_bq, L0_xattn_Wk, L0_xattn_bk, L0_xattn_Wv, L0_xattn_bv, L0_xattn_Wo, L0_xattn_bo, L0_attn_ln1_w, L0_attn_ln1_b, L0_attn_ln2_w, L0_attn_ln2_b, L0_attn_in_proj_w, L0_attn_conv_w, L0_attn_conv_b, L0_attn_dt_bias, L0_attn_A_log, L0_attn_D_param, L0_attn_norm_w, L0_attn_out_proj_w, L0_attn_fc_w, L0_attn_fc_b, L0_attn_proj_w, L0_attn_proj_b, L0_ffn_centroid, L0_ffn_Wg, L0_ffn_bg, L0_ffn_W1, L0_ffn_b1, L0_ffn_W2, L0_ffn_b2):
    import jax
    import jax.numpy as jnp

    def _L0_xattn_ref(query, key, value, Wq, bq, Wk, bk, Wv, bv, Wo, bo):
        import jax, jax.numpy as jnp
        import numpy as np
        D_MODEL = 128
        NUM_HEADS = 16
        HEAD_DIM = D_MODEL // NUM_HEADS
        B, S = (4, 256)
        b = query.shape[0]

        def split_heads(x):
            return x.reshape(b, -1, NUM_HEADS, HEAD_DIM).transpose(0, 2, 1, 3)
        q = split_heads(query @ Wq.T + bq)
        k = split_heads(key @ Wk.T + bk)
        v = split_heads(value @ Wv.T + bv)
        scores = jnp.einsum('bhqd,bhkd->bhqk', q, k) / np.sqrt(HEAD_DIM)
        weights = jax.nn.softmax(scores, axis=-1)
        out = jnp.einsum('bhqk,bhkd->bhqd', weights, v)
        out = out.transpose(0, 2, 1, 3).reshape(b, -1, D_MODEL)
        return out @ Wo.T + bo

    def _L0_attn_ref(x, ln1_w, ln1_b, ln2_w, ln2_b, in_proj_w, conv_w, conv_b, dt_bias, A_log, D_param, norm_w, out_proj_w, fc_w, fc_b, proj_w, proj_b):
        import jax, jax.numpy as jnp
        import numpy as np
        from jax import lax
        D_MODEL = 128
        D_INNER = 256
        D_STATE = 64
        D_CONV = 4
        HEADDIM = 64
        NHEADS = D_INNER // HEADDIM
        CONV_DIM = D_INNER + 2 * D_STATE
        D_IN_PROJ = 2 * D_INNER + 2 * D_STATE + NHEADS
        D_FF = 4 * D_MODEL
        EPS = 1e-05

        def _layernorm(x, w, b):
            mu = jnp.mean(x, -1, keepdims=True)
            var = jnp.mean((x - mu) ** 2, -1, keepdims=True)
            return (x - mu) * lax.rsqrt(var + EPS) * w + b

        def _silu(x):
            return x * jax.nn.sigmoid(x)

        def _mamba2(x, in_proj_w, conv_w, conv_b, dt_bias, A_log, D_param, norm_w, out_proj_w):
            B, L, _ = x.shape
            zxbcdt = jnp.einsum('bld,ed->ble', x, in_proj_w)
            z = zxbcdt[..., :D_INNER]
            xBC = zxbcdt[..., D_INNER:D_INNER + CONV_DIM]
            dt_raw = zxbcdt[..., D_INNER + CONV_DIM:]
            dt = jax.nn.softplus(dt_raw + dt_bias)
            xp = jnp.pad(xBC, ((0, 0), (D_CONV - 1, 0), (0, 0)))
            xBC = sum((conv_w[:, k] * xp[:, k:k + L, :] for k in range(D_CONV))) + conv_b
            xBC = _silu(xBC)
            xs = xBC[..., :D_INNER].reshape(B, L, NHEADS, HEADDIM)
            Bm = xBC[..., D_INNER:D_INNER + D_STATE]
            Cm = xBC[..., D_INNER + D_STATE:]
            A = -jnp.exp(A_log)
            dA = jnp.exp(dt * A)
            dtx = dt[..., None] * xs

            def step(h, inp):
                dA_t, dtx_t, B_t, C_t = inp
                h = dA_t[:, :, None, None] * h + dtx_t[..., None] * B_t[:, None, None, :]
                y_t = jnp.einsum('bhpn,bn->bhp', h, C_t)
                return (h, y_t)
            h0 = jnp.zeros((B, NHEADS, HEADDIM, D_STATE), x.dtype)
            _, ys = lax.scan(step, h0, (jnp.swapaxes(dA, 0, 1), jnp.swapaxes(dtx, 0, 1), jnp.swapaxes(Bm, 0, 1), jnp.swapaxes(Cm, 0, 1)))
            y = jnp.swapaxes(ys, 0, 1) + D_param[None, None, :, None] * xs
            y = y.reshape(B, L, D_INNER)
            y = y * _silu(z)
            y = y * lax.rsqrt(jnp.mean(y * y, -1, keepdims=True) + EPS) * norm_w
            return jnp.einsum('ble,de->bld', y, out_proj_w)

        def _mlp(x, fc_w, fc_b, proj_w, proj_b):
            h = jax.nn.gelu(jnp.einsum('bld,fd->blf', x, fc_w) + fc_b, approximate=False)
            return jnp.einsum('blf,df->bld', h, proj_w) + proj_b
        x = x + _mamba2(_layernorm(x, ln1_w, ln1_b), in_proj_w, conv_w, conv_b, dt_bias, A_log, D_param, norm_w, out_proj_w)
        x = x + _mlp(_layernorm(x, ln2_w, ln2_b), fc_w, fc_b, proj_w, proj_b)
        return x

    def _L0_ffn_ref(x, centroid, Wg, bg, W1, b1, W2, b2):
        import jax, jax.numpy as jnp
        import numpy as np
        E = 8
        K = 2
        D = 128
        H = 342
        B, S = (2, 256)

        def _moe_forward(x, centroid, Wg, bg, W1, b1, W2, b2):
            T = x.shape[0] * x.shape[1]
            xs = x.reshape(T, D)
            d2 = jnp.sum(xs * xs, axis=-1, keepdims=True) + jnp.sum(centroid * centroid, axis=-1)[None, :] - 2.0 * (xs @ centroid.T)
            dist = jnp.sqrt(jnp.maximum(d2, 1e-12))
            w, sel = jax.lax.top_k(dist, K)
            w = jax.nn.softmax(w.astype(jnp.float32), axis=1).astype(x.dtype)
            we = jnp.zeros((T, E), dtype=x.dtype).at[jnp.arange(T)[:, None], sel].add(w)
            out = jnp.zeros_like(xs)
            for e in range(E):
                h = jax.nn.silu(xs @ Wg[e] + bg[e]) * (xs @ W1[e] + b1[e])
                out = out + we[:, e:e + 1] * (h @ W2[e] + b2[e])
            return out.reshape(x.shape)
        return _moe_forward(x, centroid, Wg, bg, W1, b1, W2, b2)
    x = x + _L0_xattn_ref(_layernorm(x, axis=-1), ctx_1024, ctx_1024, L0_xattn_Wq, L0_xattn_bq, L0_xattn_Wk, L0_xattn_bk, L0_xattn_Wv, L0_xattn_bv, L0_xattn_Wo, L0_xattn_bo)
    x = x + _L0_attn_ref(_layernorm(x, axis=-1), L0_attn_ln1_w, L0_attn_ln1_b, L0_attn_ln2_w, L0_attn_ln2_b, L0_attn_in_proj_w, L0_attn_conv_w, L0_attn_conv_b, L0_attn_dt_bias, L0_attn_A_log, L0_attn_D_param, L0_attn_norm_w, L0_attn_out_proj_w, L0_attn_fc_w, L0_attn_fc_b, L0_attn_proj_w, L0_attn_proj_b)
    x = x + _L0_ffn_ref(_layernorm(x, axis=-1), L0_ffn_centroid, L0_ffn_Wg, L0_ffn_bg, L0_ffn_W1, L0_ffn_b1, L0_ffn_W2, L0_ffn_b2)
    return x

_drawn_inputs = setup_inputs


def setup_inputs(seed=0):
    import zlib

    import numpy as np

    out = dict(_drawn_inputs(seed))
    spreads = {'L0_xattn_bq': (0.0, 0.4),
     'L0_xattn_bk': (0.0, 2.0),
     'L0_xattn_bv': (0.0, 0.1),
     'L0_xattn_bo': (0.0, 0.1),
     'L0_attn_ln1_w': (1.0, 0.2),
     'L0_attn_ln1_b': (0.0, 0.647),
     'L0_attn_ln2_w': (1.0, 0.6),
     'L0_attn_ln2_b': (0.0, 0.8),
     'L0_attn_conv_b': (0.0, 0.1),
     'L0_attn_D_param': (1.0, 0.6),
     'L0_attn_norm_w': (1.0, 0.591),
     'L0_attn_fc_b': (0.0, 0.677),
     'L0_attn_proj_b': (0.0, 0.1),
     'L0_ffn_bg': (0.0, 0.8),
     'L0_ffn_b1': (0.0, 0.8),
     'L0_ffn_b2': (0.0, 0.654)}
    factors = {'L0_attn_dt_bias': 8.0,
     'L0_attn_A_log': 8.0,
     'L0_ffn_Wg': 8.0,
     'L0_ffn_W1': 8.0,
     'L0_ffn_W2': 8.0}
    for name, (base, spread) in spreads.items():
        noise = np.random.default_rng([zlib.crc32(name.encode()), seed]).standard_normal(out[name].shape)
        drawn = base * np.exp(spread * noise) if base else spread * noise
        out[name] = jnp.asarray(drawn.astype(out[name].dtype))
    for name, factor in factors.items():
        out[name] = (out[name] * factor).astype(out[name].dtype)
    return out
```

```python
from contextlib import ExitStack

import concourse.bass as bass
from concourse import mybir

ALU = mybir.AluOpType
ACT = mybir.ActivationFunctionType
AX = mybir.AxisListType
F32 = mybir.dt.float32
BF16 = mybir.dt.bfloat16

P = 128
B, LQ, LK = 16, 64, 1601
H, HD = 16, 8
T = B * LQ
NT = T // P
EPS = 1e-5

G = 4
GH = H // G
SHIFT = 96
NK = (LK + P - 1) // P
CH = 401
CHUNKS = [(0, CH), (CH, CH), (2 * CH, CH), (3 * CH, LK - 3 * CH)]
VG, VH = 6, 3
RING = 23
PER = 21

V_BK, V_BQ, V_LN1W, V_LN1B, V_LN2W, V_LN2B = 0, 1, 5, 6, 7, 8
V_CW, V_CB, V_D, V_NW, V_FCB = 9, 25, 29, 31, 33
NV = 37
R_BV, R_BO, R_PB, R_ALOG, R_DTB = 0, 128, 256, 384, 388
NR = 392

MH = 4
E, NH, HT = 8, 3, 114
DT_LAST = 15
ST1, ST2, ST3, ST4 = 34, 60, 78, 96


def keys_of(k):
    return min(P, LK - k * P)


def attention(nc, A, keep):
    with ExitStack() as ctx:
        def sb(name, shape, dt=F32):
            return ctx.enter_context(nc.sbuf_tensor(name, shape, dt))

        def pb(name, shape, dt=F32):
            return ctx.enter_context(nc.psum_tensor(name, shape, dt))

        def sem(name):
            return ctx.enter_context(nc.semaphore(name))

        wq = sb("wq", [P, G, P])
        wkv = sb("wkv", [P, 2, P])
        wkv_hi = sb("wkv_hi", [P, 2, P], BF16)
        wkv_lo = sb("wkv_lo", [P, 2, P], BF16)
        one = sb("one", [P, 1])
        nident = sb("nident", [P, P])
        bq_scaled = sb("bq_scaled", [P, G])
        stats = sb("stats", [P, NT, 6])
        mean_var = sb("mean_var", [P, NT, 2])
        rstd = sb("rstd", [P, NT])
        xn = sb("xn", [P, NT, P])
        xnT = sb("xnT", [P, T])
        q_full = sb("q_full", [P, 2, T])
        q_hi = sb("q_hi", [P, 2, T], BF16)
        q_part = sb("q_part", [P, 2, T], BF16)
        q_stack = sb("q_stack", [P, B, G, GH, LQ], BF16)
        ctx_in = sb("ctx_in", [P, 2, LK])
        ctx_hi = sb("ctx_hi", [P, 2, LK], BF16)
        ctx_lo = sb("ctx_lo", [P, 2, LK], BF16)
        k_hi = sb("k_hi", [P, LK], BF16)
        k_lo = sb("k_lo", [P, LK], BF16)
        k_stack = sb("k_stack", [P, 2, G, LK], BF16)
        q_cur = sb("q_cur", [P, 2, G * GH * LQ], BF16)
        values = sb("values", [P, 2, NK, VG * 32])
        probs = sb("probs", [P, 2, H * LQ])
        half_max = sb("half_max", [P, 8, 2])
        row_max = sb("row_max", [P, 16])
        shift_hi = sb("shift_hi", [16, P], BF16)
        shift = sb("shift", [16, P], BF16)

        wide = pb("wide", [P, 2, 1024])
        score = pb("score", [P, 2, 512])
        sums = pb("sums", [P, 2, 512])

        s_const = sem("s_const")
        s_later = sem("s_later")
        s_x = sem("s_x")
        s_ctx = [sem(f"s_ctx{i}") for i in range(2)]
        s_wsplit = sem("s_wsplit")
        s_memset = sem("s_memset")
        s_one = sem("s_one")
        s_stat = sem("s_stat")
        s_sqrt = sem("s_sqrt")
        s_xn = sem("s_xn")
        s_xt = sem("s_xt")
        s_xtc = sem("s_xtc")
        s_bq = sem("s_bq")
        s_q = sem("s_q")
        s_qf = sem("s_qf")
        s_qh = sem("s_qh")
        s_qp = sem("s_qp")
        s_qs = sem("s_qs")
        s_split = sem("s_split")
        s_wide = sem("s_wide")
        s_wfree = sem("s_wfree")
        s_khi = sem("s_khi")
        s_stack = [sem(f"s_stack{i}") for i in range(2)]
        s_rowmax = sem("s_rowmax")
        s_shift = sem("s_shift")
        s_shin = [sem(f"s_shin{i}") for i in range(2)]
        s_score = sem("s_score")
        s_last = sem("s_last")
        s_exp = sem("s_exp")
        s_pv = sem("s_pv")
        s_sums = sem("s_sums")
        SHIN_N, STACK_N = 16, 4 * 16

        block = ctx.enter_context(nc.Block())

        def run(e, body):
            body(-1, -1, 1)
            with e.Fori(0, B // 2 - 1) as j:
                body(j * 2, j, 0)
                body(j * 2 + 1, j, 1)
            body(B - 2, B // 2 - 1, 0)
            body(B - 1, B // 2 - 1, 1)

        def has(i, ahead):
            return not isinstance(i, int) or 0 <= i + ahead < B

        def slot(par, ahead):
            return (par + ahead) % 2

        def k_slot(par, k):
            return (par * NK + k) % 2

        def ring(i, use):
            if isinstance(i, int) and i == B - 2 and use > 18:
                raise ValueError("no keys any more")
            return i * PER + (RING + use)

        def ring_slot(par, use):
            return (par * PER + RING + use) % 2

        @block.sync
        def _(sp):
            sp.dma_start(keep.ident[:], A["ident"]).then_inc(s_const, 16)
            sp.dma_start(nident[:], A["nident"]).then_inc(s_const, 16)
            sp.dma_start(keep.marks[:], A["marks"]).then_inc(s_const, 16)
            sp.dma_start(keep.vecs[:], A["vecs"]).then_inc(s_const, 16)
            sp.dma_start(wkv[:], A["wkv"]).then_inc(s_const, 16)
            sp.dma_start(wq[:], A["wq"]).then_inc(s_const, 16)
            sp.dma_start(keep.x[:], A["x"].rearrange("(t p) d -> p t d", p=P)).then_inc(s_x, 16)
            sp.dma_start(ctx_in[:, 0, :], A["ctx"][:, 0, :]).then_inc(s_ctx[0], 16)
            sp.dma_start(ctx_in[:, 1, :], A["ctx"][:, 1, :]).then_inc(s_ctx[1], 16)

            def value(v):
                if isinstance(v, int):
                    return v
                r = sp.alloc_register(f"wait_value{len(held)}")
                held.append(r)
                sp.reg_mov(r, v)
                return sp.snap(r, min_val=1)

            held = []

            for to, of in ((keep.iota, A["iota"]), (keep.wo, A["wo"]), (keep.win, A["win"]), (keep.wout, A["wout"]),
                           (keep.wfc, A["wfc"]), (keep.wproj, A["wproj"])):
                sp.dma_start(to[:], of).then_inc(s_later, 16)
            sp.dma_start(keep.rows[:], A["rows"].to_broadcast([P, NR])).then_inc(s_later, 16)

            def body(i, j, par):
                n = slot(par, 1)
                if has(i, 1):
                    high_there, scores_done, low_there = value(i * 4 + 8), value(i + 1), value(ring(i, 0))
                    sp.wait_ge(s_khi, high_there)
                    if has(i, -1):
                        sp.wait_ge(s_last, scores_done)
                    if isinstance(i, int) and i < 0:
                        sp.wait_ge(s_memset, 2)
                        sp.wait_ge(s_qs, G)
                    for c in range(2):
                        sp.dma_start(k_stack[32 * c:32 * c + 32, n, :, :], k_hi[:, :]).then_inc(s_stack[n], 16)
                    sp.dma_start(q_cur[:, n, :], q_stack[:, bass.ds(i + 1, 1), :, :, :].rearrange(
                        "p b g h q -> p (b g h q)")).then_inc(s_stack[n], 16)
                    sp.wait_ge(s_wfree, low_there)
                    sp.dma_start(k_stack[64:96, n, :, :], k_lo[:, :]).then_inc(s_stack[n], 16)
                if has(i, 2) and has(i, 0):
                    sp.dma_start(ctx_in[:, par, :], A["ctx"][:, bass.ds(i + 2, 1), :].rearrange(
                        "p b k -> p (b k)")).then_inc(s_ctx[par], 16)
                if has(i, 1):
                    sp.wait_ge(s_wfree, ring(i, 18) + 1)
                    sp.dma_start(q_cur[SHIFT:SHIFT + 2, n, :], shift[:, :]).then_inc(s_shin[n], 16)

            run(sp, body)
            sp.wait_ge(s_later, 7 * 16)

        @block.gpsimd
        def _(pool):
            pool.memset(one[:], 1.0).then_inc(s_one, 1)
            pool.wait_ge(s_one, 1)
            pool.memset(k_stack[:, 0, :, :], 1.0).then_inc(s_memset, 1)
            pool.memset(k_stack[:, 1, :, :], 1.0).then_inc(s_memset, 1)

            def split(i, j, par, ahead):
                n = slot(par, ahead)
                pool.wait_ge(s_ctx[n], (j + (par + ahead) // 2 + 1) * 16)
                if has(i, ahead - 2):
                    pool.wait_ge(s_wide, ring(i + (ahead - 3), 1) + 1)
                pool.tensor_tensor(ctx_hi[:, n, :], ctx_in[:, n, :], one[:].to_broadcast([P, LK]),
                                   ALU.mult).then_inc(s_split, 1)
                pool.wait_ge(s_split, (i + ahead) * 2 + 1)
                pool.tensor_tensor(ctx_lo[:, n, :], ctx_in[:, n, :], ctx_hi[:, n, :],
                                   ALU.subtract).then_inc(s_split, 1)

            split(-1, -1, 1, 1)

            def body(i, j, par):
                if has(i, 2):
                    split(i, j, par, 2)

            run(pool, body)

        @block.tensor
        def _(pe):
            def product3(out, lhs_hi, lhs_lo, rhs_hi, rhs_lo):
                pe.matmul(out, lhs_hi, rhs_hi, start=True, stop=False)
                pe.matmul(out, lhs_hi, rhs_lo, start=False, stop=False)
                return pe.matmul(out, lhs_lo, rhs_hi, start=False, stop=True)

            def keys(i, par, ahead, half, use):
                n, w = slot(par, ahead), use[1]
                if half == 0:
                    pe.wait_ge(s_split, (i + ahead + 1) * 2)
                if not isinstance(use[0], int) or use[0] >= 2:
                    pe.wait_ge(s_wfree, use[0] - 1)
                for c in range(2):
                    at, m = CHUNKS[2 * half + c]
                    last = product3(wide[:, w, 512 * c:512 * c + m], wkv_hi[:, 0, :], wkv_lo[:, 0, :],
                                    ctx_hi[:, n, at:at + m], ctx_lo[:, n, at:at + m])
                last.then_inc(s_wide, 1)

            def vals(i, par, half):
                n, w = slot(par, 1), ring_slot(par, half)
                pe.wait_ge(s_wfree, ring(i, half) - 1)
                for k in range(7 * half, 7 + 6 * half):
                    m, at = keys_of(k), P * (k - 7 * half)
                    ks = slice(k * P, k * P + m)
                    out = wide[0:m, w, at:at + P]
                    last = product3(out, ctx_hi[:, n, ks], ctx_lo[:, n, ks],
                                    wkv_hi[:, 1, :], wkv_lo[:, 1, :])
                last.then_inc(s_wide, 1)

            def maxima(i, par, u):
                pair, half = u // 2, u % 2
                n, w, g = slot(par, 1), ring_slot(par, 2 + u), u // 4
                pe.wait_ge(s_wfree, ring(i, 2 + u) - 1)
                for c in range(2):
                    at = min(CHUNKS[2 * half + c][0], LK - CH)
                    last = pe.matmul(wide[:, w, 512 * c:512 * c + CH],
                                     q_cur[:, n, pair * P:pair * P + P],
                                     k_stack[:, n, g, at:at + CH], start=True, stop=True)
                last.then_inc(s_wide, 1)

            def turn_max(i, par):
                w = ring_slot(par, 18)
                pe.wait_ge(s_wfree, ring(i, 18) - 1)
                pe.wait_ge(s_rowmax, i * 2 + 4)
                pe.matmul(wide[0:16, w, 0:P], row_max[:, :], nident[:], start=True, stop=True).then_inc(s_wide, 1)

            def scores(i, par, k):
                n, m = slot(par, 0), keys_of(k)
                for u in range(2):
                    pe.wait_ge(s_exp, i * (2 * NK) + (2 * k + u + 1))
                    for g in (2 * u, 2 * u + 1):
                        last = pe.matmul(score[0:m, u, 256 * (g % 2):256 * (g % 2) + 256],
                                         k_stack[:, n, g, k * P:k * P + m],
                                         q_cur[:, n, 256 * g:256 * g + 256], start=True, stop=True)
                    last.then_inc(s_last if k == NK - 1 and u else s_score, 1)

            def sum_values(i, par, k):
                n, m = slot(par, 0), keys_of(k)
                if k == 0:
                    pe.wait_ge(s_wfree, ring(i - 1, 1) + 1)
                    pe.wait_ge(s_sums, i + 1)
                pe.wait_ge(s_exp, i * (2 * NK) + (2 * k + 2 + 2))
                for g in range(VG):
                    c, w = 32 * (g % 4), min(VH, H - VH * g) * LQ
                    last = pe.matmul(sums[c:c + 32, g // 4, 0:w], values[0:m, n, k, 32 * g:32 * g + 32],
                                     probs[0:m, k_slot(par, k), 192 * g:192 * g + w],
                                     start=(k == 0), stop=(k == NK - 1))
                last.then_inc(s_pv, 1)

            pe.sem_inc(s_last, 1)
            pe.wait_ge(s_const, 16 * 6)
            for t in range(NT):
                pe.wait_ge(s_xn, t + 1)
                last = pe.transpose(wide[:, 0, t * P:t * P + P], xn[:, t, :], keep.ident[:])
                if t % 4 == 3:
                    last.then_inc(s_xt, 1)
            pe.wait_ge(s_xtc, 2)
            for g in range(G):
                if g >= 2:
                    pe.wait_ge(s_qf, 2 * g - 2)
                for h in range(2):
                    out = (score if g % 2 else sums)[:, h, :]
                    pe.matmul(out, wq[:, g, :], xnT[:, 512 * h:512 * h + 512],
                              start=True, stop=True).then_inc(s_q, 1)
            pe.wait_ge(s_qf, 2 * G)
            pe.wait_ge(s_wsplit, 2)
            keys(0, 0, 0, 0, (0, 0))
            keys(0, 0, 0, 1, (1, 1))

            def body(i, j, par):
                work, more, last = has(i, 0), has(i, 1), has(i, 2)
                n = slot(par, 1)
                for k in range(NK):
                    if work:
                        if k == 0:
                            pe.wait_ge(s_shin[par], (j + 1) * SHIN_N)
                        scores(i, par, k)
                        if k:
                            sum_values(i, par, k - 1)
                    if more:
                        if k == 0:
                            vals(i, par, 0)
                        if k == 1:
                            vals(i, par, 1)
                        if k == 3:
                            pe.wait_ge(s_stack[n], (j + (par + 1) // 2 + 1) * STACK_N)
                        if 3 <= k < 11:
                            maxima(i, par, 2 * k - 6)
                            maxima(i, par, 2 * k - 5)
                        if k == 11:
                            turn_max(i, par)
                    if last and k >= 11:
                        keys(i, par, 2, k - 11, (ring(i, 8 + k), ring_slot(par, 8 + k)))
                if work:
                    sum_values(i, par, NK - 1)

            run(pe, body)

        @block.scalar
        def _(act):
            act.wait_ge(s_const, 16 * 6)
            nc.scalar.mul(bq_scaled[:], keep.vecs[:, V_BQ:V_BQ + G], HD ** -0.5).then_inc(s_bq, 1)
            act.sem_inc(s_exp, 2)
            act.wait_ge(s_stat, 2 * NT + 2)
            nc.scalar.activation(rstd[:], rstd[:], ACT.Sqrt).then_inc(s_sqrt, 1)
            for h in range(2):
                act.wait_ge(s_xt, h + 1)
                nc.scalar.copy(xnT[:, 512 * h:512 * h + 512],
                               wide[:, 0, 512 * h:512 * h + 512]).then_inc(s_xtc, 1)
            act.wait_ge(s_bq, 1)
            for g in range(G):
                if g >= 2:
                    act.wait_ge(s_qp, g - 1)
                for h in range(2):
                    act.wait_ge(s_q, 2 * g + h + 1)
                    nc.scalar.activation(q_full[:, g % 2, 512 * h:512 * h + 512],
                                         (score if g % 2 else sums)[:, h, :], ACT.Identity,
                                         bias=bq_scaled[:, g:g + 1], scale=HD ** -0.5).then_inc(s_qf, 1)

            def key_high(i, par, ahead, half, use):
                act.wait_ge(s_wide, use[0] + 1)
                for c in range(2):
                    at, m = CHUNKS[2 * half + c]
                    nc.scalar.activation(k_hi[:, at:at + m], wide[:, use[1], 512 * c:512 * c + m],
                                         ACT.Identity, bias=keep.vecs[:, V_BK:V_BK + 1]).then_inc(s_khi, 1)

            key_high(0, 0, 0, 0, (0, 0))
            key_high(0, 0, 0, 1, (1, 1))

            def body(i, j, par):
                for k in range(NK):
                    m = keys_of(k)
                    if has(i, 0):
                        for u in range(2):
                            if k == NK - 1 and u:
                                act.wait_ge(s_last, i + 2)
                            else:
                                act.wait_ge(s_score, i * (2 * NK - 1) + (2 * k + u + 1))
                            if u == 0:
                                act.wait_ge(s_pv, i * NK + (k + 1))
                            nc.scalar.activation(probs[0:m, k_slot(par, k), 512 * u:512 * u + 512],
                                                 score[0:m, u, :], ACT.Exp).then_inc(s_exp, 1)
                    if k == 11 and has(i, 2):
                        n = slot(par, 1)
                        act.wait_ge(s_stack[n], (j + (par + 1) // 2 + 1) * STACK_N)
                    if k >= 11 and has(i, 2):
                        key_high(i, par, 2, k - 11, (ring(i, 8 + k), ring_slot(par, 8 + k)))

            run(act, body)

        @block.vector
        def _(dve):
            dve.memset(values[:], 1.0).then_inc(s_memset, 1)
            dve.sem_inc(s_pv, 2)
            dve.sem_inc(s_sums, 1)
            dve.wait_ge(s_x, 16)
            for t in range(NT):
                dve.bn_stats(stats[:, t, :], keep.x[:, t, :]).then_inc(s_stat, 1)
            for t in range(NT):
                dve.wait_ge(s_stat, t + 1)
                dve.bn_aggr(mean_var[:, t, :], stats[:, t, :]).then_inc(s_stat, 1)
            dve.wait_ge(s_stat, 2 * NT)
            dve.tensor_scalar(rstd[:], mean_var[:, :, 1], EPS, None, ALU.add).then_inc(s_stat, 1)
            dve.wait_ge(s_stat, 2 * NT + 1)
            dve.reciprocal(rstd[:], rstd[:]).then_inc(s_stat, 1)
            dve.wait_ge(s_sqrt, 1)
            for t in range(NT):
                dve.tensor_scalar(xn[:, t, :], keep.x[:, t, :], mean_var[:, t, 0:1], rstd[:, t:t + 1],
                                  ALU.subtract, ALU.mult).then_inc(s_xn, 1)
            dve.wait_ge(s_const, 16 * 6)
            dve.tensor_copy(wkv_hi[:], wkv[:]).then_inc(s_wsplit, 1)
            dve.wait_ge(s_wsplit, 1)
            dve.tensor_tensor(wkv_lo[:], wkv[:], wkv_hi[:], ALU.subtract).then_inc(s_wsplit, 1)

            for g in range(G):
                s = g % 2
                dve.wait_ge(s_qf, 2 * g + 2)
                dve.tensor_copy(q_hi[:, s, :], q_full[:, s, :]).then_inc(s_qh, 1)
                dve.wait_ge(s_qh, g + 1)
                dve.scalar_tensor_tensor(out=q_part[:, s, :], in0=q_hi[:, s, :],
                                         scalar=keep.marks[:, 4:5], in1=q_full[:, s, :],
                                         op0=ALU.mult, op1=ALU.add).then_inc(s_qp, 1)
                dve.wait_ge(s_qp, g + 1)
                for h in range(GH):
                    last = dve.tensor_scalar(q_stack[:, :, g, h, :],
                                             q_part[:, s, :].rearrange("p (b q) -> p b q", b=B),
                                             keep.marks[:, h:h + 1], None, ALU.mult)
                last.then_inc(s_qs, 1)

            def key_low(i, par, ahead, half, use):
                for c in range(2):
                    at, m = CHUNKS[2 * half + c]
                    dve.wait_ge(s_khi, (i + ahead) * 4 + (2 * half + c + 1))
                    last = dve.scalar_tensor_tensor(
                        out=k_lo[:, at:at + m], in0=wide[:, use[1], 512 * c:512 * c + m],
                        scalar=keep.vecs[:, V_BK:V_BK + 1], in1=k_hi[:, at:at + m],
                        op0=ALU.add, op1=ALU.subtract)
                last.then_inc(s_wfree, 1)

            key_low(0, 0, 0, 0, (0, 0))
            key_low(0, 0, 0, 1, (1, 1))

            def vals(i, par, half):
                n, w = slot(par, 1), ring_slot(par, half)
                dve.wait_ge(s_wide, ring(i, half) + 1)
                parts = [(0, 7, P)] if half == 0 else [(7, 5, P), (12, 1, keys_of(12))]
                for k0, nk, m in parts:
                    at = P * (k0 - 7 * half)
                    src = wide[0:m, w, at:at + P * nk].rearrange("p (k c) -> p k c", k=nk)
                    dst = values[0:m, n, k0:k0 + nk, :]
                    nv = (VG - 1) * VH * HD
                    dve.tensor_copy(
                        dst[:, :, 0:32 * (VG - 1)].rearrange("p k (g c) -> p k g c", c=32)[:, :, :, 1:25],
                        src[:, :, 0:nv].rearrange("p k (g c) -> p k g c", g=VG - 1))
                    last = dve.tensor_copy(dst[:, :, 32 * (VG - 1) + 1:32 * (VG - 1) + 1 + HD],
                                           src[:, :, nv:P])
                last.then_inc(s_wfree, 1)

            def body(i, j, par):
                if has(i, 1):
                    if isinstance(i, int) and i < 0:
                        dve.wait_ge(s_memset, 3)
                    vals(i, par, 0)
                    vals(i, par, 1)
                    for u in range(16):
                        dve.wait_ge(s_wide, ring(i, 2 + u) + 1)
                        w = ring_slot(par, 2 + u)
                        dve.tensor_reduce(
                            half_max[:, u // 2, u % 2:u % 2 + 1],
                            wide[:, w, :].rearrange("p (c k) -> p c k", c=2)[:, :, 0:CH],
                            AX.XY, ALU.max).then_inc(s_wfree, 1)
                    dve.wait_ge(s_wfree, ring(i, 17) + 1)
                    dve.tensor_reduce(row_max[:, 0:8], half_max[:, :, :], AX.X, ALU.max).then_inc(s_rowmax, 1)
                    dve.tensor_reduce(row_max[:, 8:16], half_max[:, :, :], AX.X, ALU.max).then_inc(s_rowmax, 1)
                    dve.wait_ge(s_wide, ring(i, 18) + 1)
                    w = ring_slot(par, 18)
                    if has(i, 0):
                        dve.wait_ge(s_shin[par], (j + 1) * SHIN_N)
                    dve.tensor_copy(shift_hi[:, :], wide[0:16, w, 0:P]).then_inc(s_shift, 1)
                    dve.wait_ge(s_shift, i + 2)
                    dve.scalar_tensor_tensor(out=shift[:, :], in0=shift_hi[:, :],
                                             scalar=keep.marks[0:16, 5:6], in1=wide[0:16, w, 0:P],
                                             op0=ALU.mult, op1=ALU.add).then_inc(s_wfree, 1)
                if has(i, 2):
                    for half in range(2):
                        key_low(i, par, 2, half, (ring(i, 19 + half), ring_slot(par, 19 + half)))
                if has(i, 0):
                    dve.wait_ge(s_pv, i * NK + (NK + 2))
                    out = keep.sums[:, :, bass.ds(i * LQ, LQ)]
                    dve.tensor_copy(out[:, 0:3, :], sums[:, 0, 0:192].rearrange("p (j q) -> p j q", j=VH))
                    dve.tensor_copy(out[0:32, 3:6, :],
                                    sums[0:32, 1, 0:192].rearrange("p (j q) -> p j q", j=VH))
                    dve.tensor_copy(out[32:64, 3, :], sums[32:64, 1, 0:LQ]).then_inc(s_sums, 1)

            run(dve, body)


def mamba_mlp(nc, A, keep):
    with ExitStack() as ctx:
        def sb(name, shape, dt=F32):
            return ctx.enter_context(nc.sbuf_tensor(name, shape, dt))

        def pb(name, shape, dt=F32):
            return ctx.enter_context(nc.psum_tensor(name, shape, dt))

        def sem(name):
            return ctx.enter_context(nc.semaphore(name))

        rows, vecs, ident = keep.rows, keep.vecs, keep.ident
        o_tok = sb("o_tok", [P, 2, P])
        o_rden = sb("o_rden", [P, 2, 16])
        oT = sb("oT", [P, 2, P])
        x_bias = sb("x_bias", [P, NT, P])
        x1 = sb("x1", [P, NT, P])
        u = sb("u", [P, NT, P])
        v = sb("v", [P, NT, P])
        vT = sb("vT", [P, T])
        stats = sb("stats2", [P, NT, 6])
        mean_var = sb("mean_var2", [P, NT, 2])
        rstd = sb("rstd2", [P, NT])
        conv = sb("conv", [P, 4, T])
        xbc = sb("xbc", [P, 4, T])
        zg = sb("zg", [P, 2, T])
        dt_x = sb("dt_x", [P, NT, MH])
        dt_a = sb("dt_a", [P, NT, MH])
        dt_e = sb("dt_e", [P, NT, MH])
        dt_u = sb("dt_u", [P, NT, MH])
        dt_l = sb("dt_l", [P, NT, MH])
        dt_m = sb("dt_m", [P, NT, MH])
        dt = sb("dt", [P, NT, MH])
        decay = sb("decay", [P, NT, MH])
        a_exp = sb("a_exp", [P, MH])
        delta = sb("delta", [P, 8, P])
        decay_all = sb("decay_all", [P, 2, 8 * P])
        gain = sb("gain", [P, 2, 8 * P])
        mix = sb("mix", [P, NT, MH, P])
        y = sb("y", [P, 2, T])
        wout_n = sb("wout_n", [P, 2, P])
        rms = sb("rms", [P, NT])
        y1 = sb("y1", [P, NT, P])
        ones = sb("ones", [P, 1])
        one = sb("one2", [P, 1])
        w_stage = sb("w_stage", [P, 2, 2, NH * HT])
        dtx = keep.sums[:, 0:2, :].rearrange("p c (t k) -> p (c t) k", k=2 * P)
        y_sq = keep.sums[:, 2:4, :]
        hid = conv

        ps = pb("ps", [P, 3, 1024])
        pt = pb("pt", [P, 2, 512])

        s_stage = [sem(f"t_stage{i}") for i in range(2)]
        names = ("w one wsp init xb turn o ot otc att x1 st sq ln vt vtc dtp dts dte mm conv silu zin zsil "
                 "bc bcc bc0 scan cb mix xt dtx ya yb yc ysq out ss r y1 fc gelu pr x2")
        s = {n: sem("t_" + n) for n in names.split()}
        block = ctx.enter_context(nc.Block())

        def tok(t):
            return slice(t * P, t * P + P)

        @block.sync
        def _(sp):
            for e in range(E):
                if e >= 2:
                    sp.wait_ge(s["wsp"], 2 * e - 2)
                sp.dma_start(w_stage[:, e % 2], A["wgu"][:, e]).then_inc(s_stage[e % 2], 16)
            sp.dma_start(keep.w2[:], A["w2"]).then_inc(s["w"], 16)
            sp.wait_ge(s["w"], 16)

        @block.gpsimd
        def _(pool):
            pool.tensor_tensor(x_bias[:], keep.x[:], rows[:, R_BO:R_BO + P].unsqueeze(1).to_broadcast(
                [P, NT, P]), ALU.add).then_inc(s["xb"], 1)
            pool.tensor_copy(delta[:], ident[:].unsqueeze(1).to_broadcast([P, 8, P])).then_inc(s["init"], 1)
            for c in range(2):
                pool.tensor_scalar(wout_n[:, c, :], keep.wout[:, c, :], vecs[:, V_NW + c:V_NW + c + 1], None,
                                   ALU.mult).then_inc(s["init"], 1)
            pool.memset(one[:], 1.0).then_inc(s["one"], 1)
            pool.wait_ge(s["one"], 1)
            for e in range(E):
                pool.wait_ge(s_stage[e % 2], 16 * (e // 2 + 1))
                src = w_stage[:, e % 2].rearrange("p g c -> p (g c)")
                hi = keep.w_hi[:, e].rearrange("p g c -> p (g c)")
                lo = keep.w_lo[:, e].rearrange("p g c -> p (g c)")
                pool.tensor_tensor(hi, src, one[:].to_broadcast([P, 2 * NH * HT]), ALU.mult).then_inc(s["wsp"], 1)
                pool.wait_ge(s["wsp"], 2 * e + 1)
                pool.tensor_tensor(lo, src, hi, ALU.subtract).then_inc(s["wsp"], 1)
            for c in range(4):
                pool.wait_ge(s["bcc"], c + 1)
                pool.memset(decay_all[:, c % 2, :].rearrange("p (c q) -> p c q", q=LQ)[:, :, 0:1],
                            0.0).then_inc(s["bc0"], 1)

        def turn_bank(t):
            return (pt[:, 0, 0:P], ps[:, 2, 0:P])[t % 2]

        def attn_bank(t):
            return (pt[:, 1, 0:P], ps[:, 2, 512:512 + P])[t % 2]

        @block.tensor
        def _(pe):
            def project(t):
                pe.wait_ge(s["otc"], t + 1)
                if t >= 2:
                    pe.wait_ge(s["x1"], t - 1)
                pe.matmul(attn_bank(t), oT[:, t % 2, :], keep.wo[:],
                          start=True, stop=True).then_inc(s["att"], 1)

            for t in range(NT + 1):
                if t < NT:
                    if t >= 2:
                        pe.wait_ge(s["o"], t - 1)
                    w = t % 2
                    for j in range(VH):
                        pe.transpose(ps[:, w, P * j:P * j + P], keep.sums[:, j, tok(t)], ident[:])
                    for j in range(VH):
                        r = 64 if j == 0 else 32
                        last = pe.transpose(ps[:, w, 512 + 64 * j:512 + 64 * j + r],
                                            keep.sums[0:r, VH + j, tok(t)], ident[0:r, 0:r])
                    last.then_inc(s["turn"], 1)
                if t >= 1:
                    pe.wait_ge(s["o"], t)
                    if t >= 3:
                        pe.wait_ge(s["otc"], t - 2)
                    pe.transpose(turn_bank(t - 1), o_tok[:, (t - 1) % 2, :],
                                 ident[:]).then_inc(s["ot"], 1)
                    project(t - 1)

            def turn_v(n):
                for t in range(NT):
                    pe.wait_ge(s["ln"], n * NT + t + 1)
                    last = pe.transpose(ps[:, 2, tok(t)], v[:, t, :], ident[:])
                    if t % 4 == 3:
                        last.then_inc(s["vt"], 1)

            pe.wait_ge(s["x1"], NT)
            turn_v(0)
            pe.wait_ge(s["vtc"], 2)
            for t in range(NT):
                last = pe.matmul(pt[:, 0, MH * t:MH * t + MH], vT[:, tok(t)], keep.win[:, 640:644],
                                 start=True, stop=True)
            last.then_inc(s["dtp"], 1)

            def wide(n, lhs, m, sink):
                for h in range(2):
                    last = pe.matmul(ps[0:m, n, 512 * h:512 * h + 512], lhs, vT[:, 512 * h:512 * h + 512],
                                     start=True, stop=True)
                last.then_inc(s[sink], 1)

            for c, (at, m) in enumerate([(256, P), (384, P), (512, 64), (576, 64)]):
                if c == 3:
                    pe.wait_ge(s["conv"], 1)
                wide(c % 3, keep.win[:, at:at + m], m, "mm")
            for c in range(2):
                pe.wait_ge(s["conv"], c + 2)
                wide(c + 1, keep.win[:, P * c:P * c + P], P, "zin")

            pe.wait_ge(s["dts"], DT_LAST)
            for c in range(4):
                w = [0, 1, 2, 0][c]
                if c == 0:
                    pe.wait_ge(s["conv"], 4)
                elif c < 3:
                    pe.wait_ge(s["zsil"], c)
                else:
                    pe.wait_ge(s["bcc"], 1)
                for t in range(2):
                    for h in range(MH):
                        last = pe.matmul(ps[:, w, P * (MH * t + h):P * (MH * t + h) + P],
                                         decay[:, 2 * c + t, h:h + 1].to_broadcast([P, P]), ident[:],
                                         start=True, stop=True)
                last.then_inc(s["bc"], 1)
            pe.wait_ge(s["silu"], 4)
            pe.wait_ge(s["bcc"], 2)
            for t in range(NT):
                last = pe.matmul(ps[:, 1, tok(t)], xbc[0:64, 2, tok(t)], xbc[0:64, 3, tok(t)],
                                 start=True, stop=True)
            last.then_inc(s["cb"], 1)
            pe.wait_ge(s["dts"], 2)
            for t in range(NT):
                if t >= 2:
                    pe.wait_ge(s["dtx"], t - 1)
                for c in range(2):
                    last = pe.transpose(pt[:, t % 2, P * c:P * c + P], xbc[:, c, tok(t)], ident[:])
                last.then_inc(s["xt"], 1)
            for h2 in range(2):
                w = [2, 0][h2]
                pe.wait_ge(s["bcc"], 3 + h2)
                pe.wait_ge(s["dtx"], 4 * h2 + 4)
                for t in range(4):
                    pe.wait_ge(s["mix"], 4 * h2 + t + 1)
                    for h in range(MH):
                        r = 64 * (h % 2)
                        last = pe.matmul(ps[r:r + 64, w, 512 * (h // 2) + P * t:512 * (h // 2) + P * t + P],
                                         dtx[:, 4 * h2 + t, 64 * h:64 * h + 64], mix[:, 4 * h2 + t, h, :],
                                         start=True, stop=True)
                last.then_inc(s["ya"], 1)
            pe.wait_ge(s["mix"], NT)
            pe.wait_ge(s["init"], 3)
            for t in range(NT):
                if t % 4 == 0:
                    pe.wait_ge(s["yc"], 2 * (t // 4) + 2)
                    pe.wait_ge(s["ysq"], 2 * (t // 4) + 2)
                for c in range(2):
                    pe.matmul(pt[:, 0, t:t + 1], y_sq[:, c, tok(t)], ones[:], start=(c == 0), stop=(c == 1))
                for c in range(2):
                    last = pe.matmul(ps[:, 1, tok(t)], y[:, c, tok(t)], wout_n[:, c, :],
                                     start=(c == 0), stop=(c == 1))
            last.then_inc(s["out"], 1)

            turn_v(1)
            pe.wait_ge(s["vtc"], 4)
            for c in range(4):
                w = [0, 1, 2, 0][c]
                if c == 1:
                    pe.wait_ge(s["y1"], NT)
                if c == 3:
                    pe.wait_ge(s["gelu"], 1)
                wide(w, keep.wfc[:, P * c:P * c + P], P, "fc")
            pe.wait_ge(s["gelu"], 4)
            for t in range(NT):
                for c in range(4):
                    last = pe.matmul(ps[:, 1, tok(t)], hid[:, c, tok(t)], keep.wproj[:, c, :],
                                     start=(c == 0), stop=(c == 3))
                if t % 4 == 3:
                    last.then_inc(s["pr"], 1)
            for t in range(NT):
                pe.wait_ge(s["ln"], 2 * NT + t + 1)
                last = pe.transpose(ps[:, 2, tok(t)], v[:, t, :], ident[:])
                if t % 4 == 3:
                    last.then_inc(s["vt"], 1)

        @block.scalar
        def _(act):
            def root(n, buf=rstd):
                act.wait_ge(s["st"], n)
                nc.scalar.activation(buf[:], buf[:], ACT.Sqrt).then_inc(s["sq"], 1)

            for t in range(NT):
                act.wait_ge(s["ot"], t + 1)
                if t >= 2:
                    act.wait_ge(s["att"], t - 1)
                nc.scalar.copy(oT[:, t % 2, :], turn_bank(t)).then_inc(s["otc"], 1)

            def turned(n, w, b):
                for h in range(2):
                    act.wait_ge(s["vt"], 2 * n + h + 1)
                    nc.scalar.activation(vT[:, 512 * h:512 * h + 512], ps[:, 2, 512 * h:512 * h + 512],
                                         ACT.Identity, bias=vecs[:, b:b + 1],
                                         scale=vecs[:, w:w + 1]).then_inc(s["vtc"], 1)

            root(ST1)
            root(ST2)
            turned(0, V_LN1W, V_LN1B)
            act.wait_ge(s["dts"], 4)
            nc.scalar.activation(dt_e[:], dt_a[:], ACT.Exp).then_inc(s["dte"], 1)
            nc.scalar.activation(a_exp[:], rows[:, R_ALOG:R_ALOG + MH], ACT.Exp).then_inc(s["dte"], 1)
            act.wait_ge(s["dts"], 5)
            nc.scalar.activation(dt_l[:], dt_u[:], ACT.Ln).then_inc(s["dte"], 1)
            act.wait_ge(s["dts"], DT_LAST - 1)
            nc.scalar.activation(decay[:], decay[:], ACT.Exp, scale=-1.0).then_inc(s["dts"], 1)
            for c in range(4):
                m = P if c < 2 else 64
                act.wait_ge(s["conv"], c + 1)
                nc.scalar.activation(xbc[0:m, c, :], conv[0:m, c, :], ACT.Silu).then_inc(s["silu"], 1)
            for c in range(2):
                act.wait_ge(s["zin"], c + 1)
                nc.scalar.activation(zg[:, c, :], ps[:, c + 1, :], ACT.Silu).then_inc(s["zsil"], 1)
            for c in range(4):
                w = [0, 1, 2, 0][c]
                act.wait_ge(s["bc"], c + 1)
                if c >= 2:
                    act.wait_ge(s["scan"], c - 1)
                nc.scalar.copy(decay_all[:, c % 2, :], ps[:, w, :]).then_inc(s["bcc"], 1)
            for h2 in range(2):
                for c in range(2):
                    act.wait_ge(s["yc"], 2 * h2 + c + 1)
                    nc.scalar.square(y_sq[:, c, 512 * h2:512 * h2 + 512],
                                     y[:, c, 512 * h2:512 * h2 + 512]).then_inc(s["ysq"], 1)
            act.wait_ge(s["r"], 2)
            nc.scalar.activation(rms[:], rms[:], ACT.Sqrt).then_inc(s["sq"], 1)
            root(ST3)
            turned(1, V_LN2W, V_LN2B)
            for c in range(4):
                w = [0, 1, 2, 0][c]
                act.wait_ge(s["fc"], c + 1)
                nc.scalar.activation(hid[:, c, :], ps[:, w, :], ACT.Gelu,
                                     bias=vecs[:, V_FCB + c:V_FCB + c + 1]).then_inc(s["gelu"], 1)
            root(ST4)
            for h in range(2):
                act.wait_ge(s["vt"], 4 + h + 1)
                nc.scalar.copy(keep.tT[:, 512 * h:512 * h + 512],
                               ps[:, 2, 512 * h:512 * h + 512]).then_inc(s["vtc"], 1)

        @block.vector
        def _(dve):
            st = [0]

            def norm(src, dst, n, out_sem, first):
                for t in range(NT):
                    first(t)
                    dve.bn_stats(stats[:, t, :], src[:, t, :]).then_inc(s["st"], 1)
                for t in range(NT):
                    dve.wait_ge(s["st"], st[0] + t + 1)
                    dve.bn_aggr(mean_var[:, t, :], stats[:, t, :]).then_inc(s["st"], 1)
                dve.wait_ge(s["st"], st[0] + 2 * NT)
                dve.tensor_scalar(rstd[:], mean_var[:, :, 1], EPS, None, ALU.add).then_inc(s["st"], 1)
                dve.wait_ge(s["st"], st[0] + 2 * NT + 1)
                dve.reciprocal(rstd[:], rstd[:]).then_inc(s["st"], 1)
                st[0] += 2 * NT + 2
                dve.wait_ge(s["sq"], n)
                for t in range(NT):
                    dve.tensor_scalar(dst[:, t, :], src[:, t, :], mean_var[:, t, 0:1], rstd[:, t:t + 1],
                                      ALU.subtract, ALU.mult).then_inc(s[out_sem], 1)

            dve.memset(ones[:], 1.0).then_inc(s["init"], 1)
            for t in range(NT + 1):
                if t < NT:
                    w = t % 2
                    dve.wait_ge(s["turn"], t + 1)
                    if t >= 2:
                        dve.wait_ge(s["ot"], t - 1)
                    pa = ps[:, w, 0:3 * P].rearrange("p (j g c) -> p j g c", j=VH, g=4)
                    pb_ = ps[:, w, 512:512 + 3 * 64].rearrange("p (j c) -> p j c", j=VH)
                    r = o_rden[:, w, :]
                    dve.reciprocal(r[:, 0:12].rearrange("p (j g) -> p j g", j=VH), pa[:, :, :, 0])
                    dve.reciprocal(r[:, 12:15], pb_[:, :, 0])
                    dve.reciprocal(r[:, 15:16], pb_[:, 0, 32:33]).then_inc(s["st"], 1)
                    st[0] += 1
                    dve.wait_ge(s["st"], st[0])
                    o4 = o_tok[:, w, 0:96].rearrange("p (g j c) -> p g j c", g=4, j=VH)
                    for j in range(VH):
                        dve.tensor_tensor(o4[:, :, j, :], pa[:, j, :, 1 + HD * j:1 + HD * j + HD],
                                          r[:, 4 * j:4 * j + 4].unsqueeze(2).to_broadcast([P, 4, HD]), ALU.mult)
                    for j in range(VH):
                        h = 12 + j
                        dve.tensor_scalar(o_tok[:, w, HD * h:HD * h + HD],
                                          pb_[:, j, 1 + HD * j:1 + HD * j + HD], r[:, h:h + 1], None, ALU.mult)
                    dve.tensor_scalar(o_tok[:, w, HD * 15:P], pb_[:, 0, 33:33 + HD], r[:, 15:16], None,
                                      ALU.mult).then_inc(s["st"], 1)
                    st[0] += 1
                    dve.wait_ge(s["st"], st[0])
                    dve.tensor_tensor(o_tok[:, w, :], o_tok[:, w, :], rows[:, R_BV:R_BV + P],
                                      ALU.add).then_inc(s["o"], 1)
                if t >= 1:
                    k = t - 1
                    if k == 0:
                        dve.wait_ge(s["xb"], 1)
                    dve.wait_ge(s["att"], k + 1)
                    dve.tensor_tensor(x1[:, k, :], x_bias[:, k, :], attn_bank(k),
                                      ALU.add).then_inc(s["x1"], 1)
            norm(x1, u, 1, "st", lambda t: dve.wait_ge(s["x1"], t + 1))
            base = st[0]
            st[0] += NT
            norm(u, v, 2, "ln", lambda t: dve.wait_ge(s["st"], base + t + 1))

            n = [0]

            def step(ins):
                n[0] += 1
                ins.then_inc(s["dts"], 1)
                dve.wait_ge(s["dts"], n[0])

            def per_head(ap):
                return ap.unsqueeze(1).to_broadcast([P, NT, MH])

            dve.wait_ge(s["dtp"], 1)
            step(dve.tensor_tensor(dt_x[:], pt[:, 0, 0:MH * NT].rearrange("p (t h) -> p t h", h=MH),
                                   per_head(rows[:, R_DTB:R_DTB + MH]), ALU.add))
            step(dve.tensor_scalar(dt_a[:], dt_x[:], -1.0, None, ALU.mult))
            step(dve.tensor_tensor(dt_a[:], dt_a[:], dt_x[:], ALU.min))
            step(dve.tensor_scalar(dt[:], dt_x[:], 0.0, None, ALU.max))
            dve.wait_ge(s["dte"], 2)
            step(dve.tensor_scalar(dt_u[:], dt_e[:], 1.0, None, ALU.add))
            step(dve.tensor_scalar(dt_a[:], dt_u[:], -1.0, None, ALU.add))
            step(dve.tensor_scalar(dt_m[:], dt_a[:], 0.0, None, ALU.is_equal))
            step(dve.tensor_tensor(dt_a[:], dt_a[:], dt_m[:], ALU.add))
            step(dve.reciprocal(dt_a[:], dt_a[:]))
            step(dve.tensor_tensor(dt_a[:], dt_a[:], dt_e[:], ALU.mult))
            dve.wait_ge(s["dte"], 3)
            step(dve.tensor_tensor(dt_m[:], dt_m[:], dt_l[:], ALU.add))
            step(dve.tensor_tensor(dt_m[:], dt_m[:], dt_a[:], ALU.mult))
            step(dve.tensor_tensor(dt[:], dt[:], dt_m[:], ALU.add))
            step(dve.tensor_tensor(decay[:], dt[:], per_head(a_exp[:, 0:MH]), ALU.mult))
            assert n[0] == DT_LAST - 1

            for c in range(4):
                m = P if c < 2 else 64
                dve.wait_ge(s["mm"], c + 1)
                src = ps[0:m, c % 3, :].rearrange("p (b q) -> p b q", b=B)
                dst = conv[0:m, c, :].rearrange("p (b q) -> p b q", b=B)
                cw = vecs[0:m, V_CW + 4 * c:V_CW + 4 * c + 4]
                dve.tensor_scalar(dst, src, cw[:, 3:4], vecs[0:m, V_CB + c:V_CB + c + 1],
                                  ALU.mult, ALU.add).then_inc(s["yb"], 1)
                for k in range(1, 4):
                    dve.wait_ge(s["yb"], 3 * c + k)
                    dve.scalar_tensor_tensor(out=dst[:, :, k:], in0=src[:, :, 0:LQ - k],
                                             scalar=cw[:, 3 - k:4 - k], in1=dst[:, :, k:],
                                             op0=ALU.mult, op1=ALU.add).then_inc(s["conv" if k == 3 else "yb"], 1)
            for c in range(4):
                dve.wait_ge(s["bc0"], c + 1)
                if c == 0:
                    dve.wait_ge(s["init"], 4)
                dve.tensor_tensor_scan(gain[:, c % 2, :], decay_all[:, c % 2, :],
                                       delta[:].rearrange("p c q -> p (c q)"), 0.0,
                                       ALU.mult, ALU.add).then_inc(s["scan"], 1)
                if c == 0:
                    dve.wait_ge(s["cb"], 1)
                    dve.wait_ge(s["dts"], DT_LAST)
                dve.wait_ge(s["scan"], c + 1)
                for t in (2 * c, 2 * c + 1):
                    dve.tensor_tensor(mix[:, t, :, :], gain[:, c % 2, 512 * (t % 2):512 * (t % 2) + 512].rearrange(
                        "p (h q) -> p h q", h=MH), ps[:, 1, tok(t)].unsqueeze(1).to_broadcast([P, MH, P]),
                        ALU.mult).then_inc(s["mix"], 1)
                for t in (2 * c, 2 * c + 1):
                    dve.wait_ge(s["xt"], t + 1)
                    dve.tensor_tensor(dtx[:, t, :].rearrange("p (h c) -> p h c", h=MH),
                                      pt[:, t % 2, 0:2 * P].rearrange("p (h c) -> p h c", h=MH),
                                      dt[:, t, :].unsqueeze(2).to_broadcast([P, MH, 64]),
                                      ALU.mult).then_inc(s["dtx"], 1)
            for h2 in range(2):
                w = [2, 0][h2]
                dve.wait_ge(s["ya"], h2 + 1)
                if h2 == 0:
                    dve.wait_ge(s["zsil"], 2)
                for c in range(2):
                    half = slice(512 * h2, 512 * h2 + 512)
                    dve.scalar_tensor_tensor(out=y[:, c, half], in0=xbc[:, c, half],
                                             scalar=vecs[:, V_D + c:V_D + c + 1],
                                             in1=ps[:, w, 512 * c:512 * c + 512],
                                             op0=ALU.mult, op1=ALU.add).then_inc(s["yb"], 1)
                    dve.wait_ge(s["yb"], 12 + 2 * h2 + c + 1)
                    dve.tensor_tensor(y[:, c, half], y[:, c, half], zg[:, c, half],
                                      ALU.mult).then_inc(s["yc"], 1)
            dve.wait_ge(s["out"], 1)
            dve.tensor_scalar(rms[:], pt[:, 0, 0:NT], 1.0 / 256, EPS, ALU.mult, ALU.add).then_inc(s["r"], 1)
            dve.wait_ge(s["r"], 1)
            dve.reciprocal(rms[:], rms[:]).then_inc(s["r"], 1)
            dve.wait_ge(s["sq"], 3)
            for t in range(NT):
                dve.scalar_tensor_tensor(out=y1[:, t, :], in0=ps[:, 1, tok(t)], scalar=rms[:, t:t + 1],
                                         in1=u[:, t, :], op0=ALU.mult, op1=ALU.add).then_inc(s["y1"], 1)
            norm(y1, v, 4, "ln", lambda t: dve.wait_ge(s["y1"], t + 1))
            dve.tensor_tensor(keep.x[:], x1[:], y1[:], ALU.add).then_inc(s["r"], 1)
            dve.wait_ge(s["r"], 3)
            dve.tensor_tensor(keep.x[:], keep.x[:], rows[:, R_PB:R_PB + P].unsqueeze(1).to_broadcast([P, NT, P]),
                              ALU.add).then_inc(s["r"], 1)
            dve.wait_ge(s["r"], 4)
            for t in range(NT):
                dve.wait_ge(s["pr"], t // 4 + 1)
                dve.tensor_tensor(keep.x[:, t, :], keep.x[:, t, :], ps[:, 1, tok(t)], ALU.add).then_inc(s["x2"], 1)
            norm(keep.x, v, 5, "ln", lambda t: dve.wait_ge(s["x2"], t + 1))


def experts(nc, A, keep, out):
    with ExitStack() as ctx:
        def sb(name, shape, dt=F32):
            return ctx.enter_context(nc.sbuf_tensor(name, shape, dt))

        def pb(name, shape, dt=F32):
            return ctx.enter_context(nc.psum_tensor(name, shape, dt))

        def sem(name):
            return ctx.enter_context(nc.semaphore(name))

        tT, ident = keep.tT, keep.ident
        cent = sb("cent", [P, E])
        bgu = sb("bgu", [HT, E, 2, NH])
        b2 = sb("b2", [E, P])
        gate_bias = sb("gate_bias", [HT, 2, NH])
        ones = sb("ones_p", [P, P])
        t_hi = sb("t_hi", [P, T], BF16)
        t_lo = sb("t_lo", [P, T], BF16)
        w_hi, w_lo = keep.w_hi, keep.w_lo
        t_sq = sb("t_sq", [P, T])
        cent_sq = sb("cent_sq", [P, E])
        norms = sb("norms", [P, NT])
        cnorm = sb("cnorm", [P, E])
        dist2 = sb("dist2", [P, NT, E])
        top = sb("top", [P, NT, 8])
        top_i = sb("top_i", [P, NT, 8], mybir.dt.uint32)
        top_f = sb("top_f", [P, NT, 2])
        far = sb("far", [P, NT, 2])
        wts = sb("wts", [P, NT, 2])
        gap = sb("gap", [P, NT])
        pick = sb("pick", [P, NT, E])
        we = sb("we", [P, NT, E])
        weT = sb("weT", [E, NT, P])
        gate = sb("gate", [HT, 2, 512])
        hid = sb("hid_e", [HT, 2, NH, 512])
        acc = sb("acc", [P, NT, P])

        gu = pb("gu", [P, 2, 2, 512])
        down = pb("down", [P, 2, 512])
        small = pb("small", [P, 2, 512])

        names = "w c gb sp tsq csq nrm rt top te sel weT wtc gu gate hid down acc b2 out"
        s = {n: sem("e_" + n) for n in names.split()}
        block = ctx.enter_context(nc.Block())

        def tok(t):
            return slice(t * P, t * P + P)

        def per_expert(eng, up, down, route):
            up(0, 0, 0)
            route(0)
            up(0, 1, 0)
            route(1)
            down(0, 0)
            up(1, 0, 1)
            down(0, 1)

            def body(e, par, more):
                up(e, 1, par)
                down(e, 0)
                if more:
                    up(e + 1, 0, 1 - par)
                down(e, 1)

            with eng.Fori(0, E // 2 - 1) as j:
                body(j * 2 + 1, 1, True)
                body(j * 2 + 2, 0, True)
            body(E - 1, 1, False)

        @block.sync
        def _(sp):
            sp.dma_start(cent[:], A["cent"]).then_inc(s["w"], 16)
            sp.dma_start(bgu[:], A["bgu"]).then_inc(s["w"], 16)
            sp.dma_start(b2[:], A["b2"]).then_inc(s["w"], 16)
            for t in range(NT):
                sp.wait_ge(s["out"], t + 1)
                sp.dma_start(out[t * P:t * P + P, :], acc[:, t, :]).then_inc(s["w"], 16)
            sp.wait_ge(s["w"], (3 + NT) * 16)

        @block.gpsimd
        def _(pool):
            pool.memset(ones[:], 1.0).then_inc(s["c"], 1)
            pool.wait_ge(s["w"], 48)
            pool.tensor_tensor(cent_sq[:], cent[:], cent[:], ALU.mult).then_inc(s["csq"], 1)

        @block.tensor
        def _(pe):
            def route(step):
                if step:
                    return
                pe.wait_ge(s["c"], 1)
                pe.wait_ge(s["csq"], 1)
                pe.wait_ge(s["tsq"], 1)
                for t in range(NT):
                    pe.matmul(small[:, 0, t:t + 1], t_sq[:, tok(t)], ones[:, 0:1], start=True, stop=True)
                pe.matmul(small[:, 0, 8:8 + E], ones[:], cent_sq[:], start=True, stop=True)
                for t in range(NT):
                    last = pe.matmul(small[:, 0, 64 + E * t:64 + E * t + E], tT[:, tok(t)], cent[:],
                                     start=True, stop=True)
                last.then_inc(s["nrm"], 1)

            def finish(e, h):
                pe.wait_ge(s["hid"], e * 6 + (3 * h + 3 + 2))
                pe.wait_ge(s["acc"], e * 2 + (h + 1))
                for t in range(4):
                    for n in range(NH):
                        last = pe.matmul(down[:, h, P * t:P * t + P], hid[:, h, n, P * t:P * t + P],
                                         keep.w2[:, bass.ds(e, 1), n, :].rearrange("p e c -> p (e c)"),
                                         start=(n == 0), stop=(n == NH - 1))
                last.then_inc(s["down"], 1)

            def up(e, h, par):
                half = slice(512 * h, 512 * h + 512)
                for n in range(NH):
                    w = (3 * h + n) % 2
                    pe.wait_ge(s["hid"], e * 6 + (3 * h + n + 1))
                    for k in range(2):
                        o = gu[0:HT, w, k, :]
                        hi = w_hi[:, bass.ds(e, 1), k, HT * n:HT * n + HT].rearrange("p e c -> p (e c)")
                        lo = w_lo[:, bass.ds(e, 1), k, HT * n:HT * n + HT].rearrange("p e c -> p (e c)")
                        pe.matmul(o, hi, t_hi[:, half], start=True, stop=False)
                        pe.matmul(o, hi, t_lo[:, half], start=False, stop=False)
                        last = pe.matmul(o, lo, t_hi[:, half], start=False, stop=True)
                    last.then_inc(s["gu"], 1)

            pe.wait_ge(s["sp"], 2)
            per_expert(pe, up, finish, route)
            pe.wait_ge(s["sel"], 1)
            for t in range(NT):
                last = pe.transpose(small[0:E, t // 4, P * (t % 4):P * (t % 4) + P], we[:, t, :], ident[:])
            last.then_inc(s["weT"], 1)
            pe.wait_ge(s["wtc"], 2)
            for t in range(NT):
                last = pe.matmul(gu[:, 0, t // 4, P * (t % 4):P * (t % 4) + P], weT[:, t, :], b2[:],
                                 start=True, stop=True)
            last.then_inc(s["b2"], 1)

        @block.scalar
        def _(act):
            nc.scalar.square(t_sq[:], tT[:]).then_inc(s["tsq"], 1)

            def route(step):
                if step == 0:
                    act.wait_ge(s["top"], NT + 1)
                    nc.scalar.activation(far[:], far[:], ACT.Sqrt).then_inc(s["te"], 1)
                    act.wait_ge(s["rt"], 6)
                    nc.scalar.activation(gap[:], gap[:], ACT.Exp).then_inc(s["te"], 1)
            act.wait_ge(s["w"], 48)

            def gates(e, h, par):
                if h == 0:
                    nc.scalar.copy(gate_bias[:, par, :], bgu[:, bass.ds(e, 1), 0, :].rearrange(
                        "p e c -> p (e c)")).then_inc(s["gb"], 1)
                    act.wait_ge(s["gb"], e + 1)
                for n in range(NH):
                    w = (3 * h + n) % 2
                    act.wait_ge(s["gu"], e * 6 + (3 * h + n + 1))
                    act.wait_ge(s["hid"], e * 6 + (3 * h + n + 1))
                    nc.scalar.activation(gate[:, w, :], gu[0:HT, w, 0, :], ACT.Silu,
                                         bias=gate_bias[:, par, n:n + 1]).then_inc(s["gate"], 1)

            per_expert(act, gates, lambda e, h: None, route)
            for h in range(2):
                act.wait_ge(s["weT"], 1)
                nc.scalar.copy(weT[:, 4 * h:4 * h + 4, :].rearrange("p t c -> p (t c)"),
                               small[0:E, h, :]).then_inc(s["wtc"], 1)

        @block.vector
        def _(dve):
            dve.sem_inc(s["hid"], 2)
            dve.sem_inc(s["acc"], 2)
            dve.tensor_copy(t_hi[:], tT[:]).then_inc(s["sp"], 1)
            dve.wait_ge(s["sp"], 1)
            dve.tensor_tensor(t_lo[:], tT[:], t_hi[:], ALU.subtract).then_inc(s["sp"], 1)
            n = [0]

            def step(ins):
                n[0] += 1
                ins.then_inc(s["rt"], 1)
                dve.wait_ge(s["rt"], n[0])

            def per_expert_of(ap):
                return ap.to_broadcast([P, NT, E])

            def route(part):
                if part == 0:
                    dve.wait_ge(s["nrm"], 1)
                    step(dve.tensor_copy(cnorm[:], small[:, 0, 8:8 + E]))
                    step(dve.tensor_copy(norms[:], small[:, 0, 0:NT]))
                    step(dve.scalar_tensor_tensor(out=dist2[:], in0=small[:, 0, 64:64 + E * NT].rearrange(
                        "p (t e) -> p t e", e=E), scalar=-2.0, in1=per_expert_of(cnorm[:].unsqueeze(1)),
                        op0=ALU.mult, op1=ALU.add))
                    step(dve.tensor_tensor(dist2[:], dist2[:], per_expert_of(norms[:].unsqueeze(2)), ALU.add))
                    step(dve.tensor_scalar(dist2[:], dist2[:], 1e-12, None, ALU.max))
                    for t in range(NT):
                        dve.max(top[:, t, :], dist2[:, t, :]).then_inc(s["top"], 1)
                    dve.wait_ge(s["top"], NT)
                    dve.tensor_copy(far[:], top[:, :, 0:2]).then_inc(s["top"], 1)
                    for t in range(NT):
                        last = dve.max_index(top_i[:, t, :], top[:, t, :], dist2[:, t, :])
                    last.then_inc(s["top"], 1)
                    dve.wait_ge(s["te"], 1)
                    step(dve.tensor_tensor(gap[:], far[:, :, 1], far[:, :, 0], ALU.subtract))
                    return
                dve.wait_ge(s["top"], NT + 2)
                step(dve.tensor_copy(top_f[:], top_i[:, :, 0:2]))
                dve.wait_ge(s["te"], 2)
                step(dve.tensor_scalar(wts[:, :, 0], gap[:], 1.0, None, ALU.add))
                step(dve.reciprocal(wts[:, :, 0], wts[:, :, 0]))
                step(dve.tensor_tensor(wts[:, :, 1], wts[:, :, 0], gap[:], ALU.mult))
                for k, to in ((0, pick), (1, we)):
                    step(dve.tensor_tensor(to[:], per_expert_of(keep.iota[:].unsqueeze(1)),
                                           per_expert_of(top_f[:, :, k:k + 1]), ALU.is_equal))
                    step(dve.tensor_tensor(to[:], to[:], per_expert_of(wts[:, :, k:k + 1]), ALU.mult))
                dve.tensor_tensor(we[:], we[:], pick[:], ALU.add).then_inc(s["sel"], 1)
                dve.tensor_copy(acc[:], keep.x[:]).then_inc(s["sel"], 1)
                dve.wait_ge(s["sel"], 2)

            def weigh(e, h):
                dve.wait_ge(s["down"], e * 2 + (h + 1))
                for t in range(4):
                    k = 4 * h + t
                    last = dve.scalar_tensor_tensor(
                        out=acc[:, k, :], in0=down[:, h, P * t:P * t + P],
                        scalar=we[:, k, bass.ds(e, 1)], in1=acc[:, k, :], op0=ALU.mult, op1=ALU.add)
                last.then_inc(s["acc"], 1)

            def hidden(e, h, par):
                for n in range(NH):
                    w = (3 * h + n) % 2
                    dve.wait_ge(s["gate"], e * 6 + (3 * h + n + 1))
                    dve.scalar_tensor_tensor(
                        out=hid[:, h, n, :], in0=gu[0:HT, w, 1, :],
                        scalar=bgu[:, bass.ds(e, 1), 1, n:n + 1].rearrange("p e c -> p (e c)"),
                        in1=gate[:, w, :], op0=ALU.add, op1=ALU.mult).then_inc(s["hid"], 1)

            per_expert(dve, hidden, weigh, route)
            dve.wait_ge(s["b2"], 1)
            dve.wait_ge(s["acc"], 2 * E + 2)
            for t in range(NT):
                dve.tensor_tensor(acc[:, t, :], acc[:, t, :], gu[:, 0, t // 4, P * (t % 4):P * (t % 4) + P],
                                  ALU.add).then_inc(s["out"], 1)


class Keep:
    pass


def program(nc, A, out):
    with ExitStack() as ctx:
        def sb(name, shape, dt=F32):
            return ctx.enter_context(nc.sbuf_tensor("keep_" + name, shape, dt))

        keep = Keep()
        keep.x = sb("x", [P, NT, P])
        keep.ident = sb("ident", [P, P])
        keep.marks = sb("marks", [P, GH + 2])
        keep.vecs = sb("vecs", [P, NV])
        keep.rows = sb("rows", [P, NR])
        keep.iota = sb("iota", [P, E])
        keep.sums = sb("sums", [P, 2 * VH, T])
        keep.wo = sb("wo", [P, P])
        keep.win = sb("win", [P, 644])
        keep.wout = sb("wout", [P, 2, P])
        keep.wfc = sb("wfc", [P, 4 * P])
        keep.wproj = sb("wproj", [P, 4, P])
        attention(nc, A, keep)
        keep.tT = sb("tT", [P, T])
        keep.w_hi = sb("w_hi", [P, E, 2, NH * HT], BF16)
        keep.w_lo = sb("w_lo", [P, E, 2, NH * HT], BF16)
        keep.w2 = sb("w2", [HT, E, NH, P])
        mamba_mlp(nc, A, keep)
        experts(nc, A, keep, out)


def lay_out(a):
    import numpy as np
    f = np.float32
    g = {k.replace("L0_", ""): np.asarray(v) for k, v in a.items()}
    wq = np.zeros((P, G, 4, GH, HD), f)
    bq = np.zeros((4, GH, HD, G), f)
    wq[:, :, :3] = g["xattn_Wq"].T.reshape(P, G, 1, GH, HD)
    bq[:3] = g["xattn_bq"].reshape(G, GH, HD).transpose(1, 2, 0)
    marks = np.zeros((4, GH, HD, GH + 2), f)
    for h in range(GH):
        marks[:3, h, :, h] = 1
    marks[1, :, :, GH] = -1
    marks[0, 1, :, GH + 1] = -1

    wk = g["xattn_Wk"].T.reshape(P, G, GH, HD).transpose(0, 2, 3, 1)
    bk = g["xattn_bk"].reshape(G, GH, HD).transpose(1, 2, 0)

    def cols(v):
        return v.reshape(-1, P).T

    conv = np.zeros((4, P, 5), f)
    for i, (at, m) in enumerate([(0, P), (P, P), (2 * P, 64), (2 * P + 64, 64)]):
        conv[i, :m, :4] = g["attn_conv_w"][at:at + m]
        conv[i, :m, 4] = g["attn_conv_b"][at:at + m]
    vecs = np.concatenate([
        cols(bk.reshape(-1)), bq.reshape(P, G), cols(g["attn_ln1_w"]), cols(g["attn_ln1_b"]),
        cols(g["attn_ln2_w"]), cols(g["attn_ln2_b"]), conv[:, :, :4].transpose(1, 0, 2).reshape(P, 16), conv[:, :, 4].T,
        cols(np.repeat(g["attn_D_param"], 64)), cols(g["attn_norm_w"]), cols(g["attn_fc_b"])], 1)
    rows = np.concatenate([g["xattn_bv"], g["xattn_bo"], g["attn_proj_b"], g["attn_A_log"],
                           g["attn_dt_bias"]])[None]
    c = np.ascontiguousarray
    return {
        "x": c(g["x"].reshape(T, P)),
        "ctx": c(g["ctx_1024"].transpose(2, 0, 1)),
        "ident": np.eye(P, dtype=f),
        "nident": -np.eye(P, dtype=f),
        "marks": marks.reshape(P, GH + 2),
        "vecs": c(vecs),
        "iota": np.tile(np.arange(E, dtype=f), (P, 1)),
        "rows": c(rows),
        "wkv": c(np.stack([wk.reshape(P, P), g["xattn_Wv"].T], 1)),
        "wq": wq.reshape(P, G, P),
        "wo": c(g["xattn_Wo"].T),
        "win": c(g["attn_in_proj_w"].T),
        "wout": c(g["attn_out_proj_w"].T.reshape(2, P, P).transpose(1, 0, 2)),
        "wfc": c(g["attn_fc_w"].T),
        "wproj": c(g["attn_proj_w"].T.reshape(4, P, P).transpose(1, 0, 2)),
        "cent": c(g["ffn_centroid"].T),
        "wgu": c(np.stack([g["ffn_Wg"], g["ffn_W1"]], 0).transpose(2, 1, 0, 3)),
        "bgu": c(np.stack([g["ffn_bg"], g["ffn_b1"]], 0).reshape(2, E, NH, HT).transpose(3, 1, 0, 2)),
        "w2": c(g["ffn_W2"].reshape(E, NH, HT, P).transpose(2, 0, 1, 3)),
        "b2": c(g["ffn_b2"]),
    }


def kernel(**inputs):
    import numpy as np
    import concourse.bacc as bacc
    from concourse.bass_utils import run_bass_kernel_spmd

    nc = bacc.Bacc("TRN2", target_bir_lowering=False, num_devices=1)
    arrays = lay_out(inputs)
    aps = {k: nc.dram_tensor(f"in_{k}", v.shape, F32, kind="ExternalInput").ap()
           for k, v in arrays.items()}
    out = nc.dram_tensor("out_0", (T, P), F32, kind="ExternalOutput").ap()
    program(nc, aps, out)
    r = run_bass_kernel_spmd(nc, [{f"in_{k}": v for k, v in arrays.items()}], core_ids=[0])
    return np.asarray(r.results[0]["out_0"]).reshape(B, LQ, P)
```

```python
from contextlib import ExitStack

import concourse.bass as bass
from concourse import mybir

ALU = mybir.AluOpType
ACT = mybir.ActivationFunctionType
AX = mybir.AxisListType
F32 = mybir.dt.float32
BF16 = mybir.dt.bfloat16

P = 128
B, LQ, LK = 16, 64, 1601
H, HD = 16, 8
T = B * LQ
NT = T // P
EPS = 1e-5

G = 4
GH = H // G
SHIFT = 96
NK = (LK + P - 1) // P
CH = 401
CHUNKS = [(0, CH), (CH, CH), (2 * CH, CH), (3 * CH, LK - 3 * CH)]
VG, VH = 6, 3
RING = 23
PER = 21

V_BK, V_BQ, V_LN1W, V_LN1B, V_LN2W, V_LN2B = 0, 1, 5, 6, 7, 8
V_CW, V_CB, V_D, V_NW, V_FCB = 9, 21, 24, 26, 28
NV = 32
R_BV, R_BO, R_PB, R_ALOG, R_DTB = 0, 128, 256, 384, 388
NR = 392

MH = 4
E, NH, HT = 8, 3, 114
DT_LAST = 15


def keys_of(k):
    return min(P, LK - k * P)


def attention(nc, A, keep):
    with ExitStack() as ctx:
        def sb(name, shape, dt=F32):
            return ctx.enter_context(nc.sbuf_tensor(name, shape, dt))

        def pb(name, shape, dt=F32):
            return ctx.enter_context(nc.psum_tensor(name, shape, dt))

        def sem(name):
            return ctx.enter_context(nc.semaphore(name))

        wq = sb("wq", [P, G, P])
        wkv = sb("wkv", [P, 2, P])
        wkv_hi = sb("wkv_hi", [P, 2, P], BF16)
        wkv_lo = sb("wkv_lo", [P, 2, P], BF16)
        one = sb("one", [P, 1])
        nident = sb("nident", [P, P])
        bq_scaled = sb("bq_scaled", [P, G])
        stats = sb("stats", [P, NT, 6])
        mean_var = sb("mean_var", [P, NT, 2])
        rstd = sb("rstd", [P, NT])
        xn = sb("xn", [P, NT, P])
        xnT = sb("xnT", [P, T])
        q_full = sb("q_full", [P, 2, T])
        q_hi = sb("q_hi", [P, 2, T], BF16)
        q_part = sb("q_part", [P, 2, T], BF16)
        q_stack = sb("q_stack", [P, B, G, GH, LQ], BF16)
        ctx_in = sb("ctx_in", [P, 2, LK])
        ctx_hi = sb("ctx_hi", [P, 2, LK], BF16)
        ctx_lo = sb("ctx_lo", [P, 2, LK], BF16)
        k_hi = sb("k_hi", [P, LK], BF16)
        k_lo = sb("k_lo", [P, LK], BF16)
        k_stack = sb("k_stack", [P, 2, G, LK], BF16)
        q_cur = sb("q_cur", [P, 2, G * GH * LQ], BF16)
        values = sb("values", [P, 2, NK, VG * 32])
        probs = sb("probs", [P, 2, H * LQ])
        half_max = sb("half_max", [P, 8, 2])
        row_max = sb("row_max", [P, 16])
        shift_hi = sb("shift_hi", [16, P], BF16)
        shift = sb("shift", [16, P], BF16)

        wide = pb("wide", [P, 2, 1024])
        score = pb("score", [P, 2, 512])
        sums = pb("sums", [P, 2, 512])

        s_const = sem("s_const")
        s_later = sem("s_later")
        s_x = sem("s_x")
        s_ctx = [sem(f"s_ctx{i}") for i in range(2)]
        s_wsplit = sem("s_wsplit")
        s_memset = sem("s_memset")
        s_one = sem("s_one")
        s_stat = sem("s_stat")
        s_sqrt = sem("s_sqrt")
        s_xn = sem("s_xn")
        s_xt = sem("s_xt")
        s_xtc = sem("s_xtc")
        s_bq = sem("s_bq")
        s_q = sem("s_q")
        s_qf = sem("s_qf")
        s_qh = sem("s_qh")
        s_qp = sem("s_qp")
        s_ql = sem("s_ql")
        s_ones = sem("s_ones")
        s_qs = sem("s_qs")
        s_split = sem("s_split")
        s_wide = sem("s_wide")
        s_wfree = sem("s_wfree")
        s_khi = sem("s_khi")
        s_stack = [sem(f"s_stack{i}") for i in range(2)]
        s_rowmax = sem("s_rowmax")
        s_shift = sem("s_shift")
        s_shin = [sem(f"s_shin{i}") for i in range(2)]
        s_score = sem("s_score")
        s_last = sem("s_last")
        s_exp = sem("s_exp")
        s_pv = sem("s_pv")
        s_sums = sem("s_sums")
        SHIN_N, STACK_N = 16, 4 * 16

        block = ctx.enter_context(nc.Block())

        def run(e, body):
            body(-1, -1, 1)
            with e.Fori(0, B // 2 - 1) as j:
                body(j * 2, j, 0)
                body(j * 2 + 1, j, 1)
            body(B - 2, B // 2 - 1, 0)
            body(B - 1, B // 2 - 1, 1)

        def has(i, ahead):
            return not isinstance(i, int) or 0 <= i + ahead < B

        def slot(par, ahead):
            return (par + ahead) % 2

        def k_slot(par, k):
            return (par * NK + k) % 2

        def ring(i, use):
            if isinstance(i, int) and i == B - 2 and use > 18:
                raise ValueError("no keys any more")
            return i * PER + (RING + use)

        def ring_slot(par, use):
            return (par * PER + RING + use) % 2

        @block.sync
        def _(sp):
            sp.dma_start(keep.x[:], A["x"].rearrange("(t p) d -> p t d", p=P)).then_inc(s_x, 16)
            sp.dma_start(keep.ident[:], A["ident"]).then_inc(s_const, 16)
            sp.dma_start(nident[:], A["nident"]).then_inc(s_const, 16)
            sp.dma_start(keep.marks[:], A["marks"]).then_inc(s_const, 16)
            sp.dma_start(keep.vecs[:], A["vecs"]).then_inc(s_const, 16)
            sp.dma_start(wkv[:], A["wkv"]).then_inc(s_const, 16)
            sp.dma_start(wq[:], A["wq"]).then_inc(s_const, 16)
            sp.dma_start(ctx_in[:, 0, :], A["ctx"][:, 0, :]).then_inc(s_ctx[0], 16)
            sp.dma_start(ctx_in[:, 1, :], A["ctx"][:, 1, :]).then_inc(s_ctx[1], 16)

            def value(v):
                if isinstance(v, int):
                    return v
                r = sp.alloc_register(f"wait_value{len(held)}")
                held.append(r)
                sp.reg_mov(r, v)
                return sp.snap(r, min_val=1)

            held = []

            for to, of in ((keep.iota, A["iota"]), (keep.wo, A["wo"]), (keep.win, A["win"]), (keep.wout, A["wout"]),
                           (keep.wfc, A["wfc"]), (keep.wproj, A["wproj"])):
                sp.dma_start(to[:], of).then_inc(s_later, 16)
            sp.dma_start(keep.rows[:], A["rows"].to_broadcast([P, NR])).then_inc(s_later, 16)

            def body(i, j, par):
                n = slot(par, 1)
                if has(i, 1):
                    high_there, scores_done, low_there = value(i * 4 + 8), value(i + 1), value(ring(i, 0))
                    sp.wait_ge(s_khi, high_there)
                    if has(i, -1):
                        sp.wait_ge(s_last, scores_done)
                    first = isinstance(i, int) and i < 0
                    if first:
                        sp.wait_ge(s_memset, 1)
                    for c in range(2):
                        sp.dma_start(k_stack[32 * c:32 * c + 32, n, :, :], k_hi[:, :]).then_inc(s_stack[n], 16)
                    def queries():
                        sp.dma_start(q_cur[:, n, :], q_stack[:, bass.ds(i + 1, 1), :, :, :].rearrange(
                            "p b g h q -> p (b g h q)")).then_inc(s_stack[n], 16)

                    if not first:
                        queries()
                    sp.wait_ge(s_wfree, low_there)
                    sp.dma_start(k_stack[64:96, n, :, :], k_lo[:, :]).then_inc(s_stack[n], 16)
                    if first:
                        sp.wait_ge(s_qs, G)
                        sp.wait_ge(s_ql, G)
                        queries()
                        sp.wait_ge(s_memset, 2)
                if has(i, 2) and has(i, 0):
                    sp.dma_start(ctx_in[:, par, :], A["ctx"][:, bass.ds(i + 2, 1), :].rearrange(
                        "p b k -> p (b k)")).then_inc(s_ctx[par], 16)
                if has(i, 1):
                    sp.wait_ge(s_wfree, ring(i, 18) + 1)
                    sp.dma_start(q_cur[SHIFT:SHIFT + 2, n, :], shift[:, :]).then_inc(s_shin[n], 16)

            run(sp, body)
            sp.wait_ge(s_later, 7 * 16)

        @block.gpsimd
        def _(pool):
            pool.memset(one[:], 1.0).then_inc(s_one, 1)
            pool.wait_ge(s_one, 1)
            pool.memset(k_stack[:, 0, :, :], 1.0).then_inc(s_memset, 1)

            def split(i, j, par, ahead):
                n = slot(par, ahead)
                pool.wait_ge(s_ctx[n], (j + (par + ahead) // 2 + 1) * 16)
                if has(i, ahead - 2):
                    pool.wait_ge(s_wide, ring(i + (ahead - 3), 1) + 1)
                pool.tensor_tensor(ctx_hi[:, n, :], ctx_in[:, n, :], one[:].to_broadcast([P, LK]),
                                   ALU.mult).then_inc(s_split, 1)
                pool.wait_ge(s_split, (i + ahead) * 2 + 1)
                pool.tensor_tensor(ctx_lo[:, n, :], ctx_in[:, n, :], ctx_hi[:, n, :],
                                   ALU.subtract).then_inc(s_split, 1)

            split(-1, -1, 1, 1)
            pool.memset(k_stack[:, 1, :, :], 1.0).then_inc(s_memset, 1)

            def body(i, j, par):
                if has(i, 2):
                    split(i, j, par, 2)

            run(pool, body)

        @block.tensor
        def _(pe):
            def product3(out, lhs_hi, lhs_lo, rhs_hi, rhs_lo):
                pe.matmul(out, lhs_hi, rhs_hi, start=True, stop=False)
                pe.matmul(out, lhs_hi, rhs_lo, start=False, stop=False)
                return pe.matmul(out, lhs_lo, rhs_hi, start=False, stop=True)

            def keys(i, par, ahead, half, use):
                n, w = slot(par, ahead), use[1]
                if half == 0:
                    pe.wait_ge(s_split, (i + ahead + 1) * 2)
                if not isinstance(use[0], int) or use[0] >= 2:
                    pe.wait_ge(s_wfree, use[0] - 1)
                for c in range(2):
                    at, m = CHUNKS[2 * half + c]
                    last = product3(wide[:, w, 512 * c:512 * c + m], wkv_hi[:, 0, :], wkv_lo[:, 0, :],
                                    ctx_hi[:, n, at:at + m], ctx_lo[:, n, at:at + m])
                last.then_inc(s_wide, 1)

            def vals(i, par, half):
                n, w = slot(par, 1), ring_slot(par, half)
                pe.wait_ge(s_wfree, ring(i, half) - 1)
                for k in range(7 * half, 7 + 6 * half):
                    m, at = keys_of(k), P * (k - 7 * half)
                    ks = slice(k * P, k * P + m)
                    out = wide[0:m, w, at:at + P]
                    last = product3(out, ctx_hi[:, n, ks], ctx_lo[:, n, ks],
                                    wkv_hi[:, 1, :], wkv_lo[:, 1, :])
                last.then_inc(s_wide, 1)

            def maxima(i, par, u):
                pair, half = u // 2, u % 2
                n, w, g = slot(par, 1), ring_slot(par, 2 + u), u // 4
                pe.wait_ge(s_wfree, ring(i, 2 + u) - 1)
                for c in range(2):
                    at = min(CHUNKS[2 * half + c][0], LK - CH)
                    last = pe.matmul(wide[:, w, 512 * c:512 * c + CH],
                                     q_cur[:, n, pair * P:pair * P + P],
                                     k_stack[:, n, g, at:at + CH], start=True, stop=True)
                last.then_inc(s_wide, 1)

            def turn_max(i, par):
                w = ring_slot(par, 18)
                pe.wait_ge(s_wfree, ring(i, 18) - 1)
                pe.wait_ge(s_rowmax, i + 2)
                pe.matmul(wide[0:16, w, 0:P], row_max[:, :], nident[:], start=True, stop=True).then_inc(s_wide, 1)

            def scores(i, par, k):
                n, m = slot(par, 0), keys_of(k)
                for u in range(2):
                    pe.wait_ge(s_exp, i * (2 * NK) + (2 * k + u + 1))
                    for g in (2 * u, 2 * u + 1):
                        last = pe.matmul(score[0:m, u, 256 * (g % 2):256 * (g % 2) + 256],
                                         k_stack[:, n, g, k * P:k * P + m],
                                         q_cur[:, n, 256 * g:256 * g + 256], start=True, stop=True)
                    last.then_inc(s_last if k == NK - 1 and u else s_score, 1)

            def sum_values(i, par, k):
                n, m = slot(par, 0), keys_of(k)
                if k == 0:
                    pe.wait_ge(s_wfree, ring(i - 1, 1) + 1)
                    pe.wait_ge(s_sums, i + 1)
                pe.wait_ge(s_exp, i * (2 * NK) + (2 * k + 2 + 2))
                for g in range(VG):
                    c, w = 32 * (g % 4), min(VH, H - VH * g) * LQ
                    last = pe.matmul(sums[c:c + 32, g // 4, 0:w], values[0:m, n, k, 32 * g:32 * g + 32],
                                     probs[0:m, k_slot(par, k), 192 * g:192 * g + w],
                                     start=(k == 0), stop=(k == NK - 1))
                last.then_inc(s_pv, 1)

            pe.sem_inc(s_last, 1)
            pe.wait_ge(s_const, 16 * 6)
            for t in range(NT):
                pe.wait_ge(s_xn, t + 1)
                last = pe.transpose(wide[:, 0, t * P:t * P + P], xn[:, t, :], keep.ident[:])
                if t % 4 == 3:
                    last.then_inc(s_xt, 1)
            pe.wait_ge(s_xtc, 2)
            for g in range(G):
                if g >= 2:
                    pe.wait_ge(s_qh, 2 * g - 2)
                for h in range(2):
                    out = (score if g % 2 else sums)[:, h, :]
                    pe.matmul(out, wq[:, g, :], xnT[:, 512 * h:512 * h + 512],
                              start=True, stop=True).then_inc(s_q, 1)
                if g == 1:
                    pe.wait_ge(s_wsplit, 2)
                if g in (1, 2):
                    keys(0, 0, 0, g - 1, (g - 1, g - 1))
            pe.wait_ge(s_qh, 2 * G)

            def body(i, j, par):
                work, more, last = has(i, 0), has(i, 1), has(i, 2)
                n = slot(par, 1)
                for k in range(NK):
                    if work:
                        if k == 0:
                            pe.wait_ge(s_shin[par], (j + 1) * SHIN_N)
                        scores(i, par, k)
                    if more:
                        if k < 2:
                            vals(i, par, k)
                        if k == 3:
                            pe.wait_ge(s_stack[n], (j + (par + 1) // 2 + 1) * STACK_N)
                        if 3 <= k < 11:
                            maxima(i, par, 2 * k - 6)
                    if last and k == 12:
                        keys(i, par, 2, 1, (ring(i, 20), ring_slot(par, 20)))
                    if work and k:
                        sum_values(i, par, k - 1)
                    if more:
                        if 3 <= k < 11:
                            maxima(i, par, 2 * k - 5)
                        if k == 11:
                            turn_max(i, par)
                    if last and k == 11:
                        keys(i, par, 2, 0, (ring(i, 19), ring_slot(par, 19)))
                if work:
                    sum_values(i, par, NK - 1)

            run(pe, body)

        @block.scalar
        def _(act):
            act.wait_ge(s_const, 16 * 6)
            nc.scalar.mul(bq_scaled[:], keep.vecs[:, V_BQ:V_BQ + G], HD ** -0.5).then_inc(s_bq, 1)
            act.sem_inc(s_exp, 2)
            act.wait_ge(s_stat, 2 * NT + 2)
            nc.scalar.activation(rstd[:], rstd[:], ACT.Sqrt).then_inc(s_sqrt, 1)
            for h in range(2):
                act.wait_ge(s_xt, h + 1)
                nc.scalar.copy(xnT[:, 512 * h:512 * h + 512],
                               wide[:, 0, 512 * h:512 * h + 512]).then_inc(s_xtc, 1)
            act.wait_ge(s_bq, 1)

            def last_head(g):
                act.wait_ge(s_qp, g + 1)
                nc.scalar.mul(q_stack[:, :, g, GH - 1, :], q_part[:, g % 2, :].rearrange("p (b q) -> p b q", b=B),
                              keep.marks[:, GH - 1:GH]).then_inc(s_ql, 1)

            def key_high(i, par, ahead, half, use):
                act.wait_ge(s_wide, use[0] + 1)
                for c in range(2):
                    at, m = CHUNKS[2 * half + c]
                    nc.scalar.activation(k_hi[:, at:at + m], wide[:, use[1], 512 * c:512 * c + m],
                                         ACT.Identity, bias=keep.vecs[:, V_BK:V_BK + 1]).then_inc(s_khi, 1)

            for g in range(G):
                if g >= 2:
                    act.wait_ge(s_qp, g - 1)
                for h in range(2):
                    act.wait_ge(s_q, 2 * g + h + 1)
                    for to, done in ((q_full, s_qf), (q_hi, s_qh)):
                        nc.scalar.activation(to[:, g % 2, 512 * h:512 * h + 512],
                                             (score if g % 2 else sums)[:, h, :], ACT.Identity,
                                             bias=bq_scaled[:, g:g + 1], scale=HD ** -0.5).then_inc(done, 1)
                if g:
                    last_head(g - 1)
                if g in (1, 2):
                    key_high(0, 0, 0, g - 1, (g - 1, g - 1))
            last_head(G - 1)

            def body(i, j, par):
                for k in range(NK):
                    m = keys_of(k)
                    if has(i, 0):
                        for u in range(2):
                            if k == NK - 1 and u:
                                act.wait_ge(s_last, i + 2)
                            else:
                                act.wait_ge(s_score, i * (2 * NK - 1) + (2 * k + u + 1))
                            if u == 0:
                                act.wait_ge(s_pv, i * NK + (k + 1))
                            nc.scalar.activation(probs[0:m, k_slot(par, k), 512 * u:512 * u + 512],
                                                 score[0:m, u, :], ACT.Exp).then_inc(s_exp, 1)
                    if k == 11 and has(i, 2):
                        n = slot(par, 1)
                        act.wait_ge(s_stack[n], (j + (par + 1) // 2 + 1) * STACK_N)
                    if k >= 11 and has(i, 2):
                        key_high(i, par, 2, k - 11, (ring(i, 8 + k), ring_slot(par, 8 + k)))

            run(act, body)

        @block.vector
        def _(dve):
            dve.sem_inc(s_pv, 2)
            dve.sem_inc(s_sums, 1)
            dve.wait_ge(s_x, 16)
            for t in range(NT):
                dve.bn_stats(stats[:, t, :], keep.x[:, t, :]).then_inc(s_stat, 1)
            for t in range(NT):
                dve.wait_ge(s_stat, t + 1)
                dve.bn_aggr(mean_var[:, t, :], stats[:, t, :]).then_inc(s_stat, 1)
            dve.wait_ge(s_stat, 2 * NT)
            dve.tensor_scalar(rstd[:], mean_var[:, :, 1], EPS, None, ALU.add).then_inc(s_stat, 1)
            dve.wait_ge(s_stat, 2 * NT + 1)
            dve.reciprocal(rstd[:], rstd[:]).then_inc(s_stat, 1)
            dve.wait_ge(s_sqrt, 1)
            for t in range(NT):
                dve.tensor_scalar(xn[:, t, :], keep.x[:, t, :], mean_var[:, t, 0:1], rstd[:, t:t + 1],
                                  ALU.subtract, ALU.mult).then_inc(s_xn, 1)
            dve.wait_ge(s_const, 16 * 6)
            dve.tensor_copy(wkv_hi[:], wkv[:]).then_inc(s_wsplit, 1)
            dve.wait_ge(s_wsplit, 1)
            dve.tensor_tensor(wkv_lo[:], wkv[:], wkv_hi[:], ALU.subtract).then_inc(s_wsplit, 1)
            dve.memset(values[:], 1.0).then_inc(s_ones, 1)

            def key_low(i, par, ahead, half, use):
                for c in range(2):
                    at, m = CHUNKS[2 * half + c]
                    dve.wait_ge(s_khi, (i + ahead) * 4 + (2 * half + c + 1))
                    last = dve.scalar_tensor_tensor(
                        out=k_lo[:, at:at + m], in0=wide[:, use[1], 512 * c:512 * c + m],
                        scalar=keep.vecs[:, V_BK:V_BK + 1], in1=k_hi[:, at:at + m],
                        op0=ALU.add, op1=ALU.subtract)
                last.then_inc(s_wfree, 1)

            for g in range(G):
                s = g % 2
                dve.wait_ge(s_qh, 2 * g + 2)
                if g >= 2:
                    dve.wait_ge(s_ql, g - 1)
                dve.scalar_tensor_tensor(out=q_part[:, s, :], in0=q_hi[:, s, :],
                                         scalar=keep.marks[:, 4:5], in1=q_full[:, s, :],
                                         op0=ALU.mult, op1=ALU.add).then_inc(s_qp, 1)
                dve.wait_ge(s_qp, g + 1)
                for h in range(GH - 1):
                    last = dve.tensor_scalar(q_stack[:, :, g, h, :],
                                             q_part[:, s, :].rearrange("p (b q) -> p b q", b=B),
                                             keep.marks[:, h:h + 1], None, ALU.mult)
                last.then_inc(s_qs, 1)
                if g in (1, 2):
                    key_low(0, 0, 0, g - 1, (g - 1, g - 1))

            def vals(i, par, half):
                n, w = slot(par, 1), ring_slot(par, half)
                dve.wait_ge(s_wide, ring(i, half) + 1)
                parts = [(0, 7, P)] if half == 0 else [(7, 5, P), (12, 1, keys_of(12))]
                for k0, nk, m in parts:
                    at = P * (k0 - 7 * half)
                    src = wide[0:m, w, at:at + P * nk].rearrange("p (k c) -> p k c", k=nk)
                    dst = values[0:m, n, k0:k0 + nk, :]
                    nv = (VG - 1) * VH * HD
                    dve.tensor_copy(
                        dst[:, :, 0:32 * (VG - 1)].rearrange("p k (g c) -> p k g c", c=32)[:, :, :, 1:25],
                        src[:, :, 0:nv].rearrange("p k (g c) -> p k g c", g=VG - 1))
                    last = dve.tensor_copy(dst[:, :, 32 * (VG - 1) + 1:32 * (VG - 1) + 1 + HD],
                                           src[:, :, nv:P])
                last.then_inc(s_wfree, 1)

            def body(i, j, par):
                if has(i, 1):
                    if isinstance(i, int) and i < 0:
                        dve.wait_ge(s_ones, 1)
                    vals(i, par, 0)
                    vals(i, par, 1)
                    for u in range(16):
                        dve.wait_ge(s_wide, ring(i, 2 + u) + 1)
                        w = ring_slot(par, 2 + u)
                        dve.tensor_reduce(
                            half_max[:, u // 2, u % 2:u % 2 + 1],
                            wide[:, w, :].rearrange("p (c k) -> p c k", c=2)[:, :, 0:CH],
                            AX.XY, ALU.max).then_inc(s_wfree, 1)
                    dve.wait_ge(s_wfree, ring(i, 17) + 1)
                    dve.tensor_reduce(row_max[:].rearrange("p (a m) -> p a m", a=2),
                                      half_max[:].unsqueeze(1).to_broadcast([P, 2, 8, 2]),
                                      AX.X, ALU.max).then_inc(s_rowmax, 1)
                    dve.wait_ge(s_wide, ring(i, 18) + 1)
                    w = ring_slot(par, 18)
                    if has(i, 0):
                        dve.wait_ge(s_shin[par], (j + 1) * SHIN_N)
                    dve.tensor_copy(shift_hi[:, :], wide[0:16, w, 0:P]).then_inc(s_shift, 1)
                    dve.wait_ge(s_shift, i + 2)
                    dve.scalar_tensor_tensor(out=shift[:, :], in0=shift_hi[:, :],
                                             scalar=keep.marks[0:16, 5:6], in1=wide[0:16, w, 0:P],
                                             op0=ALU.mult, op1=ALU.add).then_inc(s_wfree, 1)
                if has(i, 2):
                    for half in range(2):
                        key_low(i, par, 2, half, (ring(i, 19 + half), ring_slot(par, 19 + half)))
                if has(i, 0):
                    dve.wait_ge(s_pv, i * NK + (NK + 2))
                    out = keep.sums[:, :, bass.ds(i * LQ, LQ)]
                    dve.tensor_copy(out[:, 0:3, :], sums[:, 0, 0:192].rearrange("p (j q) -> p j q", j=VH))
                    dve.tensor_copy(out[0:32, 3:6, :],
                                    sums[0:32, 1, 0:192].rearrange("p (j q) -> p j q", j=VH))
                    dve.tensor_copy(out[32:64, 3, :], sums[32:64, 1, 0:LQ]).then_inc(s_sums, 1)

            run(dve, body)


def mamba_mlp(nc, A, keep):
    with ExitStack() as ctx:
        def sb(name, shape, dt=F32):
            return ctx.enter_context(nc.sbuf_tensor(name, shape, dt))

        def pb(name, shape, dt=F32):
            return ctx.enter_context(nc.psum_tensor(name, shape, dt))

        def sem(name):
            return ctx.enter_context(nc.semaphore(name))

        rows, vecs, ident = keep.rows, keep.vecs, keep.ident
        o_tok = sb("o_tok", [P, 4, P])
        o_rden = sb("o_rden", [P, 2, 2, H])
        oT = sb("oT", [P, 4, P])
        x_bias = sb("x_bias", [P, NT, P])
        x1 = sb("x1", [P, NT, P])
        u = sb("u", [P, NT, P])
        v = sb("v", [P, NT, P])
        vT = sb("vT", [P, T])
        stats = sb("stats2", [P, NT, 6])
        mean_var = sb("mean_var2", [P, NT, 2])
        rstd = sb("rstd2", [P, NT])
        rstd12 = sb("rstd12", [P, 2, NT])
        var12 = sb("var12", [P, NT])
        conv = sb("conv", [P, 4, T])
        xbc = sb("xbc", [P, 4, T])
        zg = sb("zg", [P, 2, T])
        dt_x = sb("dt_x", [P, NT, MH])
        dt_a = sb("dt_a", [P, NT, MH])
        dt_e = sb("dt_e", [P, NT, MH])
        dt_u = sb("dt_u", [P, NT, MH])
        dt_l = sb("dt_l", [P, NT, MH])
        dt_m = sb("dt_m", [P, NT, MH])
        dt = sb("dt", [P, NT, MH])
        decay = sb("decay", [P, NT, MH])
        a_exp = sb("a_exp", [P, MH])
        delta = sb("delta", [P, 8, P])
        decay_all = sb("decay_all", [P, 2, 8 * P])
        gain = sb("gain", [P, 2, 8 * P])
        mix = sb("mix", [P, NT, MH, P])
        y = sb("y", [P, 2, T])
        wout_n = sb("wout_n", [P, 2, P])
        rms = sb("rms", [P, NT])
        y1 = sb("y1", [P, NT, P])
        ones = sb("ones", [P, 1])
        one = sb("one2", [P, 1])
        w_stage = sb("w_stage", [P, 2, 2, NH * HT])
        dtx = keep.sums[:, 0:2, :].rearrange("p c (t k) -> p (c t) k", k=2 * P)
        y_sq = keep.sums[:, 2:4, :]
        hid = conv

        ps = pb("ps", [P, 3, 1024])
        pt = pb("pt", [P, 2, 512])

        s_stage = [sem(f"t_stage{i}") for i in range(2)]
        names = ("w one wsp init xb turn o ot otc att x1 st var sq u ln vt vtc dtp dts dte mm conv silu zin zsil "
                 "ones tsp cen csq bc bcc bc0 scan cb mix xt dtx ya yc ysq out r rq y1 fc gelu pr x2")
        s = {n: sem("t_" + n) for n in names.split()}
        block = ctx.enter_context(nc.Block())

        def tok(t):
            return slice(t * P, t * P + P)

        def half(h):
            return slice(512 * h, 512 * h + 512)

        def bank(n):
            return ps[:, n // 2, half(n % 2)] if n < 6 else pt[:, n - 6, :]

        MM_BANK = ((2, 3, 4), (5, 0, 1))
        Z_BANK = ((2, 3), (4, 7))
        FC_BANK = ((2, 3, 4, 6), (7, 0, 1, 5))
        TURN_BANK = (4, 6)
        BC_SLOT, CB_SLOT, YA_SLOT = (1, 2, 0, 1), 2, (0, 1)

        @block.sync
        def _(sp):
            for e in range(E):
                if e >= 2:
                    sp.wait_ge(s["wsp"], 2 * e - 2)
                sp.dma_start(w_stage[:, e % 2], A["wgu"][:, e]).then_inc(s_stage[e % 2], 16)
            sp.dma_start(keep.w2[:], A["w2"]).then_inc(s["w"], 16)
            sp.dma_start(keep.bgu[:], A["bgu"]).then_inc(s["w"], 16)
            sp.dma_start(keep.b2[:], A["b2"]).then_inc(s["w"], 16)
            sp.dma_start(keep.cent[:], A["cent"]).then_inc(s["w"], 16)
            sp.wait_ge(s["w"], 64)

        @block.gpsimd
        def _(pool):
            pool.tensor_tensor(x_bias[:], keep.x[:], rows[:, R_BO:R_BO + P].unsqueeze(1).to_broadcast(
                [P, NT, P]), ALU.add).then_inc(s["xb"], 1)
            pool.tensor_copy(delta[:], ident[:].unsqueeze(1).to_broadcast([P, 8, P])).then_inc(s["init"], 1)
            for c in range(2):
                pool.tensor_scalar(wout_n[:, c, :], keep.wout[:, c, :], vecs[:, V_NW + c:V_NW + c + 1], None,
                                   ALU.mult).then_inc(s["init"], 1)
            pool.memset(one[:], 1.0).then_inc(s["one"], 1)
            pool.wait_ge(s["one"], 1)
            for e in range(E):
                pool.wait_ge(s_stage[e % 2], 16 * (e // 2 + 1))
                src = w_stage[:, e % 2].rearrange("p g c -> p (g c)")
                hi = keep.w_hi[:, e].rearrange("p g c -> p (g c)")
                lo = keep.w_lo[:, e].rearrange("p g c -> p (g c)")
                pool.tensor_tensor(hi, src, one[:].to_broadcast([P, 2 * NH * HT]), ALU.mult).then_inc(s["wsp"], 1)
                pool.wait_ge(s["wsp"], 2 * e + 1)
                pool.tensor_tensor(lo, src, hi, ALU.subtract).then_inc(s["wsp"], 1)
            for t in range(NT):
                pool.wait_ge(s["sq"], t // 4 + 1)
                pool.tensor_scalar(u[:, t, :], x1[:, t, :], mean_var[:, t, 0:1], rstd12[:, 0, t:t + 1],
                                   ALU.subtract, ALU.mult).then_inc(s["u"], 1)
            pool.memset(keep.ones[:], 1.0).then_inc(s["cen"], 1)
            pool.wait_ge(s["w"], 64)
            pool.tensor_tensor(keep.cent_sq[:], keep.cent[:], keep.cent[:], ALU.mult).then_inc(s["cen"], 1)
            for c in range(4):
                pool.wait_ge(s["bcc"], c + 1)
                pool.memset(decay_all[:, c % 2, :].rearrange("p (c q) -> p c q", q=LQ)[:, :, 0:1],
                            0.0).then_inc(s["bc0"], 1)

        @block.tensor
        def _(pe):
            def turn(p):
                if p >= 2:
                    pe.wait_ge(s["o"], p - 1)
                for k in range(2):
                    t = 2 * p + k
                    for j in range(VH):
                        pe.transpose(bank(3 * (p % 2) + k)[:, P * j:P * j + P], keep.sums[:, j, tok(t)], ident[:])
                    for j in range(VH):
                        r, at = 64 if j == 0 else 32, 64 * (VH * k + j)
                        last = pe.transpose(bank(3 * (p % 2) + 2)[:, at:at + r],
                                            keep.sums[0:r, VH + j, tok(t)], ident[0:r, 0:r])
                last.then_inc(s["turn"], 1)

            turn(0)
            turn(1)
            for p in range(NT // 2):
                pe.wait_ge(s["o"], p + 1)
                if p:
                    pe.wait_ge(s["otc"], p)
                for k in range(2):
                    last = pe.transpose(bank(6)[:, tok(k)], o_tok[:, 2 * (p % 2) + k, :], ident[:])
                last.then_inc(s["ot"], 1)
                if p + 2 < NT // 2:
                    turn(p + 2)
                pe.wait_ge(s["otc"], p + 1)
                if p:
                    pe.wait_ge(s["x1"], p)
                for k in range(2):
                    last = pe.matmul(bank(7)[:, tok(k)], oT[:, 2 * (p % 2) + k, :], keep.wo[:],
                                     start=True, stop=True)
                last.then_inc(s["att"], 1)

            def turn_v(n, h, b):
                for t in range(4 * h, 4 * h + 4):
                    pe.wait_ge(s["ln"], n * NT + t + 1)
                    last = pe.transpose(bank(b)[:, tok(t % 4)], v[:, t, :], ident[:])
                last.then_inc(s["vt"], 1)

            for h in range(2):
                turn_v(0, h, h)
                pe.wait_ge(s["vtc"], h + 1)
                for t in range(4 * h, 4 * h + 4):
                    last = pe.matmul(bank(6)[:, MH * t:MH * t + MH], vT[:, tok(t)], keep.win[:, 640:644],
                                     start=True, stop=True)
                last.then_inc(s["dtp"], 1)
                for c in range(3):
                    pe.matmul(bank(MM_BANK[h][c]), keep.win[:, 256 + P * c:256 + P * c + P], vT[:, half(h)],
                              start=True, stop=True).then_inc(s["mm"], 1)
            for h in range(2):
                for c in range(2):
                    pe.wait_ge(s["conv"], min(2 * h + c + 1, 3))
                    pe.matmul(bank(Z_BANK[h][c]), keep.win[:, P * c:P * c + P], vT[:, half(h)],
                              start=True, stop=True).then_inc(s["zin"], 1)

            def spread(c):
                if c < 2:
                    pe.wait_ge(s["zsil"], c + 2)
                if c == 3:
                    pe.wait_ge(s["bcc"], 2)
                else:
                    pe.wait_ge(s["conv"], (3, 4, 6)[c])
                for t in range(2):
                    for h in range(MH):
                        last = pe.matmul(ps[:, BC_SLOT[c], P * (MH * t + h):P * (MH * t + h) + P],
                                         decay[:, 2 * c + t, h:h + 1].to_broadcast([P, P]), ident[:],
                                         start=True, stop=True)
                last.then_inc(s["bc"], 1)

            def turn_x(t):
                if t >= 2:
                    pe.wait_ge(s["dtx"], t - 1)
                for c in range(2):
                    last = pe.transpose(pt[:, t % 2, P * c:P * c + P], xbc[:, c, tok(t)], ident[:])
                last.then_inc(s["xt"], 1)

            pe.wait_ge(s["dts"], DT_LAST)
            spread(0)
            spread(1)
            pe.wait_ge(s["silu"], 8)
            pe.wait_ge(s["bcc"], 2)
            for t in range(NT):
                last = pe.matmul(ps[:, CB_SLOT, tok(t)], xbc[0:64, 2, tok(t)], xbc[0:64, 3, tok(t)],
                                 start=True, stop=True)
            last.then_inc(s["cb"], 1)
            pe.wait_ge(s["zsil"], 4)
            turn_x(0)
            turn_x(1)
            spread(2)
            spread(3)
            for t in range(2, NT):
                turn_x(t)
            for h2 in range(2):
                pe.wait_ge(s["bcc"], 3 + h2)
                pe.wait_ge(s["dtx"], 4 * h2 + 4)
                for t in range(4):
                    pe.wait_ge(s["mix"], 4 * h2 + t + 1)
                    for h in range(MH):
                        r = 64 * (h % 2)
                        last = pe.matmul(ps[r:r + 64, YA_SLOT[h2], 512 * (h // 2) + P * t:512 * (h // 2) + P * t + P],
                                         dtx[:, 4 * h2 + t, 64 * h:64 * h + 64], mix[:, 4 * h2 + t, h, :],
                                         start=True, stop=True)
                last.then_inc(s["ya"], 1)
            pe.wait_ge(s["mix"], NT)
            pe.wait_ge(s["init"], 3)
            pe.wait_ge(s["ones"], 1)
            for h in range(2):
                pe.wait_ge(s["yc"], 2 * h + 2)
                pe.wait_ge(s["ysq"], 2 * h + 2)
                for t in range(4 * h, 4 * h + 4):
                    for c in range(2):
                        pe.matmul(bank(6 + h)[:, t:t + 1], y_sq[:, c, tok(t)], ones[:],
                                  start=(c == 0), stop=(c == 1))
                    for c in range(2):
                        last = pe.matmul(ps[:, CB_SLOT, tok(t)], y[:, c, tok(t)], wout_n[:, c, :],
                                         start=(c == 0), stop=(c == 1))
                last.then_inc(s["out"], 1)

            for h in range(2):
                turn_v(1, h, h)
                pe.wait_ge(s["vtc"], 3 + h)
                for c in range(4):
                    pe.matmul(bank(FC_BANK[h][c]), keep.wfc[:, P * c:P * c + P], vT[:, half(h)],
                              start=True, stop=True).then_inc(s["fc"], 1)
            for h in range(2):
                pe.wait_ge(s["gelu"], 4 * h + 4)
                for t in range(4):
                    for c in range(4):
                        last = pe.matmul(bank(2 + h)[:, tok(t)], hid[:, c, tok(4 * h + t)], keep.wproj[:, c, :],
                                         start=(c == 0), stop=(c == 3))
                last.then_inc(s["pr"], 1)
            for h in range(2):
                turn_v(2, h, TURN_BANK[h])

        @block.scalar
        def _(act):
            def root(n, buf):
                act.wait_ge(s["var"], n)
                nc.scalar.activation(buf, buf, ACT.Sqrt).then_inc(s["sq"], 1)

            for p in range(NT // 2):
                act.wait_ge(s["ot"], p + 1)
                if p >= 2:
                    act.wait_ge(s["att"], p - 1)
                nc.scalar.copy(oT[:, 2 * (p % 2):2 * (p % 2) + 2, :].rearrange("p t c -> p (t c)"),
                               bank(6)[:, 0:2 * P]).then_inc(s["otc"], 1)

            def turned(n, h, w, b):
                act.wait_ge(s["vt"], 2 * n + h + 1)
                nc.scalar.activation(vT[:, half(h)], bank(h), ACT.Identity, bias=vecs[:, b:b + 1],
                                     scale=vecs[:, w:w + 1]).then_inc(s["vtc"], 1)

            for h in range(2):
                root(h + 1, rstd12[:, :, 4 * h:4 * h + 4])
                turned(0, h, V_LN1W, V_LN1B)

            def conv_silu(h):
                for c in range(4):
                    act.wait_ge(s["conv"], 3 * h + min(c, 2) + 1)
                    m, src = (P, conv[:, c, half(h)]) if c < 2 else (64, conv[64 * (c - 2):64 * (c - 1), 2, half(h)])
                    nc.scalar.activation(xbc[0:m, c, half(h)], src, ACT.Silu).then_inc(s["silu"], 1)

            def gate_silu(h):
                for c in range(2):
                    act.wait_ge(s["zin"], 2 * h + c + 1)
                    nc.scalar.activation(zg[:, c, half(h)], bank(Z_BANK[h][c]), ACT.Silu).then_inc(s["zsil"], 1)

            act.wait_ge(s["dts"], 4)
            nc.scalar.activation(dt_e[:], dt_a[:], ACT.Exp).then_inc(s["dte"], 1)
            nc.scalar.activation(a_exp[:], rows[:, R_ALOG:R_ALOG + MH], ACT.Exp).then_inc(s["dte"], 1)
            act.wait_ge(s["dts"], 5)
            nc.scalar.activation(dt_l[:], dt_u[:], ACT.Ln).then_inc(s["dte"], 1)
            act.wait_ge(s["dts"], DT_LAST - 1)
            nc.scalar.activation(decay[:], decay[:], ACT.Exp, scale=-1.0).then_inc(s["dts"], 1)
            gate_silu(0)
            conv_silu(0)
            gate_silu(1)
            for c in range(4):
                if c == 2:
                    conv_silu(1)
                act.wait_ge(s["bc"], c + 1)
                if c >= 2:
                    act.wait_ge(s["scan"], c - 1)
                nc.scalar.copy(decay_all[:, c % 2, :], ps[:, BC_SLOT[c], :]).then_inc(s["bcc"], 1)
            for h in range(2):
                for c in range(2):
                    act.wait_ge(s["yc"], 2 * h + c + 1)
                    nc.scalar.square(y_sq[:, c, half(h)], y[:, c, half(h)]).then_inc(s["ysq"], 1)
            for h in range(2):
                act.wait_ge(s["r"], 2 * h + 2)
                nc.scalar.activation(rms[:, 4 * h:4 * h + 4], rms[:, 4 * h:4 * h + 4], ACT.Sqrt).then_inc(s["rq"], 1)
                root(3 + h, rstd[:, 4 * h:4 * h + 4])
            for h in range(2):
                turned(1, h, V_LN2W, V_LN2B)
            for h in range(2):
                for c in range(4):
                    act.wait_ge(s["fc"], 4 * h + c + 1)
                    nc.scalar.activation(hid[:, c, half(h)], bank(FC_BANK[h][c]), ACT.Gelu,
                                         bias=vecs[:, V_FCB + c:V_FCB + c + 1]).then_inc(s["gelu"], 1)
            for h in range(2):
                root(5 + h, rstd[:, 4 * h:4 * h + 4])
                if h == 0:
                    act.wait_ge(s["vt"], 5)
                    nc.scalar.copy(keep.tT[:, half(0)], bank(TURN_BANK[0])).then_inc(s["vtc"], 1)
                    act.wait_ge(s["vtc"], 5)
                    nc.scalar.square(keep.t_sq[:, half(0)], keep.tT[:, half(0)])
            act.wait_ge(s["vt"], 6)
            nc.scalar.copy(keep.tT[:, half(1)], bank(TURN_BANK[1])).then_inc(s["vtc"], 1)

        @block.vector
        def _(dve):
            st = [0]

            def count(ins):
                st[0] += 1
                ins.then_inc(s["st"], 1)

            def settle():
                dve.wait_ge(s["st"], st[0])

            def one_by_one(*steps):
                for ins in steps:
                    count(ins())
                    settle()

            def moments(src, h):
                for t in range(4 * h, 4 * h + 4):
                    count(dve.bn_stats(stats[:, t, :], src[:, t, :]))
                settle()
                for t in range(4 * h, 4 * h + 4):
                    count(dve.bn_aggr(mean_var[:, t, :], stats[:, t, :]))
                settle()

            def norm_request(src, h):
                moments(src, h)
                r = rstd[:, 4 * h:4 * h + 4]
                one_by_one(lambda: dve.tensor_scalar(r, mean_var[:, 4 * h:4 * h + 4, 1], EPS, None, ALU.add))
                dve.reciprocal(r, r).then_inc(s["var"], 1)

            def norm_apply(src, h, n, scales):
                dve.wait_ge(s["sq"], n)
                for t in range(4 * h, 4 * h + 4):
                    dve.tensor_scalar(v[:, t, :], src[:, t, :], mean_var[:, t, 0:1], scales[:, t:t + 1],
                                      ALU.subtract, ALU.mult).then_inc(s["ln"], 1)

            dve.memset(ones[:], 1.0).then_inc(s["ones"], 1)

            def divide(p):
                w = p % 2
                dve.wait_ge(s["turn"], p + 1)
                if p >= 2:
                    dve.wait_ge(s["ot"], p - 1)
                both = slice(2 * w, 2 * w + 2)
                r = o_rden[:, w, :, :]
                pb_ = bank(3 * w + 2)[:, 0:2 * VH * 64].rearrange("p (t j c) -> p t j c", t=2, j=VH)
                pas = [bank(3 * w + k)[:, 0:VH * P].rearrange("p (j g c) -> p j g c", j=VH, g=4) for k in range(2)]
                for k in range(2):
                    count(dve.reciprocal(r[:, k, 0:12].rearrange("p (j g) -> p j g", j=VH), pas[k][:, :, :, 0]))
                count(dve.reciprocal(r[:, :, 12:15], pb_[:, :, :, 0]))
                count(dve.reciprocal(r[:, :, 15:16], pb_[:, :, 0, 32:33]))
                settle()
                for k in range(2):
                    o4 = o_tok[:, 2 * w + k, 0:96].rearrange("p (g j c) -> p g j c", g=4, j=VH)
                    for j in range(VH):
                        count(dve.tensor_tensor(o4[:, :, j, :], pas[k][:, j, :, 1 + HD * j:1 + HD * j + HD],
                                                r[:, k, 4 * j:4 * j + 4].unsqueeze(2).to_broadcast([P, 4, HD]),
                                                ALU.mult))
                for h in range(12, 16):
                    j, at = (h - 12, 1 + HD * (h - 12)) if h < 15 else (0, 33)
                    count(dve.tensor_tensor(o_tok[:, both, HD * h:HD * h + HD], pb_[:, :, j, at:at + HD],
                                            r[:, :, h:h + 1].to_broadcast([P, 2, HD]), ALU.mult))
                settle()
                dve.tensor_tensor(o_tok[:, both, :], o_tok[:, both, :],
                                  rows[:, R_BV:R_BV + P].unsqueeze(1).to_broadcast([P, 2, P]),
                                  ALU.add).then_inc(s["o"], 1)

            def residual(p):
                if p == 0:
                    dve.wait_ge(s["xb"], 1)
                dve.wait_ge(s["att"], p + 1)
                dve.tensor_tensor(x1[:, 2 * p:2 * p + 2, :], x_bias[:, 2 * p:2 * p + 2, :],
                                  bank(7)[:, 0:2 * P].rearrange("p (t c) -> p t c", t=2),
                                  ALU.add).then_inc(s["x1"], 1)

            def norm_twice_request(h):
                dve.wait_ge(s["x1"], 2 * h + 2)
                moments(x1, h)
                tiles = slice(4 * h, 4 * h + 4)
                var, a, both, w = mean_var[:, tiles, 1], rstd12[:, 0, tiles], rstd12[:, 1, tiles], var12[:, tiles]
                one_by_one(lambda: dve.tensor_scalar(a, var, EPS, None, ALU.add),
                           lambda: dve.reciprocal(a, a),
                           lambda: dve.tensor_tensor(w, var, a, ALU.mult),
                           lambda: dve.tensor_scalar(w, w, EPS, None, ALU.add),
                           lambda: dve.reciprocal(w, w))
                dve.tensor_tensor(both, w, a, ALU.mult).then_inc(s["var"], 1)

            divide(0)
            divide(1)
            residual(0)
            divide(2)
            residual(1)
            divide(3)
            norm_twice_request(0)
            residual(2)
            norm_apply(x1, 0, 1, rstd12[:, 1, :])
            residual(3)
            norm_twice_request(1)
            norm_apply(x1, 1, 2, rstd12[:, 1, :])

            def convolve(h, c):
                dve.wait_ge(s["mm"], 3 * h + c + 1)
                src = bank(MM_BANK[h][c]).rearrange("p (b q) -> p b q", q=LQ)
                dst = conv[:, c, half(h)].rearrange("p (b q) -> p b q", q=LQ)
                cw = vecs[:, V_CW + 4 * c:V_CW + 4 * c + 4]
                count(dve.tensor_scalar(dst, src, cw[:, 3:4], vecs[:, V_CB + c:V_CB + c + 1], ALU.mult, ALU.add))
                for k in range(1, 4):
                    settle()
                    ins = dve.scalar_tensor_tensor(out=dst[:, :, k:], in0=src[:, :, 0:LQ - k],
                                                   scalar=cw[:, 3 - k:4 - k], in1=dst[:, :, k:],
                                                   op0=ALU.mult, op1=ALU.add)
                    if k < 3:
                        count(ins)
                    else:
                        ins.then_inc(s["conv"], 1)

            n = [0]

            def step(ins):
                n[0] += 1
                ins.then_inc(s["dts"], 1)
                dve.wait_ge(s["dts"], n[0])

            def per_head(ap):
                return ap.unsqueeze(1).to_broadcast([P, NT, MH])

            dve.wait_ge(s["dtp"], 2)
            step(dve.tensor_tensor(dt_x[:], bank(6)[:, 0:MH * NT].rearrange("p (t h) -> p t h", h=MH),
                                   per_head(rows[:, R_DTB:R_DTB + MH]), ALU.add))
            step(dve.tensor_scalar(dt_a[:], dt_x[:], -1.0, None, ALU.mult))
            step(dve.tensor_tensor(dt_a[:], dt_a[:], dt_x[:], ALU.min))
            step(dve.tensor_scalar(dt[:], dt_x[:], 0.0, None, ALU.max))
            convolve(0, 0)
            dve.wait_ge(s["dte"], 2)
            step(dve.tensor_scalar(dt_u[:], dt_e[:], 1.0, None, ALU.add))
            step(dve.tensor_scalar(dt_a[:], dt_u[:], -1.0, None, ALU.add))
            step(dve.tensor_scalar(dt_m[:], dt_a[:], 0.0, None, ALU.is_equal))
            step(dve.tensor_tensor(dt_a[:], dt_a[:], dt_m[:], ALU.add))
            step(dve.reciprocal(dt_a[:], dt_a[:]))
            step(dve.tensor_tensor(dt_a[:], dt_a[:], dt_e[:], ALU.mult))
            convolve(0, 1)
            dve.wait_ge(s["dte"], 3)
            step(dve.tensor_tensor(dt_m[:], dt_m[:], dt_l[:], ALU.add))
            step(dve.tensor_tensor(dt_m[:], dt_m[:], dt_a[:], ALU.mult))
            step(dve.tensor_tensor(dt[:], dt[:], dt_m[:], ALU.add))
            step(dve.tensor_tensor(decay[:], dt[:], per_head(a_exp[:, 0:MH]), ALU.mult))
            assert n[0] == DT_LAST - 1
            for h, c in ((0, 2), (1, 0), (1, 1), (1, 2)):
                convolve(h, c)

            for c in range(4):
                dve.wait_ge(s["bc0"], c + 1)
                if c == 0:
                    dve.wait_ge(s["init"], 3)
                dve.tensor_tensor_scan(gain[:, c % 2, :], decay_all[:, c % 2, :],
                                       delta[:].rearrange("p c q -> p (c q)"), 0.0,
                                       ALU.mult, ALU.add).then_inc(s["scan"], 1)
                if c == 0:
                    dve.wait_ge(s["cb"], 1)
                    dve.wait_ge(s["dts"], DT_LAST)
                dve.wait_ge(s["scan"], c + 1)
                for t in (2 * c, 2 * c + 1):
                    dve.tensor_tensor(mix[:, t, :, :], gain[:, c % 2, half(t % 2)].rearrange(
                        "p (h q) -> p h q", h=MH), ps[:, CB_SLOT, tok(t)].unsqueeze(1).to_broadcast([P, MH, P]),
                        ALU.mult).then_inc(s["mix"], 1)
                for t in (2 * c, 2 * c + 1):
                    dve.wait_ge(s["xt"], t + 1)
                    dve.tensor_tensor(dtx[:, t, :].rearrange("p (h c) -> p h c", h=MH),
                                      pt[:, t % 2, 0:2 * P].rearrange("p (h c) -> p h c", h=MH),
                                      dt[:, t, :].unsqueeze(2).to_broadcast([P, MH, 64]),
                                      ALU.mult).then_inc(s["dtx"], 1)
            dve.wait_ge(s["zsil"], 4)
            for h in range(2):
                dve.wait_ge(s["ya"], h + 1)
                for c in range(2):
                    count(dve.scalar_tensor_tensor(out=y[:, c, half(h)], in0=xbc[:, c, half(h)],
                                                   scalar=vecs[:, V_D + c:V_D + c + 1],
                                                   in1=ps[:, YA_SLOT[h], half(c)], op0=ALU.mult, op1=ALU.add))
                    settle()
                    dve.tensor_tensor(y[:, c, half(h)], y[:, c, half(h)], zg[:, c, half(h)],
                                      ALU.mult).then_inc(s["yc"], 1)
            dve.wait_ge(s["u"], NT)
            for h in range(2):
                tiles = slice(4 * h, 4 * h + 4)
                dve.wait_ge(s["out"], h + 1)
                dve.tensor_scalar(rms[:, tiles], bank(6 + h)[:, tiles], 1.0 / 256, EPS,
                                  ALU.mult, ALU.add).then_inc(s["r"], 1)
                dve.wait_ge(s["r"], 2 * h + 1)
                dve.reciprocal(rms[:, tiles], rms[:, tiles]).then_inc(s["r"], 1)
                if h:
                    norm_apply(y1, 0, 3, rstd)
                dve.wait_ge(s["rq"], h + 1)
                for t in range(4 * h, 4 * h + 4):
                    dve.scalar_tensor_tensor(out=y1[:, t, :], in0=ps[:, CB_SLOT, tok(t)], scalar=rms[:, t:t + 1],
                                             in1=u[:, t, :], op0=ALU.mult, op1=ALU.add).then_inc(s["y1"], 1)
                dve.wait_ge(s["y1"], 4 * h + 4)
                norm_request(y1, h)
            norm_apply(y1, 1, 4, rstd)
            one_by_one(lambda: dve.tensor_tensor(keep.x[:], x1[:], y1[:], ALU.add),
                       lambda: dve.tensor_tensor(keep.x[:], keep.x[:], rows[:, R_PB:R_PB + P].unsqueeze(
                           1).to_broadcast([P, NT, P]), ALU.add))
            for h in range(2):
                tiles = slice(4 * h, 4 * h + 4)
                dve.wait_ge(s["pr"], h + 1)
                one_by_one(lambda: dve.tensor_tensor(keep.x[:, tiles, :], keep.x[:, tiles, :], bank(2 + h).rearrange(
                    "p (t c) -> p t c", t=4), ALU.add))
                norm_request(keep.x, h)
                norm_apply(keep.x, h, 5 + h, rstd)
            dve.wait_ge(s["vtc"], 5)
            dve.tensor_copy(keep.t_hi[:, half(0)], keep.tT[:, half(0)]).then_inc(s["tsp"], 1)
            dve.wait_ge(s["tsp"], 1)
            dve.tensor_tensor(keep.t_lo[:, half(0)], keep.tT[:, half(0)], keep.t_hi[:, half(0)],
                              ALU.subtract).then_inc(s["tsp"], 1)


def experts(nc, A, keep, out):
    with ExitStack() as ctx:
        def sb(name, shape, dt=F32):
            return ctx.enter_context(nc.sbuf_tensor(name, shape, dt))

        def pb(name, shape, dt=F32):
            return ctx.enter_context(nc.psum_tensor(name, shape, dt))

        def sem(name):
            return ctx.enter_context(nc.semaphore(name))

        tT, ident = keep.tT, keep.ident
        bgu, b2, cent, cent_sq, ones = keep.bgu, keep.b2, keep.cent, keep.cent_sq, keep.ones
        acc = keep.x
        gate_bias = sb("gate_bias", [HT, 2, NH])
        t_hi, t_lo, t_sq = keep.t_hi, keep.t_lo, keep.t_sq
        w_hi, w_lo = keep.w_hi, keep.w_lo
        norms = sb("norms", [P, NT])
        cnorm = sb("cnorm", [P, E])
        dist2 = sb("dist2", [P, NT, E])
        top = sb("top", [P, NT, 8])
        top_i = sb("top_i", [P, NT, 8], mybir.dt.uint32)
        top_f = sb("top_f", [P, NT, 2])
        far = sb("far", [P, NT, 2])
        wts = sb("wts", [P, NT, 2])
        gap = sb("gap", [P, NT])
        pick = sb("pick", [P, NT, E])
        we = sb("we", [P, NT, E])
        weT = sb("weT", [E, NT, P])
        gate = sb("gate", [HT, 2, 512])
        hid = sb("hid_e", [HT, 2, NH, 512])

        gu = pb("gu", [P, 2, 2, 512])
        down = pb("down", [P, 2, 512])
        small = pb("small", [P, 2, 512])

        names = "w c gb sp tsq csq nrm rt top te sel weT wtc gu gate hid down acc b2 out"
        s = {n: sem("e_" + n) for n in names.split()}
        block = ctx.enter_context(nc.Block())

        def tok(t):
            return slice(t * P, t * P + P)

        def per_expert(eng, up, down, route):
            route(0)
            up(0, 0, 0, None)
            route(1)
            up(0, 1, 0, None)
            route(2)
            down(0, 0, 0)
            down(0, 0, 1)
            up(1, 0, 1, lambda part: down(0, 1, part))
            route(3)

            def body(e, par, more):
                up(e, 1, par, lambda part: down(e, 0, part))
                if more:
                    up(e + 1, 0, 1 - par, lambda part: down(e, 1, part))
                else:
                    down(e, 1, 0)
                    down(e, 1, 1)

            with eng.Fori(0, E // 2 - 1) as j:
                body(j * 2 + 1, 1, True)
                body(j * 2 + 2, 0, True)
            route(4)
            body(E - 1, 1, False)

        @block.sync
        def _(sp):
            rows_out = out.rearrange("(t p) d -> p t d", p=P)
            for h in range(2):
                sp.wait_ge(s["acc"], 2 * E + 1 + h)
                sp.dma_start(rows_out[:, 4 * h:4 * h + 4, :], acc[:, 4 * h:4 * h + 4, :]).then_inc(s["w"], 16)
            sp.wait_ge(s["w"], 2 * 16)

        @block.tensor
        def _(pe):
            def route(step):
                if step == 0:
                    pe.wait_ge(s["tsq"], 1)
                    for t in range(NT):
                        pe.matmul(small[:, 0, t:t + 1], t_sq[:, tok(t)], ones[:, 0:1], start=True, stop=True)
                    pe.matmul(small[:, 0, 8:8 + E], ones[:], cent_sq[:], start=True, stop=True)
                    for t in range(NT):
                        last = pe.matmul(small[:, 0, 64 + E * t:64 + E * t + E], tT[:, tok(t)], cent[:],
                                         start=True, stop=True)
                    last.then_inc(s["nrm"], 1)
                if step == 3:
                    pe.wait_ge(s["sel"], 1)
                    for t in range(NT):
                        last = pe.transpose(small[0:E, t // 4, tok(t % 4)], we[:, t, :], ident[:])
                    last.then_inc(s["weT"], 1)
                if step == 4:
                    pe.wait_ge(s["wtc"], 2)
                    for t in range(NT):
                        last = pe.matmul(small[:, t // 4, tok(t % 4)], weT[:, t, :], b2[:], start=True, stop=True)
                    last.then_inc(s["b2"], 1)

            def finish(e, h, part):
                if part == 0:
                    pe.wait_ge(s["hid"], e * 6 + (3 * h + 3 + 2))
                    pe.wait_ge(s["acc"], e * 2 + (h + 1))
                for t in (2 * part, 2 * part + 1):
                    for n in range(NH):
                        last = pe.matmul(down[:, h, P * t:P * t + P], hid[:, h, n, P * t:P * t + P],
                                         keep.w2[:, bass.ds(e, 1), n, :].rearrange("p e c -> p (e c)"),
                                         start=(n == 0), stop=(n == NH - 1))
                if part:
                    last.then_inc(s["down"], 1)

            def up(e, h, par, between):
                if isinstance(e, int) and e == 0 and h == 1:
                    pe.wait_ge(s["sp"], 2)
                half = slice(512 * h, 512 * h + 512)
                for n in range(NH):
                    w = (3 * h + n) % 2
                    pe.wait_ge(s["hid"], e * 6 + (3 * h + n + 1))
                    for k in range(2):
                        o = gu[0:HT, w, k, :]
                        hi = w_hi[:, bass.ds(e, 1), k, HT * n:HT * n + HT].rearrange("p e c -> p (e c)")
                        lo = w_lo[:, bass.ds(e, 1), k, HT * n:HT * n + HT].rearrange("p e c -> p (e c)")
                        pe.matmul(o, hi, t_hi[:, half], start=True, stop=False)
                        pe.matmul(o, hi, t_lo[:, half], start=False, stop=False)
                        last = pe.matmul(o, lo, t_hi[:, half], start=False, stop=True)
                    last.then_inc(s["gu"], 1)
                    if between and n:
                        between(n - 1)

            per_expert(pe, up, finish, route)

        @block.scalar
        def _(act):
            nc.scalar.square(t_sq[:, 512:1024], tT[:, 512:1024]).then_inc(s["tsq"], 1)

            def route(step):
                if step == 0:
                    act.wait_ge(s["top"], NT + 1)
                    nc.scalar.activation(far[:], far[:], ACT.Sqrt).then_inc(s["te"], 1)
                if step == 1:
                    act.wait_ge(s["rt"], 6)
                    nc.scalar.activation(gap[:], gap[:], ACT.Tanh, scale=0.5).then_inc(s["te"], 1)
                if step == 3:
                    act.wait_ge(s["weT"], 1)
                    for h in range(2):
                        nc.scalar.copy(weT[:, 4 * h:4 * h + 4, :].rearrange("p t c -> p (t c)"),
                                       small[0:E, h, :]).then_inc(s["wtc"], 1)

            def gates(e, h, par, between):
                if h == 0:
                    nc.scalar.copy(gate_bias[:, par, :], bgu[:, bass.ds(e, 1), 0, :].rearrange(
                        "p e c -> p (e c)")).then_inc(s["gb"], 1)
                    act.wait_ge(s["gb"], e + 1)
                for n in range(NH):
                    w = (3 * h + n) % 2
                    act.wait_ge(s["gu"], e * 6 + (3 * h + n + 1))
                    act.wait_ge(s["hid"], e * 6 + (3 * h + n + 1))
                    nc.scalar.activation(gate[:, w, :], gu[0:HT, w, 0, :], ACT.Silu,
                                         bias=gate_bias[:, par, n:n + 1]).then_inc(s["gate"], 1)

            per_expert(act, gates, lambda e, h, part: None, route)
        @block.vector
        def _(dve):
            dve.sem_inc(s["hid"], 2)
            dve.sem_inc(s["acc"], 2)
            second = slice(512, 1024)
            dve.tensor_copy(t_hi[:, second], tT[:, second]).then_inc(s["sp"], 1)
            dve.wait_ge(s["sp"], 1)
            dve.tensor_tensor(t_lo[:, second], tT[:, second], t_hi[:, second], ALU.subtract).then_inc(s["sp"], 1)
            n = [0]

            def step(ins):
                n[0] += 1
                ins.then_inc(s["rt"], 1)
                dve.wait_ge(s["rt"], n[0])

            def per_expert_of(ap):
                return ap.to_broadcast([P, NT, E])

            def route(part):
                if part == 0:
                    dve.wait_ge(s["nrm"], 1)
                    step(dve.tensor_copy(cnorm[:], small[:, 0, 8:8 + E]))
                    step(dve.tensor_copy(norms[:], small[:, 0, 0:NT]))
                    step(dve.scalar_tensor_tensor(out=dist2[:], in0=small[:, 0, 64:64 + E * NT].rearrange(
                        "p (t e) -> p t e", e=E), scalar=-2.0, in1=per_expert_of(cnorm[:].unsqueeze(1)),
                        op0=ALU.mult, op1=ALU.add))
                    step(dve.tensor_tensor(dist2[:], dist2[:], per_expert_of(norms[:].unsqueeze(2)), ALU.add))
                    step(dve.tensor_scalar(dist2[:], dist2[:], 1e-12, None, ALU.max))
                    for t in range(NT):
                        dve.max(top[:, t, :], dist2[:, t, :]).then_inc(s["top"], 1)
                    dve.wait_ge(s["top"], NT)
                    dve.tensor_copy(far[:], top[:, :, 0:2]).then_inc(s["top"], 1)
                    for t in range(NT):
                        last = dve.max_index(top_i[:, t, :], top[:, t, :], dist2[:, t, :])
                    last.then_inc(s["top"], 1)
                    dve.wait_ge(s["te"], 1)
                    step(dve.tensor_tensor(gap[:], far[:, :, 1], far[:, :, 0], ALU.subtract))
                if part == 4:
                    dve.wait_ge(s["b2"], 1)
                    dve.wait_ge(s["acc"], 2 * E)
                    dve.tensor_tensor(acc[:], acc[:], small[:].rearrange("p h (t c) -> p (h t) c", c=P),
                                      ALU.add).then_inc(s["sel"], 1)
                    dve.wait_ge(s["sel"], 2)
                if part != 2:
                    return
                dve.wait_ge(s["top"], NT + 2)
                step(dve.tensor_copy(top_f[:], top_i[:, :, 0:2]))
                dve.wait_ge(s["te"], 2)
                step(dve.tensor_scalar(wts[:, :, 0], gap[:], -0.5, 0.5, ALU.mult, ALU.add))
                step(dve.tensor_scalar(wts[:, :, 1], gap[:], 0.5, 0.5, ALU.mult, ALU.add))
                for k, to in ((0, pick), (1, we)):
                    step(dve.tensor_tensor(to[:], per_expert_of(keep.iota[:].unsqueeze(1)),
                                           per_expert_of(top_f[:, :, k:k + 1]), ALU.is_equal))
                    step(dve.tensor_tensor(to[:], to[:], per_expert_of(wts[:, :, k:k + 1]), ALU.mult))
                dve.tensor_tensor(we[:], we[:], pick[:], ALU.add).then_inc(s["sel"], 1)
                dve.wait_ge(s["sel"], 1)

            def weigh(e, h, part):
                if part == 0:
                    return
                dve.wait_ge(s["down"], e * 2 + (h + 1))
                for t in range(4):
                    k = 4 * h + t
                    last = dve.scalar_tensor_tensor(
                        out=acc[:, k, :], in0=down[:, h, P * t:P * t + P],
                        scalar=we[:, k, bass.ds(e, 1)], in1=acc[:, k, :], op0=ALU.mult, op1=ALU.add)
                last.then_inc(s["acc"], 1)

            def hidden(e, h, par, between):
                for n in range(NH):
                    w = (3 * h + n) % 2
                    dve.wait_ge(s["gate"], e * 6 + (3 * h + n + 1))
                    dve.scalar_tensor_tensor(
                        out=hid[:, h, n, :], in0=gu[0:HT, w, 1, :],
                        scalar=bgu[:, bass.ds(e, 1), 1, n:n + 1].rearrange("p e c -> p (e c)"),
                        in1=gate[:, w, :], op0=ALU.add, op1=ALU.mult).then_inc(s["hid"], 1)
                if between:
                    between(1)

            per_expert(dve, hidden, weigh, route)


class Keep:
    pass


def program(nc, A, out):
    with ExitStack() as ctx:
        def sb(name, shape, dt=F32):
            return ctx.enter_context(nc.sbuf_tensor("keep_" + name, shape, dt))

        keep = Keep()
        keep.x = sb("x", [P, NT, P])
        keep.ident = sb("ident", [P, P])
        keep.marks = sb("marks", [P, GH + 2])
        keep.vecs = sb("vecs", [P, NV])
        keep.rows = sb("rows", [P, NR])
        keep.iota = sb("iota", [P, E])
        keep.sums = sb("sums", [P, 2 * VH, T])
        keep.wo = sb("wo", [P, P])
        keep.win = sb("win", [P, 644])
        keep.wout = sb("wout", [P, 2, P])
        keep.wfc = sb("wfc", [P, 4 * P])
        keep.wproj = sb("wproj", [P, 4, P])
        attention(nc, A, keep)
        keep.tT = sb("tT", [P, T])
        keep.w_hi = sb("w_hi", [P, E, 2, NH * HT], BF16)
        keep.w_lo = sb("w_lo", [P, E, 2, NH * HT], BF16)
        keep.bgu = sb("bgu", [HT, E, 2, NH])
        keep.b2 = sb("b2", [E, P])
        keep.cent = sb("cent", [P, E])
        keep.cent_sq = sb("cent_sq", [P, E])
        keep.ones = sb("ones", [P, P])
        keep.t_sq = sb("t_sq", [P, T])
        keep.t_hi = sb("t_hi", [P, T], BF16)
        keep.t_lo = sb("t_lo", [P, T], BF16)
        keep.w2 = sb("w2", [HT, E, NH, P])
        mamba_mlp(nc, A, keep)
        experts(nc, A, keep, out)


def lay_out(a):
    import numpy as np
    f = np.float32
    g = {k.replace("L0_", ""): np.asarray(v) for k, v in a.items()}
    wq = np.zeros((P, G, 4, GH, HD), f)
    bq = np.zeros((4, GH, HD, G), f)
    wq[:, :, :3] = g["xattn_Wq"].T.reshape(P, G, 1, GH, HD)
    bq[:3] = g["xattn_bq"].reshape(G, GH, HD).transpose(1, 2, 0)
    marks = np.zeros((4, GH, HD, GH + 2), f)
    for h in range(GH):
        marks[:3, h, :, h] = 1
    marks[1, :, :, GH] = -1
    marks[0, 1, :, GH + 1] = -1

    wk = g["xattn_Wk"].T.reshape(P, G, GH, HD).transpose(0, 2, 3, 1)
    bk = g["xattn_bk"].reshape(G, GH, HD).transpose(1, 2, 0)

    def cols(v):
        return v.reshape(-1, P).T

    conv = g["attn_conv_w"].reshape(3, P, 4).transpose(1, 0, 2).reshape(P, 12)
    vecs = np.concatenate([
        cols(bk.reshape(-1)), bq.reshape(P, G), cols(g["attn_ln1_w"]), cols(g["attn_ln1_b"]),
        cols(g["attn_ln2_w"]), cols(g["attn_ln2_b"]), conv, cols(g["attn_conv_b"]),
        cols(np.repeat(g["attn_D_param"], 64)), cols(g["attn_norm_w"]), cols(g["attn_fc_b"])], 1)
    rows = np.concatenate([g["xattn_bv"], g["xattn_bo"], g["attn_proj_b"], g["attn_A_log"],
                           g["attn_dt_bias"]])[None]
    c = np.ascontiguousarray
    return {
        "x": c(g["x"].reshape(T, P)),
        "ctx": c(g["ctx_1024"].transpose(2, 0, 1)),
        "ident": np.eye(P, dtype=f),
        "nident": -np.eye(P, dtype=f),
        "marks": marks.reshape(P, GH + 2),
        "vecs": c(vecs),
        "iota": np.tile(np.arange(E, dtype=f), (P, 1)),
        "rows": c(rows),
        "wkv": c(np.stack([wk.reshape(P, P), g["xattn_Wv"].T], 1)),
        "wq": wq.reshape(P, G, P),
        "wo": c(g["xattn_Wo"].T),
        "win": c(g["attn_in_proj_w"].T),
        "wout": c(g["attn_out_proj_w"].T.reshape(2, P, P).transpose(1, 0, 2)),
        "wfc": c(g["attn_fc_w"].T),
        "wproj": c(g["attn_proj_w"].T.reshape(4, P, P).transpose(1, 0, 2)),
        "cent": c(g["ffn_centroid"].T),
        "wgu": c(np.stack([g["ffn_Wg"], g["ffn_W1"]], 0).transpose(2, 1, 0, 3)),
        "bgu": c(np.stack([g["ffn_bg"], g["ffn_b1"]], 0).reshape(2, E, NH, HT).transpose(3, 1, 0, 2)),
        "w2": c(g["ffn_W2"].reshape(E, NH, HT, P).transpose(2, 0, 1, 3)),
        "b2": c(g["ffn_b2"]),
    }


def kernel(**inputs):
    import numpy as np
    import concourse.bacc as bacc
    from concourse.bass_utils import run_bass_kernel_spmd

    nc = bacc.Bacc("TRN2", target_bir_lowering=False, num_devices=1)
    arrays = lay_out(inputs)
    aps = {k: nc.dram_tensor(f"in_{k}", v.shape, F32, kind="ExternalInput").ap()
           for k, v in arrays.items()}
    out = nc.dram_tensor("out_0", (T, P), F32, kind="ExternalOutput").ap()
    program(nc, aps, out)
    r = run_bass_kernel_spmd(nc, [{f"in_{k}": v for k, v in arrays.items()}], core_ids=[0])
    return np.asarray(r.results[0]["out_0"]).reshape(B, LQ, P)
```

```python
from contextlib import ExitStack

import concourse.bass as bass
from concourse import mybir

ALU = mybir.AluOpType
ACT = mybir.ActivationFunctionType
AX = mybir.AxisListType
F32 = mybir.dt.float32
BF16 = mybir.dt.bfloat16

P = 128
B, LQ, LK = 16, 64, 1601
H, HD = 16, 8
T = B * LQ
NT = T // P
EPS = 1e-5

G = 4
GH = H // G
SHIFT = 96
NK = (LK + P - 1) // P
CH = 401
CHUNKS = [(0, CH), (CH, CH), (2 * CH, CH), (3 * CH, LK - 3 * CH)]
VW, VH, ONE_AT = GH * HD + 1, GH - 1, (GH - 1) * HD
RING = 23
PER = 21

V_BK, V_BQ, V_LN1W, V_LN1B, V_LN2W, V_LN2B = 0, 1, 5, 6, 7, 8
V_CW, V_CB, V_D, V_NW, V_FCB = 9, 21, 24, 26, 28
NV = 32
R_BV, R_BO, R_PB, R_ALOG, R_DTB = 0, 128, 256, 384, 388
NR = 392

MH = 4
E, NH, HT = 8, 3, 114
DT_LAST = 15


def keys_of(k):
    return min(P, LK - k * P)


def attention(nc, A, keep):
    with ExitStack() as ctx:
        def sb(name, shape, dt=F32):
            return ctx.enter_context(nc.sbuf_tensor(name, shape, dt))

        def pb(name, shape, dt=F32):
            return ctx.enter_context(nc.psum_tensor(name, shape, dt))

        def sem(name):
            return ctx.enter_context(nc.semaphore(name))

        wq = sb("wq", [P, G, P])
        wkv = sb("wkv", [P, 2, P])
        wkv_hi = sb("wkv_hi", [P, 2, P], BF16)
        wkv_lo = sb("wkv_lo", [P, 2, P], BF16)
        one = sb("one", [P, 1])
        nident = sb("nident", [P, P])
        bq_scaled = sb("bq_scaled", [P, G])
        bq_exp = sb("bq_exp", [P, G])
        stats = sb("stats", [P, NT, 6])
        mean_var = sb("mean_var", [P, NT, 2])
        rstd = sb("rstd", [P, NT])
        xn = sb("xn", [P, NT, P])
        xnT = sb("xnT", [P, T])
        q_full = sb("q_full", [P, 2, T])
        q_hi = sb("q_hi", [P, 2, T], BF16)
        q_part = sb("q_part", [P, 2, T], BF16)
        q_stack = sb("q_stack", [P, B, G, GH, LQ], BF16)
        ctx_in = sb("ctx_in", [P, 2, LK])
        ctx_hi = sb("ctx_hi", [P, 2, LK], BF16)
        ctx_lo = sb("ctx_lo", [P, 2, LK], BF16)
        k_hi = sb("k_hi", [P, LK], BF16)
        k_lo = sb("k_lo", [P, LK], BF16)
        k_stack = sb("k_stack", [P, 2, G, LK], BF16)
        q_cur = sb("q_cur", [P, 2, G * GH * LQ], BF16)
        values = sb("values", [P, 2, NK, G * VW])
        probs = sb("probs", [P, 2, H * LQ])
        half_max = sb("half_max", [P, 8, 2])
        row_max = sb("row_max", [P, 16])
        shift_hi = sb("shift_hi", [16, P], BF16)
        shift = sb("shift", [16, P], BF16)

        wide = pb("wide", [P, 2, 1024])
        score = pb("score", [P, 2, 512])
        sums = pb("sums", [P, 2, 512])

        s_const = sem("s_const")
        s_later = sem("s_later")
        s_x = sem("s_x")
        s_ctx = [sem(f"s_ctx{i}") for i in range(2)]
        s_wsplit = sem("s_wsplit")
        s_memset = sem("s_memset")
        s_one = sem("s_one")
        s_stat = sem("s_stat")
        s_sqrt = sem("s_sqrt")
        s_xn = sem("s_xn")
        s_xt = sem("s_xt")
        s_xtc = sem("s_xtc")
        s_bq = sem("s_bq")
        s_q = sem("s_q")
        s_qf = sem("s_qf")
        s_qh = sem("s_qh")
        s_qp = sem("s_qp")
        s_ql = sem("s_ql")
        s_ones = sem("s_ones")
        s_qs = sem("s_qs")
        s_split = sem("s_split")
        s_wide = sem("s_wide")
        s_wfree = sem("s_wfree")
        s_khi = sem("s_khi")
        s_stack = [sem(f"s_stack{i}") for i in range(2)]
        s_queries = [sem(f"s_queries{i}") for i in range(2)]
        s_rowmax = sem("s_rowmax")
        s_shift = sem("s_shift")
        s_shin = [sem(f"s_shin{i}") for i in range(2)]
        s_score = sem("s_score")
        s_last = sem("s_last")
        s_exp = sem("s_exp")
        s_pv = sem("s_pv")
        s_sums = sem("s_sums")
        SHIN_N, STACK_N = 16, 3 * 16

        block = ctx.enter_context(nc.Block())

        def run(e, body):
            body(-1, -1, 1)
            with e.Fori(0, B // 2 - 1) as j:
                body(j * 2, j, 0)
                body(j * 2 + 1, j, 1)
            body(B - 2, B // 2 - 1, 0)
            body(B - 1, B // 2 - 1, 1)

        def has(i, ahead):
            return not isinstance(i, int) or 0 <= i + ahead < B

        def slot(par, ahead):
            return (par + ahead) % 2

        def k_slot(par, k):
            return (par * NK + k) % 2

        def ring(i, use):
            if isinstance(i, int) and i == B - 2 and use > 18:
                raise ValueError("no keys any more")
            return i * PER + (RING + use)

        def ring_slot(par, use):
            return (par * PER + RING + use) % 2

        @block.sync
        def _(sp):
            sp.dma_start(keep.x[:], A["x"].rearrange("(t p) d -> p t d", p=P)).then_inc(s_x, 16)
            sp.dma_start(keep.ident[:], A["ident"]).then_inc(s_const, 16)
            sp.dma_start(nident[:], A["nident"]).then_inc(s_const, 16)
            sp.dma_start(keep.marks[:], A["marks"]).then_inc(s_const, 16)
            sp.dma_start(keep.vecs[:], A["vecs"]).then_inc(s_const, 16)
            sp.dma_start(wkv[:], A["wkv"]).then_inc(s_const, 16)
            sp.dma_start(wq[:], A["wq"]).then_inc(s_const, 16)
            sp.dma_start(ctx_in[:, 0, :], A["ctx"][:, 0, :]).then_inc(s_ctx[0], 16)
            sp.dma_start(ctx_in[:, 1, :], A["ctx"][:, 1, :]).then_inc(s_ctx[1], 16)

            def value(v):
                if isinstance(v, int):
                    return v
                r = sp.alloc_register(f"wait_value{len(held)}")
                held.append(r)
                sp.reg_mov(r, v)
                return sp.snap(r, min_val=1)

            held = []

            for to, of in ((keep.iota, A["iota"]), (keep.wo, A["wo"]), (keep.win, A["win"]), (keep.wout, A["wout"]),
                           (keep.wfc, A["wfc"]), (keep.wproj, A["wproj"])):
                sp.dma_start(to[:], of).then_inc(s_later, 16)
            sp.dma_start(keep.rows[:], A["rows"].to_broadcast([P, NR])).then_inc(s_later, 16)

            def body(i, j, par):
                n = slot(par, 1)
                if has(i, 1):
                    high_there, scores_done, low_there = value(i * 4 + 8), value(i + 1), value(ring(i, 0))
                    sp.wait_ge(s_khi, high_there)
                    if has(i, -1):
                        sp.wait_ge(s_last, scores_done)
                    first = isinstance(i, int) and i < 0
                    if first:
                        sp.wait_ge(s_memset, 1)
                    for c in range(2):
                        sp.dma_start(k_stack[32 * c:32 * c + 32, n, :, :], k_hi[:, :]).then_inc(s_stack[n], 16)
                    sp.wait_ge(s_wfree, low_there)
                    sp.dma_start(k_stack[64:96, n, :, :], k_lo[:, :]).then_inc(s_stack[n], 16)
                    if first:
                        sp.wait_ge(s_memset, 2)
                if has(i, 2) and has(i, 0):
                    sp.dma_start(ctx_in[:, par, :], A["ctx"][:, bass.ds(i + 2, 1), :].rearrange(
                        "p b k -> p (b k)")).then_inc(s_ctx[par], 16)
                if has(i, 1):
                    if first:
                        sp.wait_ge(s_queries[n], 16)
                    sp.wait_ge(s_wfree, ring(i, 18) + 1)
                    sp.dma_start(q_cur[SHIFT:SHIFT + 2, n, :], shift[:, :]).then_inc(s_shin[n], 16)

            run(sp, body)
            sp.wait_ge(s_later, 7 * 16)

        @block.gpsimd
        def _(pool):
            pool.memset(one[:], 1.0).then_inc(s_one, 1)
            pool.wait_ge(s_one, 1)
            pool.memset(k_stack[:, 0, :, :], 1.0).then_inc(s_memset, 1)

            def split(i, j, par, ahead):
                n = slot(par, ahead)
                pool.wait_ge(s_ctx[n], (j + (par + ahead) // 2 + 1) * 16)
                if has(i, ahead - 2):
                    pool.wait_ge(s_wide, ring(i + (ahead - 3), 1) + 1)
                pool.tensor_tensor(ctx_hi[:, n, :], ctx_in[:, n, :], one[:].to_broadcast([P, LK]),
                                   ALU.mult).then_inc(s_split, 1)
                pool.wait_ge(s_split, (i + ahead) * 2 + 1)
                pool.tensor_tensor(ctx_lo[:, n, :], ctx_in[:, n, :], ctx_hi[:, n, :],
                                   ALU.subtract).then_inc(s_split, 1)

            split(-1, -1, 1, 1)
            pool.memset(k_stack[:, 1, :, :], 1.0).then_inc(s_memset, 1)

            def body(i, j, par):
                n = slot(par, 1)
                if has(i, 1):
                    if has(i, -1):
                        pool.wait_ge(s_last, i + 1)
                    if isinstance(i, int) and i < 0:
                        pool.wait_ge(s_qs, G)
                        pool.wait_ge(s_ql, G)
                    pool.dma_start(q_cur[:, n, :], q_stack[:, bass.ds(i + 1, 1), :, :, :].rearrange(
                        "p b g h q -> p (b g h q)")).then_inc(s_queries[n], 16)
                if has(i, 2):
                    split(i, j, par, 2)

            run(pool, body)

        @block.tensor
        def _(pe):
            def product3(out, lhs_hi, lhs_lo, rhs_hi, rhs_lo):
                pe.matmul(out, lhs_hi, rhs_hi, start=True, stop=False)
                pe.matmul(out, lhs_hi, rhs_lo, start=False, stop=False)
                return pe.matmul(out, lhs_lo, rhs_hi, start=False, stop=True)

            def keys(i, par, ahead, half, use):
                n, w = slot(par, ahead), use[1]
                if half == 0:
                    pe.wait_ge(s_split, (i + ahead + 1) * 2)
                if not isinstance(use[0], int) or use[0] >= 2:
                    pe.wait_ge(s_wfree, use[0] - 1)
                for c in range(2):
                    at, m = CHUNKS[2 * half + c]
                    last = product3(wide[:, w, 512 * c:512 * c + m], wkv_hi[:, 0, :], wkv_lo[:, 0, :],
                                    ctx_hi[:, n, at:at + m], ctx_lo[:, n, at:at + m])
                last.then_inc(s_wide, 1)

            def vals(i, par, half):
                n, w = slot(par, 1), ring_slot(par, half)
                pe.wait_ge(s_wfree, ring(i, half) - 1)
                for k in range(7 * half, 7 + 6 * half):
                    m, at = keys_of(k), P * (k - 7 * half)
                    ks = slice(k * P, k * P + m)
                    out = wide[0:m, w, at:at + P]
                    last = product3(out, ctx_hi[:, n, ks], ctx_lo[:, n, ks],
                                    wkv_hi[:, 1, :], wkv_lo[:, 1, :])
                last.then_inc(s_wide, 1)

            def maxima(i, par, u):
                pair, half = u // 2, u % 2
                n, w, g = slot(par, 1), ring_slot(par, 2 + u), u // 4
                pe.wait_ge(s_wfree, ring(i, 2 + u) - 1)
                if isinstance(i, int) and i < 0:
                    queries = q_stack[:, 0, g, 2 * (pair % 2):2 * (pair % 2) + 2, :].rearrange("p h q -> p (h q)")
                else:
                    queries = q_cur[:, n, pair * P:pair * P + P]
                for c in range(2):
                    at = min(CHUNKS[2 * half + c][0], LK - CH)
                    last = pe.matmul(wide[:, w, 512 * c:512 * c + CH], queries,
                                     k_stack[:, n, g, at:at + CH], start=True, stop=True)
                last.then_inc(s_wide, 1)

            def turn_max(i, par):
                w = ring_slot(par, 18)
                pe.wait_ge(s_wfree, ring(i, 18) - 1)
                pe.wait_ge(s_rowmax, i + 2)
                pe.matmul(wide[0:16, w, 0:P], row_max[:, :], nident[:], start=True, stop=True).then_inc(s_wide, 1)

            def scores(i, par, k):
                n, m = slot(par, 0), keys_of(k)
                for u in range(2):
                    pe.wait_ge(s_exp, i * (2 * NK) + (2 * k + u + 1))
                    for g in (2 * u, 2 * u + 1):
                        last = pe.matmul(score[0:m, u, 256 * (g % 2):256 * (g % 2) + 256],
                                         k_stack[:, n, g, k * P:k * P + m],
                                         q_cur[:, n, 256 * g:256 * g + 256], start=True, stop=True)
                    last.then_inc(s_last if k == NK - 1 and u else s_score, 1)

            def sum_values(i, par, k):
                n, m = slot(par, 0), keys_of(k)
                if k == 0:
                    pe.wait_ge(s_wfree, ring(i - 1, 1) + 1)
                    pe.wait_ge(s_sums, i + 1)
                pe.wait_ge(s_exp, i * (2 * NK) + (2 * k + 2 + 2))
                for c, (first, heads) in enumerate(((0, VH), (VH, 1))):
                    for g in range(G):
                        q = (GH * g + first) * LQ
                        last = pe.matmul(sums[32 * g:32 * g + 32, c, 0:heads * LQ],
                                         values[0:m, n, k, VW * g + c:VW * g + c + 32],
                                         probs[0:m, k_slot(par, k), q:q + heads * LQ],
                                         start=(k == 0), stop=(k == NK - 1))
                last.then_inc(s_pv, 1)

            pe.sem_inc(s_last, 1)
            pe.wait_ge(s_const, 16 * 6)
            for t in range(NT):
                pe.wait_ge(s_xn, t + 1)
                last = pe.transpose(wide[:, 0, t * P:t * P + P], xn[:, t, :], keep.ident[:])
                if t % 4 == 3:
                    last.then_inc(s_xt, 1)
            pe.wait_ge(s_xtc, 2)
            for g in range(G):
                if g >= 2:
                    pe.wait_ge(s_qh, 2 * g - 2)
                for h in range(2):
                    out = (score if g % 2 else sums)[:, h, :]
                    pe.matmul(out, wq[:, g, :], xnT[:, 512 * h:512 * h + 512],
                              start=True, stop=True).then_inc(s_q, 1)
                if g == 1:
                    pe.wait_ge(s_wsplit, 2)
                if g in (1, 2):
                    keys(0, 0, 0, g - 1, (g - 1, g - 1))
            pe.wait_ge(s_qh, 2 * G)

            def body(i, j, par):
                work, more, last = has(i, 0), has(i, 1), has(i, 2)
                n = slot(par, 1)
                for k in range(NK):
                    if work:
                        if k == 0:
                            pe.wait_ge(s_shin[par], (j + 1) * SHIN_N)
                        scores(i, par, k)
                    if more:
                        if k < 2:
                            vals(i, par, k)
                        if 3 < k < 11:
                            maxima(i, par, 2 * k - 6)
                    if last and k == 12:
                        keys(i, par, 2, 1, (ring(i, 20), ring_slot(par, 20)))
                    if work and k:
                        sum_values(i, par, k - 1)
                    if more:
                        if k == 3:
                            pe.wait_ge(s_stack[n], (j + (par + 1) // 2 + 1) * STACK_N)
                            if work:
                                pe.wait_ge(s_queries[n], (j + (par + 1) // 2 + 1) * 16)
                            else:
                                pe.wait_ge(s_qs, G)
                                pe.wait_ge(s_ql, G)
                            maxima(i, par, 0)
                        if 3 <= k < 11:
                            maxima(i, par, 2 * k - 5)
                        if k == 11:
                            turn_max(i, par)
                    if last and k == 11:
                        keys(i, par, 2, 0, (ring(i, 19), ring_slot(par, 19)))
                if work:
                    sum_values(i, par, NK - 1)

            run(pe, body)

        @block.scalar
        def _(act):
            act.wait_ge(s_const, 16 * 6)
            nc.scalar.mul(bq_scaled[:], keep.vecs[:, V_BQ:V_BQ + G], HD ** -0.5).then_inc(s_bq, 1)
            act.sem_inc(s_exp, 2)
            act.wait_ge(s_stat, 2 * NT + 2)
            nc.scalar.activation(rstd[:], rstd[:], ACT.Sqrt).then_inc(s_sqrt, 1)
            for h in range(2):
                act.wait_ge(s_xt, h + 1)
                nc.scalar.copy(xnT[:, 512 * h:512 * h + 512],
                               wide[:, 0, 512 * h:512 * h + 512]).then_inc(s_xtc, 1)
            act.wait_ge(s_bq, 1)

            def last_head(g):
                act.wait_ge(s_qp, g + 1)
                nc.scalar.mul(q_stack[:, :, g, GH - 1, :], q_part[:, g % 2, :].rearrange("p (b q) -> p b q", b=B),
                              keep.marks[:, GH - 1:GH]).then_inc(s_ql, 1)

            def key_high(i, par, ahead, half, use):
                act.wait_ge(s_wide, use[0] + 1)
                for c in range(2):
                    at, m = CHUNKS[2 * half + c]
                    nc.scalar.activation(k_hi[:, at:at + m], wide[:, use[1], 512 * c:512 * c + m],
                                         ACT.Identity, bias=keep.vecs[:, V_BK:V_BK + 1]).then_inc(s_khi, 1)

            for g in range(G):
                if g >= 2:
                    act.wait_ge(s_qp, g - 1)
                for h in range(2):
                    act.wait_ge(s_q, 2 * g + h + 1)
                    for to, done in ((q_full, s_qf), (q_hi, s_qh)):
                        nc.scalar.activation(to[:, g % 2, 512 * h:512 * h + 512],
                                             (score if g % 2 else sums)[:, h, :], ACT.Identity,
                                             bias=bq_scaled[:, g:g + 1], scale=HD ** -0.5).then_inc(done, 1)
                if g:
                    last_head(g - 1)
                if g in (1, 2):
                    key_high(0, 0, 0, g - 1, (g - 1, g - 1))
            last_head(G - 1)
            nc.scalar.activation(bq_exp[:], bq_scaled[:], ACT.Exp)

            def body(i, j, par):
                for k in range(NK):
                    m = keys_of(k)
                    if has(i, 0):
                        for u in range(2):
                            if k == NK - 1 and u:
                                act.wait_ge(s_last, i + 2)
                            else:
                                act.wait_ge(s_score, i * (2 * NK - 1) + (2 * k + u + 1))
                            if u == 0:
                                act.wait_ge(s_pv, i * NK + (k + 1))
                            nc.scalar.activation(probs[0:m, k_slot(par, k), 512 * u:512 * u + 512],
                                                 score[0:m, u, :], ACT.Exp).then_inc(s_exp, 1)
                    if k == 11 and has(i, 2):
                        n = slot(par, 1)
                        act.wait_ge(s_stack[n], (j + (par + 1) // 2 + 1) * STACK_N)
                    if k >= 11 and has(i, 2):
                        key_high(i, par, 2, k - 11, (ring(i, 8 + k), ring_slot(par, 8 + k)))

            run(act, body)

        @block.vector
        def _(dve):
            dve.sem_inc(s_pv, 2)
            dve.sem_inc(s_sums, 1)
            dve.wait_ge(s_x, 16)
            for t in range(NT):
                dve.bn_stats(stats[:, t, :], keep.x[:, t, :]).then_inc(s_stat, 1)
            for t in range(NT):
                dve.wait_ge(s_stat, t + 1)
                dve.bn_aggr(mean_var[:, t, :], stats[:, t, :]).then_inc(s_stat, 1)
            dve.wait_ge(s_stat, 2 * NT)
            dve.tensor_scalar(rstd[:], mean_var[:, :, 1], EPS, None, ALU.add).then_inc(s_stat, 1)
            dve.wait_ge(s_stat, 2 * NT + 1)
            dve.reciprocal(rstd[:], rstd[:]).then_inc(s_stat, 1)
            dve.wait_ge(s_sqrt, 1)
            for t in range(NT):
                dve.tensor_scalar(xn[:, t, :], keep.x[:, t, :], mean_var[:, t, 0:1], rstd[:, t:t + 1],
                                  ALU.subtract, ALU.mult).then_inc(s_xn, 1)
            dve.wait_ge(s_const, 16 * 6)
            dve.tensor_copy(wkv_hi[:], wkv[:]).then_inc(s_wsplit, 1)
            dve.wait_ge(s_wsplit, 1)
            dve.tensor_tensor(wkv_lo[:], wkv[:], wkv_hi[:], ALU.subtract).then_inc(s_wsplit, 1)
            dve.memset(values[:], 1.0).then_inc(s_ones, 1)

            def key_low(i, par, ahead, half, use):
                for c in range(2):
                    at, m = CHUNKS[2 * half + c]
                    dve.wait_ge(s_khi, (i + ahead) * 4 + (2 * half + c + 1))
                    last = dve.scalar_tensor_tensor(
                        out=k_lo[:, at:at + m], in0=wide[:, use[1], 512 * c:512 * c + m],
                        scalar=keep.vecs[:, V_BK:V_BK + 1], in1=k_hi[:, at:at + m],
                        op0=ALU.add, op1=ALU.subtract)
                last.then_inc(s_wfree, 1)

            for g in range(G):
                s = g % 2
                dve.wait_ge(s_qh, 2 * g + 2)
                if g >= 2:
                    dve.wait_ge(s_ql, g - 1)
                dve.scalar_tensor_tensor(out=q_part[:, s, :], in0=q_hi[:, s, :],
                                         scalar=keep.marks[:, 4:5], in1=q_full[:, s, :],
                                         op0=ALU.mult, op1=ALU.add).then_inc(s_qp, 1)
                dve.wait_ge(s_qp, g + 1)
                for h in range(GH - 1):
                    last = dve.tensor_scalar(q_stack[:, :, g, h, :],
                                             q_part[:, s, :].rearrange("p (b q) -> p b q", b=B),
                                             keep.marks[:, h:h + 1], None, ALU.mult)
                last.then_inc(s_qs, 1)
                if g in (1, 2):
                    key_low(0, 0, 0, g - 1, (g - 1, g - 1))

            def vals(i, par, half):
                n, w = slot(par, 1), ring_slot(par, half)
                dve.wait_ge(s_wide, ring(i, half) + 1)
                parts = [(0, 7, P)] if half == 0 else [(7, 5, P), (12, 1, keys_of(12))]
                for k0, nk, m in parts:
                    at = P * (k0 - 7 * half)
                    src = wide[0:m, w, at:at + P * nk].rearrange("p (k c) -> p k c", k=nk)
                    dst = values[0:m, n, k0:k0 + nk, :]
                    dst, src = (ap.rearrange("p k (g c) -> p k g c", g=G) for ap in (dst, src))
                    dve.tensor_copy(dst[:, :, :, 0:ONE_AT], src[:, :, :, 0:ONE_AT])
                    last = dve.tensor_copy(dst[:, :, :, ONE_AT + 1:VW], src[:, :, :, ONE_AT:GH * HD])
                last.then_inc(s_wfree, 1)

            def body(i, j, par):
                if has(i, 1):
                    if isinstance(i, int) and i < 0:
                        dve.wait_ge(s_ones, 1)
                    vals(i, par, 0)
                    vals(i, par, 1)
                    for u in range(16):
                        dve.wait_ge(s_wide, ring(i, 2 + u) + 1)
                        w = ring_slot(par, 2 + u)
                        dve.tensor_reduce(
                            half_max[:, u // 2, u % 2:u % 2 + 1],
                            wide[:, w, :].rearrange("p (c k) -> p c k", c=2)[:, :, 0:CH],
                            AX.XY, ALU.max).then_inc(s_wfree, 1)
                    dve.wait_ge(s_wfree, ring(i, 17) + 1)
                    dve.tensor_reduce(row_max[:].rearrange("p (a m) -> p a m", a=2),
                                      half_max[:].unsqueeze(1).to_broadcast([P, 2, 8, 2]),
                                      AX.X, ALU.max).then_inc(s_rowmax, 1)
                    dve.wait_ge(s_wide, ring(i, 18) + 1)
                    w = ring_slot(par, 18)
                    if has(i, 0):
                        dve.wait_ge(s_shin[par], (j + 1) * SHIN_N)
                    dve.tensor_copy(shift_hi[:, :], wide[0:16, w, 0:P]).then_inc(s_shift, 1)
                    dve.wait_ge(s_shift, i + 2)
                    dve.scalar_tensor_tensor(out=shift[:, :], in0=shift_hi[:, :],
                                             scalar=keep.marks[0:16, 5:6], in1=wide[0:16, w, 0:P],
                                             op0=ALU.mult, op1=ALU.add).then_inc(s_wfree, 1)
                if has(i, 2):
                    for half in range(2):
                        key_low(i, par, 2, half, (ring(i, 19 + half), ring_slot(par, 19 + half)))
                if has(i, 0):
                    dve.wait_ge(s_pv, i * NK + (NK + 2))
                    out = keep.sums[:, :, bass.ds(i * LQ, LQ)]
                    dve.tensor_copy(out[:, 0:VH, :], sums[:, 0, 0:VH * LQ].rearrange("p (j q) -> p j q", j=VH))
                    dve.tensor_copy(out[:, VH, :], sums[:, 1, 0:LQ]).then_inc(s_sums, 1)

            run(dve, body)


def mamba_mlp(nc, A, keep):
    with ExitStack() as ctx:
        def sb(name, shape, dt=F32):
            return ctx.enter_context(nc.sbuf_tensor(name, shape, dt))

        def pb(name, shape, dt=F32):
            return ctx.enter_context(nc.psum_tensor(name, shape, dt))

        def sem(name):
            return ctx.enter_context(nc.semaphore(name))

        rows, vecs, ident = keep.rows, keep.vecs, keep.ident
        o_tok = sb("o_tok", [P, 4, P])
        o_rden = sb("o_rden", [P, 2, 2, H])
        oT = sb("oT", [P, 4, P])
        x_bias = sb("x_bias", [P, NT, P])
        x1 = sb("x1", [P, NT, P])
        u = sb("u", [P, NT, P])
        v = sb("v", [P, NT, P])
        vT = sb("vT", [P, T])
        stats = sb("stats2", [P, NT, 6])
        mean_var = sb("mean_var2", [P, NT, 2])
        rstd = sb("rstd2", [P, NT])
        rstd12 = sb("rstd12", [P, 2, NT])
        var12 = sb("var12", [P, NT])
        conv = sb("conv", [P, 4, T])
        xbc = sb("xbc", [P, 4, T])
        zg = sb("zg", [P, 2, T])
        dt_x = sb("dt_x", [P, NT, MH])
        dt_a = sb("dt_a", [P, NT, MH])
        dt_e = sb("dt_e", [P, NT, MH])
        dt_u = sb("dt_u", [P, NT, MH])
        dt_l = sb("dt_l", [P, NT, MH])
        dt_m = sb("dt_m", [P, NT, MH])
        dt = sb("dt", [P, NT, MH])
        decay = sb("decay", [P, NT, MH])
        a_exp = sb("a_exp", [P, MH])
        sel_in = sb("sel_in", [3 * MH, MH, P])
        sel = sb("sel", [3 * MH, MH, P], BF16)
        ident_bf = sb("ident_bf", [P, P], BF16)
        decay_parts = sb("decay_parts", [P, NT, 3 * MH], BF16)
        decay_rest = sb("decay_rest", [P, NT, MH])
        decayT = sb("decayT", [3 * MH, T], BF16)
        delta = sb("delta", [P, 8, P])
        decay_all = sb("decay_all", [P, 2, 8 * P])
        gain = sb("gain", [P, 2, 8 * P])
        mix = sb("mix", [P, NT, MH, P])
        y = sb("y", [P, 2, T])
        wout_n = sb("wout_n", [P, 2, P])
        rms = sb("rms", [P, NT])
        y1 = sb("y1", [P, NT, P])
        ones = sb("ones", [P, 1])
        one = sb("one2", [P, 1])
        w_stage = sb("w_stage", [P, 2, 2, NH * HT])
        dtx = keep.sums[:, 0:2, :].rearrange("p c (t k) -> p (c t) k", k=2 * P)
        y_sq = keep.sums[:, 2:4, :]
        hid = conv

        ps = pb("ps", [P, 3, 1024])
        pt = pb("pt", [P, 2, 512])

        s_stage = [sem(f"t_stage{i}") for i in range(2)]
        names = ("w one wsp init xb turn o ot otc att x1 st var sq u ln vt vtc dtp dts dte mm conv silu zin zsil "
                 "ones sel selc dp dpt dpc tsp cen dots tap bc bcc bc0 scan cb mix xt dtx ya yc ysq yss out r rq y1 "
                 "fc gelu pr")
        s = {n: sem("t_" + n) for n in names.split()}
        block = ctx.enter_context(nc.Block())

        def tok(t):
            return slice(t * P, t * P + P)

        def half(h):
            return slice(512 * h, 512 * h + 512)

        def bank(n):
            return ps[:, n // 2, half(n % 2)] if n < 6 else pt[:, n - 6, :]

        MM_BANK = ((2, 3, 4), (5, 0, 1))
        Z_BANK = ((4, 7), (6, 5))
        FC_BANK = ((2, 3, 4, 6), (7, 0, 1, 5))
        TURN_BANK = (4, 6)
        EARLY = 5
        BC_SLOT, CB_SLOT, YA_SLOT = (1, 0, 1, 0), 2, (0, 1)

        @block.sync
        def _(sp):
            sp.dma_start(sel_in[:], A["sel"]).then_inc(s["sel"], 16)
            for e in range(E):
                if e >= 2:
                    sp.wait_ge(s["wsp"], 2 * e - 2)
                sp.dma_start(w_stage[:, e % 2], A["wgu"][:, e]).then_inc(s_stage[e % 2], 16)
            sp.dma_start(keep.w2[:], A["w2"]).then_inc(s["w"], 16)
            sp.dma_start(keep.bgu[:], A["bgu"]).then_inc(s["w"], 16)
            sp.dma_start(keep.b2[:], A["b2"]).then_inc(s["w"], 16)
            sp.dma_start(keep.cent[:], A["cent"]).then_inc(s["w"], 16)
            sp.wait_ge(s["w"], 64)

        @block.gpsimd
        def _(pool):
            pool.tensor_tensor(x_bias[:], keep.x[:], rows[:, R_BO:R_BO + P].unsqueeze(1).to_broadcast(
                [P, NT, P]), ALU.add).then_inc(s["xb"], 1)
            pool.tensor_copy(delta[:], ident[:].unsqueeze(1).to_broadcast([P, 8, P])).then_inc(s["init"], 1)
            for c in range(2):
                pool.tensor_scalar(wout_n[:, c, :], keep.wout[:, c, :], vecs[:, V_NW + c:V_NW + c + 1], None,
                                   ALU.mult).then_inc(s["init"], 1)
            pool.memset(one[:], 1.0).then_inc(s["one"], 1)
            pool.wait_ge(s["one"], 1)
            pool.wait_ge(s["sel"], 16)
            pool.tensor_copy(sel[:], sel_in[:]).then_inc(s["selc"], 1)
            pool.tensor_copy(ident_bf[:], ident[:]).then_inc(s["selc"], 1)

            def split(e):
                pool.wait_ge(s_stage[e % 2], 16 * (e // 2 + 1))
                src = w_stage[:, e % 2].rearrange("p g c -> p (g c)")
                hi = keep.w_hi[:, e].rearrange("p g c -> p (g c)")
                lo = keep.w_lo[:, e].rearrange("p g c -> p (g c)")
                pool.tensor_tensor(hi, src, one[:].to_broadcast([P, 2 * NH * HT]), ALU.mult).then_inc(s["wsp"], 1)
                pool.wait_ge(s["wsp"], 2 * e + 1)
                pool.tensor_tensor(lo, src, hi, ALU.subtract).then_inc(s["wsp"], 1)

            for e in range(EARLY):
                split(e)
            for t in range(NT):
                pool.wait_ge(s["sq"], t // 4 + 1)
                pool.tensor_scalar(u[:, t, :], x1[:, t, :], mean_var[:, t, 0:1], rstd12[:, 0, t:t + 1],
                                   ALU.subtract, ALU.mult).then_inc(s["u"], 1)
            for c in range(4):
                pool.wait_ge(s["bcc"], c + 1)
                pool.memset(decay_all[:, c % 2, :].rearrange("p (c q) -> p c q", q=LQ)[:, :, 0:1],
                            0.0).then_inc(s["bc0"], 1)
            for e in range(EARLY, E):
                split(e)
            pool.memset(keep.ones[:], 1.0).then_inc(s["cen"], 1)
            pool.wait_ge(s["w"], 64)
            pool.tensor_tensor(keep.cent_sq[:], keep.cent[:], keep.cent[:], ALU.mult).then_inc(s["cen"], 1)
            for h in range(2):
                pool.wait_ge(s["ysq"], 2 * h + 2)
                pool.tensor_tensor(y_sq[:, 0, half(h)], y_sq[:, 0, half(h)], y_sq[:, 1, half(h)],
                                   ALU.add).then_inc(s["yss"], 1)

        @block.tensor
        def _(pe):
            def turn(p):
                if p >= 2:
                    pe.wait_ge(s["o"], p - 1)
                for k in range(2):
                    t = 2 * p + k
                    for j in range(GH):
                        last = pe.transpose(bank(2 * (p % 2) + k)[:, tok(j)], keep.sums[:, j, tok(t)], ident[:])
                last.then_inc(s["turn"], 1)

            turn(0)
            turn(1)
            for p in range(NT // 2):
                pe.wait_ge(s["o"], p + 1)
                if p:
                    pe.wait_ge(s["otc"], p)
                for k in range(2):
                    last = pe.transpose(bank(6)[:, tok(k)], o_tok[:, 2 * (p % 2) + k, :], ident[:])
                last.then_inc(s["ot"], 1)
                if p + 2 < NT // 2:
                    turn(p + 2)
                pe.wait_ge(s["otc"], p + 1)
                if p:
                    pe.wait_ge(s["x1"], p)
                for k in range(2):
                    last = pe.matmul(bank(7)[:, tok(k)], oT[:, 2 * (p % 2) + k, :], keep.wo[:],
                                     start=True, stop=True)
                last.then_inc(s["att"], 1)

            def turn_v(n, h, b):
                for t in range(4 * h, 4 * h + 4):
                    pe.wait_ge(s["ln"], n * NT + t + 1)
                    last = pe.transpose(bank(b)[:, tok(t % 4)], v[:, t, :], ident[:])
                last.then_inc(s["vt"], 1)

            def project_x(h, c):
                pe.matmul(bank(MM_BANK[h][c]), keep.win[:, 256 + P * c:256 + P * c + P], vT[:, half(h)],
                          start=True, stop=True).then_inc(s["mm"], 1)

            for h in range(2):
                turn_v(0, h, h)
                pe.wait_ge(s["vtc"], h + 1)
                if h == 0:
                    project_x(0, 0)
                    project_x(0, 1)
            for t in range(NT):
                last = pe.matmul(bank(6)[:, MH * t:MH * t + MH], vT[:, tok(t)], keep.win[:, 640:644],
                                 start=True, stop=True)
            last.then_inc(s["dtp"], 1)
            for h, c in ((0, 2), (1, 0), (1, 1), (1, 2)):
                project_x(h, c)
            for h in range(2):
                for c in range(2):
                    if c == 0:
                        pe.wait_ge(*((s["conv"], 3), (s["dts"], 2))[h])
                    elif h:
                        pe.wait_ge(s["conv"], 4)
                    pe.matmul(bank(Z_BANK[h][c]), keep.win[:, P * c:P * c + P], vT[:, half(h)],
                              start=True, stop=True).then_inc(s["zin"], 1)

            def spread(c):
                if c == 1:
                    pe.wait_ge(s["conv"], 6)
                if c >= 2:
                    pe.wait_ge(s["bcc"], c - 1)
                for t in range(2):
                    for h in range(MH):
                        last = pe.matmul(ps[:, BC_SLOT[c], P * (MH * t + h):P * (MH * t + h) + P],
                                         sel[:, h, :], decayT[:, tok(2 * c + t)], start=True, stop=True)
                last.then_inc(s["bc"], 1)

            def turn_x(t):
                if t >= 2:
                    pe.wait_ge(s["dtx"], t - 1)
                for c in range(2):
                    last = pe.transpose(pt[:, t % 2, P * c:P * c + P], xbc[:, c, tok(t)], ident[:])
                last.then_inc(s["xt"], 1)

            pe.wait_ge(s["selc"], 2)
            pe.wait_ge(s["dp"], 3)
            for t in range(NT):
                last = pe.matmul(ps[0:3 * MH, 1, tok(t)], decay_parts[:, t, :], ident_bf[:], start=True, stop=True)
            last.then_inc(s["dpt"], 1)
            pe.wait_ge(s["dpc"], 1)
            spread(0)

            def overlap(h):
                pe.wait_ge(s["silu"], 4 * h + 4)
                for t in range(4 * h, 4 * h + 4):
                    last = pe.matmul(ps[:, CB_SLOT, tok(t)], xbc[0:64, 2, tok(t)], xbc[0:64, 3, tok(t)],
                                     start=True, stop=True)
                last.then_inc(s["cb"], 1)

            pe.wait_ge(s["zsil"], 1)
            overlap(0)
            spread(1)
            pe.wait_ge(s["zsil"], 4)
            turn_x(0)
            turn_x(1)
            spread(2)
            overlap(1)
            spread(3)
            for t in range(2, NT):
                turn_x(t)
            for h2 in range(2):
                pe.wait_ge(s["bcc"], 4)
                pe.wait_ge(s["dtx"], 4 * h2 + 4)
                for t in range(4):
                    pe.wait_ge(s["mix"], 4 * h2 + t + 1)
                    for h in range(MH):
                        r = 64 * (h % 2)
                        last = pe.matmul(ps[r:r + 64, YA_SLOT[h2], 512 * (h // 2) + P * t:512 * (h // 2) + P * t + P],
                                         dtx[:, 4 * h2 + t, 64 * h:64 * h + 64], mix[:, 4 * h2 + t, h, :],
                                         start=True, stop=True)
                last.then_inc(s["ya"], 1)
            pe.wait_ge(s["mix"], NT)
            pe.wait_ge(s["init"], 3)
            pe.wait_ge(s["ones"], 1)
            for h in range(2):
                pe.wait_ge(s["yc"], 2 * h + 2)
                for t in range(4 * h, 4 * h + 4):
                    for c in range(2):
                        last = pe.matmul(ps[:, CB_SLOT, tok(t)], y[:, c, tok(t)], wout_n[:, c, :],
                                         start=(c == 0), stop=(c == 1))
                pe.wait_ge(s["yss"], h + 1)
                for t in range(4 * h, 4 * h + 4):
                    last = pe.matmul(bank(6 + h)[:, t:t + 1], y_sq[:, 0, tok(t)], ones[:], start=True, stop=True)
                last.then_inc(s["out"], 1)

            turn_v(1, 0, 0)
            for h in range(2):
                pe.wait_ge(s["vtc"], 3 + h)
                for c in range(4):
                    if h == 0 and c == 3:
                        turn_v(1, 1, 1)
                    pe.matmul(bank(FC_BANK[h][c]), keep.wfc[:, P * c:P * c + P], vT[:, half(h)],
                              start=True, stop=True).then_inc(s["fc"], 1)
            for h in range(2):
                pe.wait_ge(s["gelu"], 4 * h + 4)
                for t in range(4):
                    for c in range(4):
                        last = pe.matmul(bank(FC_BANK[h][t])[:, 0:P], hid[:, c, tok(4 * h + t)], keep.wproj[:, c, :],
                                         start=(c == 0), stop=(c == 3))
                    last.then_inc(s["pr"], 1)
            turn_v(2, 0, TURN_BANK[0])
            pe.wait_ge(s["cen"], 2)
            pe.wait_ge(s["vtc"], 5)
            pe.matmul(bank(2)[:, 0:E], keep.ones[:], keep.cent_sq[:], start=True, stop=True)
            for t in range(4):
                last = pe.matmul(bank(2)[:, E * t + E:E * t + 2 * E], keep.tT[:, tok(t)], keep.cent[:],
                                 start=True, stop=True)
            last.then_inc(s["dots"], 1)
            turn_v(2, 1, TURN_BANK[1])

        @block.scalar
        def _(act):
            def root(n, buf):
                act.wait_ge(s["var"], n)
                nc.scalar.activation(buf, buf, ACT.Sqrt).then_inc(s["sq"], 1)

            for p in range(NT // 2):
                act.wait_ge(s["ot"], p + 1)
                if p >= 2:
                    act.wait_ge(s["att"], p - 1)
                nc.scalar.copy(oT[:, 2 * (p % 2):2 * (p % 2) + 2, :].rearrange("p t c -> p (t c)"),
                               bank(6)[:, 0:2 * P]).then_inc(s["otc"], 1)

            def turned(n, h, w, b):
                act.wait_ge(s["vt"], 2 * n + h + 1)
                nc.scalar.activation(vT[:, half(h)], bank(h), ACT.Identity, bias=vecs[:, b:b + 1],
                                     scale=vecs[:, w:w + 1]).then_inc(s["vtc"], 1)

            def last_tap(h, c):
                act.wait_ge(s["mm"], 3 * h + c + 1)
                nc.scalar.activation(conv[:, c, half(h)], bank(MM_BANK[h][c]), ACT.Identity,
                                     bias=vecs[:, V_CB + c:V_CB + c + 1],
                                     scale=vecs[:, V_CW + 4 * c + 3:V_CW + 4 * c + 4]).then_inc(s["tap"], 1)

            root(1, rstd12[:, :, 0:4])
            turned(0, 0, V_LN1W, V_LN1B)
            root(2, rstd12[:, :, 4:8])
            last_tap(0, 0)
            turned(0, 1, V_LN1W, V_LN1B)
            last_tap(0, 1)

            def conv_silu(h):
                for c in range(4):
                    act.wait_ge(s["conv"], 3 * h + min(c, 2) + 1)
                    m, src = (P, conv[:, c, half(h)]) if c < 2 else (64, conv[64 * (c - 2):64 * (c - 1), 2, half(h)])
                    nc.scalar.activation(xbc[0:m, c, half(h)], src, ACT.Silu).then_inc(s["silu"], 1)

            def gate_silu(h):
                for c in range(2):
                    act.wait_ge(s["zin"], 2 * h + c + 1)
                    nc.scalar.activation(zg[:, c, half(h)], bank(Z_BANK[h][c]), ACT.Silu).then_inc(s["zsil"], 1)

            act.wait_ge(s["dts"], 4)
            nc.scalar.activation(dt_e[:], dt_a[:], ACT.Exp).then_inc(s["dte"], 1)
            nc.scalar.activation(a_exp[:], rows[:, R_ALOG:R_ALOG + MH], ACT.Exp).then_inc(s["dte"], 1)
            last_tap(0, 2)
            last_tap(1, 0)
            act.wait_ge(s["dts"], 5)
            nc.scalar.activation(dt_l[:], dt_u[:], ACT.Ln).then_inc(s["dte"], 1)
            last_tap(1, 1)
            last_tap(1, 2)
            act.wait_ge(s["dts"], DT_LAST - 1)
            nc.scalar.activation(decay[:], decay[:], ACT.Exp, scale=-1.0).then_inc(s["dts"], 1)
            conv_silu(0)
            act.wait_ge(s["dpt"], 1)
            nc.scalar.copy(decayT[:], ps[0:3 * MH, 1, :]).then_inc(s["dpc"], 1)
            gate_silu(0)
            for c in range(4):
                if c == 1:
                    gate_silu(1)
                    conv_silu(1)
                act.wait_ge(s["bc"], c + 1)
                if c >= 2:
                    act.wait_ge(s["scan"], c - 1)
                nc.scalar.copy(decay_all[:, c % 2, :], ps[:, BC_SLOT[c], :]).then_inc(s["bcc"], 1)
            for h in range(2):
                for c in range(2):
                    act.wait_ge(s["yc"], 2 * h + c + 1)
                    nc.scalar.square(y_sq[:, c, half(h)], y[:, c, half(h)]).then_inc(s["ysq"], 1)
            for h in range(2):
                act.wait_ge(s["r"], 2 * h + 2)
                nc.scalar.activation(rms[:, 4 * h:4 * h + 4], rms[:, 4 * h:4 * h + 4], ACT.Sqrt).then_inc(s["rq"], 1)
                if h:
                    turned(1, 0, V_LN2W, V_LN2B)
                root(3 + h, rstd[:, 4 * h:4 * h + 4])
            turned(1, 1, V_LN2W, V_LN2B)
            for h in range(2):
                for c in range(4):
                    act.wait_ge(s["fc"], 4 * h + c + 1)
                    nc.scalar.activation(hid[:, c, half(h)], bank(FC_BANK[h][c]), ACT.Gelu,
                                         bias=vecs[:, V_FCB + c:V_FCB + c + 1]).then_inc(s["gelu"], 1)
            for h in range(2):
                root(5 + h, rstd[:, 4 * h:4 * h + 4])
                if h == 0:
                    act.wait_ge(s["vt"], 5)
                    nc.scalar.copy(keep.tT[:, half(0)], bank(TURN_BANK[0])).then_inc(s["vtc"], 1)
            act.wait_ge(s["vt"], 6)
            nc.scalar.copy(keep.tT[:, half(1)], bank(TURN_BANK[1])).then_inc(s["vtc"], 1)

        @block.vector
        def _(dve):
            st = [0]

            def count(ins):
                st[0] += 1
                ins.then_inc(s["st"], 1)

            def settle():
                dve.wait_ge(s["st"], st[0])

            def one_by_one(*steps):
                for ins in steps:
                    count(ins())
                    settle()

            def moments(src, h, ahead=None):
                for t in range(4 * h, 4 * h + 4):
                    if ahead:
                        ahead(t)
                    count(dve.bn_stats(stats[:, t, :], src[:, t, :]))
                settle()
                for t in range(4 * h, 4 * h + 4):
                    count(dve.bn_aggr(mean_var[:, t, :], stats[:, t, :]))
                settle()

            def norm_request(src, h, ahead=None):
                moments(src, h, ahead)
                r = rstd[:, 4 * h:4 * h + 4]
                one_by_one(lambda: dve.tensor_scalar(r, mean_var[:, 4 * h:4 * h + 4, 1], EPS, None, ALU.add))
                dve.reciprocal(r, r).then_inc(s["var"], 1)

            def norm_apply(src, h, n, scales):
                dve.wait_ge(s["sq"], n)
                for t in range(4 * h, 4 * h + 4):
                    dve.tensor_scalar(v[:, t, :], src[:, t, :], mean_var[:, t, 0:1], scales[:, t:t + 1],
                                      ALU.subtract, ALU.mult).then_inc(s["ln"], 1)

            dve.memset(ones[:], 1.0).then_inc(s["ones"], 1)

            def divide(p):
                w = p % 2
                dve.wait_ge(s["turn"], p + 1)
                if p >= 2:
                    dve.wait_ge(s["ot"], p - 1)
                both = slice(2 * w, 2 * w + 2)
                r = o_rden[:, w, :, :].rearrange("p t (g j) -> p t g j", j=GH)
                o = o_tok[:, both, :].rearrange("p t (g j c) -> p t g j c", g=G, j=GH)
                raw = ps[:, w, :].rearrange("p (t j g c) -> p t g j c", t=2, j=GH, g=G)
                count(dve.reciprocal(r[:, :, :, 0:VH], raw[:, :, :, 0:VH, ONE_AT]))
                count(dve.reciprocal(r[:, :, :, VH], raw[:, :, :, VH, ONE_AT - 1]))
                settle()
                for j in range(GH):
                    count(dve.tensor_tensor(o[:, :, :, j, :], raw[:, :, :, j, HD * j:HD * j + HD],
                                            r[:, :, :, j].unsqueeze(3).to_broadcast([P, 2, G, HD]), ALU.mult))
                settle()
                dve.tensor_tensor(o_tok[:, both, :], o_tok[:, both, :],
                                  rows[:, R_BV:R_BV + P].unsqueeze(1).to_broadcast([P, 2, P]),
                                  ALU.add).then_inc(s["o"], 1)

            def residual(p):
                if p == 0:
                    dve.wait_ge(s["xb"], 1)
                dve.wait_ge(s["att"], p + 1)
                dve.tensor_tensor(x1[:, 2 * p:2 * p + 2, :], x_bias[:, 2 * p:2 * p + 2, :],
                                  bank(7)[:, 0:2 * P].rearrange("p (t c) -> p t c", t=2),
                                  ALU.add).then_inc(s["x1"], 1)

            def norm_twice_request(h):
                dve.wait_ge(s["x1"], 2 * h + 2)
                moments(x1, h)
                tiles = slice(4 * h, 4 * h + 4)
                var, a, both, w = mean_var[:, tiles, 1], rstd12[:, 0, tiles], rstd12[:, 1, tiles], var12[:, tiles]
                one_by_one(lambda: dve.tensor_scalar(a, var, EPS, None, ALU.add),
                           lambda: dve.reciprocal(a, a),
                           lambda: dve.tensor_tensor(w, var, a, ALU.mult),
                           lambda: dve.tensor_scalar(w, w, EPS, None, ALU.add),
                           lambda: dve.reciprocal(w, w))
                dve.tensor_tensor(both, w, a, ALU.mult).then_inc(s["var"], 1)

            divide(0)
            divide(1)
            residual(0)
            divide(2)
            residual(1)
            divide(3)
            norm_twice_request(0)
            residual(2)
            norm_apply(x1, 0, 1, rstd12[:, 1, :])
            residual(3)
            norm_twice_request(1)
            norm_apply(x1, 1, 2, rstd12[:, 1, :])

            def convolve(h, c):
                dve.wait_ge(s["tap"], 3 * h + c + 1)
                src = bank(MM_BANK[h][c]).rearrange("p (b q) -> p b q", q=LQ)
                dst = conv[:, c, half(h)].rearrange("p (b q) -> p b q", q=LQ)
                cw = vecs[:, V_CW + 4 * c:V_CW + 4 * c + 4]
                for k in range(1, 4):
                    settle()
                    ins = dve.scalar_tensor_tensor(out=dst[:, :, k:], in0=src[:, :, 0:LQ - k],
                                                   scalar=cw[:, 3 - k:4 - k], in1=dst[:, :, k:],
                                                   op0=ALU.mult, op1=ALU.add)
                    if k < 3:
                        count(ins)
                    else:
                        ins.then_inc(s["conv"], 1)

            n = [0]

            def step(ins):
                n[0] += 1
                ins.then_inc(s["dts"], 1)
                dve.wait_ge(s["dts"], n[0])

            def per_head(ap):
                return ap.unsqueeze(1).to_broadcast([P, NT, MH])

            convolve(0, 0)
            convolve(0, 1)
            dve.wait_ge(s["dtp"], 1)
            step(dve.tensor_tensor(dt_x[:], bank(6)[:, 0:MH * NT].rearrange("p (t h) -> p t h", h=MH),
                                   per_head(rows[:, R_DTB:R_DTB + MH]), ALU.add))
            step(dve.tensor_scalar(dt_a[:], dt_x[:], -1.0, None, ALU.mult))
            step(dve.tensor_tensor(dt_a[:], dt_a[:], dt_x[:], ALU.min))
            step(dve.tensor_scalar(dt[:], dt_x[:], 0.0, None, ALU.max))
            convolve(0, 2)
            dve.wait_ge(s["dte"], 2)
            step(dve.tensor_scalar(dt_u[:], dt_e[:], 1.0, None, ALU.add))
            step(dve.tensor_scalar(dt_a[:], dt_u[:], -1.0, None, ALU.add))
            step(dve.tensor_scalar(dt_m[:], dt_a[:], 0.0, None, ALU.is_equal))
            step(dve.tensor_tensor(dt_a[:], dt_a[:], dt_m[:], ALU.add))
            step(dve.reciprocal(dt_a[:], dt_a[:]))
            step(dve.tensor_tensor(dt_a[:], dt_a[:], dt_e[:], ALU.mult))
            convolve(1, 0)
            dve.wait_ge(s["dte"], 3)
            step(dve.tensor_tensor(dt_m[:], dt_m[:], dt_l[:], ALU.add))
            step(dve.tensor_tensor(dt_m[:], dt_m[:], dt_a[:], ALU.mult))
            step(dve.tensor_tensor(dt[:], dt[:], dt_m[:], ALU.add))
            step(dve.tensor_tensor(decay[:], dt[:], per_head(a_exp[:, 0:MH]), ALU.mult))
            assert n[0] == DT_LAST - 1
            convolve(1, 1)
            dve.wait_ge(s["dts"], DT_LAST)
            rest = decay
            for part in range(3):
                to = decay_parts[:, :, MH * part:MH * part + MH]
                if part < 2:
                    count(dve.tensor_copy(to, rest[:]))
                    settle()
                    dve.tensor_tensor(decay_rest[:], rest[:], to, ALU.subtract).then_inc(s["dp"], 1)
                    dve.wait_ge(s["dp"], part + 1)
                    rest = decay_rest
                else:
                    dve.tensor_copy(to, rest[:]).then_inc(s["dp"], 1)
            convolve(1, 2)

            for c in range(4):
                dve.wait_ge(s["bc0"], c + 1)
                if c == 0:
                    dve.wait_ge(s["init"], 3)
                dve.tensor_tensor_scan(gain[:, c % 2, :], decay_all[:, c % 2, :],
                                       delta[:].rearrange("p c q -> p (c q)"), 0.0,
                                       ALU.mult, ALU.add).then_inc(s["scan"], 1)
                if c % 2 == 0:
                    dve.wait_ge(s["cb"], c // 2 + 1)
                if c == 0:
                    dve.wait_ge(s["dts"], DT_LAST)
                dve.wait_ge(s["scan"], c + 1)
                for t in (2 * c, 2 * c + 1):
                    dve.tensor_tensor(mix[:, t, :, :], gain[:, c % 2, half(t % 2)].rearrange(
                        "p (h q) -> p h q", h=MH), ps[:, CB_SLOT, tok(t)].unsqueeze(1).to_broadcast([P, MH, P]),
                        ALU.mult).then_inc(s["mix"], 1)
                for t in (2 * c, 2 * c + 1):
                    dve.wait_ge(s["xt"], t + 1)
                    dve.tensor_tensor(dtx[:, t, :].rearrange("p (h c) -> p h c", h=MH),
                                      pt[:, t % 2, 0:2 * P].rearrange("p (h c) -> p h c", h=MH),
                                      dt[:, t, :].unsqueeze(2).to_broadcast([P, MH, 64]),
                                      ALU.mult).then_inc(s["dtx"], 1)
            dve.wait_ge(s["zsil"], 4)
            for h in range(2):
                dve.wait_ge(s["ya"], h + 1)
                for c in range(2):
                    count(dve.scalar_tensor_tensor(out=y[:, c, half(h)], in0=xbc[:, c, half(h)],
                                                   scalar=vecs[:, V_D + c:V_D + c + 1],
                                                   in1=ps[:, YA_SLOT[h], half(c)], op0=ALU.mult, op1=ALU.add))
                    settle()
                    dve.tensor_tensor(y[:, c, half(h)], y[:, c, half(h)], zg[:, c, half(h)],
                                      ALU.mult).then_inc(s["yc"], 1)
            dve.wait_ge(s["u"], NT)
            for h in range(2):
                tiles = slice(4 * h, 4 * h + 4)
                dve.wait_ge(s["out"], h + 1)
                dve.tensor_scalar(rms[:, tiles], bank(6 + h)[:, tiles], 1.0 / 256, EPS,
                                  ALU.mult, ALU.add).then_inc(s["r"], 1)
                dve.wait_ge(s["r"], 2 * h + 1)
                dve.reciprocal(rms[:, tiles], rms[:, tiles]).then_inc(s["r"], 1)
                if h:
                    norm_apply(y1, 0, 3, rstd)
                dve.wait_ge(s["rq"], h + 1)
                for t in range(4 * h, 4 * h + 4):
                    dve.scalar_tensor_tensor(out=y1[:, t, :], in0=ps[:, CB_SLOT, tok(t)], scalar=rms[:, t:t + 1],
                                             in1=u[:, t, :], op0=ALU.mult, op1=ALU.add).then_inc(s["y1"], 1)
                dve.wait_ge(s["y1"], 4 * h + 4)
                norm_request(y1, h)
            norm_apply(y1, 1, 4, rstd)
            one_by_one(lambda: dve.tensor_tensor(keep.x[:], x1[:], y1[:], ALU.add),
                       lambda: dve.tensor_tensor(keep.x[:], keep.x[:], rows[:, R_PB:R_PB + P].unsqueeze(
                           1).to_broadcast([P, NT, P]), ALU.add))
            for h in range(2):
                def add(t):
                    dve.wait_ge(s["pr"], t + 1)
                    one_by_one(lambda: dve.tensor_tensor(keep.x[:, t, :], keep.x[:, t, :],
                                                         bank(FC_BANK[h][t % 4])[:, 0:P], ALU.add))

                norm_request(keep.x, h, add)
                norm_apply(keep.x, h, 5 + h, rstd)
            dve.wait_ge(s["dots"], 1)
            count(dve.tensor_copy(keep.dots[:], bank(2)[:, 0:5 * E]))
            one_by_one(lambda: dve.tensor_tensor(keep.norms[:], rstd[:], rstd[:], ALU.mult),
                       lambda: dve.scalar_tensor_tensor(out=keep.norms[:], in0=mean_var[:, :, 1], scalar=float(P),
                                                        in1=keep.norms[:], op0=ALU.mult, op1=ALU.mult))
            dve.wait_ge(s["vtc"], 5)
            dve.tensor_copy(keep.t_hi[:, half(0)], keep.tT[:, half(0)]).then_inc(s["tsp"], 1)
            dve.wait_ge(s["tsp"], 1)
            dve.tensor_tensor(keep.t_lo[:, half(0)], keep.tT[:, half(0)], keep.t_hi[:, half(0)],
                              ALU.subtract).then_inc(s["tsp"], 1)


def experts(nc, A, keep, out):
    with ExitStack() as ctx:
        def sb(name, shape, dt=F32):
            return ctx.enter_context(nc.sbuf_tensor(name, shape, dt))

        def pb(name, shape, dt=F32):
            return ctx.enter_context(nc.psum_tensor(name, shape, dt))

        def sem(name):
            return ctx.enter_context(nc.semaphore(name))

        tT, ident = keep.tT, keep.ident
        bgu, b2, cent = keep.bgu, keep.b2, keep.cent
        acc = keep.x
        gate_bias = sb("gate_bias", [HT, 2, NH])
        t_hi, t_lo, norms = keep.t_hi, keep.t_lo, keep.norms
        w_hi, w_lo = keep.w_hi, keep.w_lo
        dist2 = sb("dist2", [P, NT, E])
        top = sb("top", [P, NT, 8])
        top_i = sb("top_i", [P, NT, 8], mybir.dt.uint32)
        top_f = sb("top_f", [P, NT, 2])
        far = sb("far", [P, NT, 2])
        wts = sb("wts", [P, NT, 2])
        gap = sb("gap", [P, NT])
        pick = sb("pick", [P, NT, E])
        we = sb("we", [P, NT, E])
        weT = sb("weT", [E, NT, P])
        gate = sb("gate", [HT, 2, 512])
        hid = sb("hid_e", [HT, 2, NH, 512])

        gu = pb("gu", [P, 2, 2, 512])
        down = pb("down", [P, 2, 512])
        small = pb("small", [P, 2, 512])

        names = "w gb sp nrm rt top te sel weT wtc gu gate hid down acc b2"
        s = {n: sem("e_" + n) for n in names.split()}
        block = ctx.enter_context(nc.Block())

        def tok(t):
            return slice(t * P, t * P + P)

        def per_expert(eng, up, down, route):
            route(0)
            up(0, 0, 0, None)
            route(1)
            up(0, 1, 0, None)
            route(2)
            down(0, 0, 0)
            down(0, 0, 1)
            up(1, 0, 1, lambda part: down(0, 1, part))
            route(3)

            def body(e, par, more):
                up(e, 1, par, lambda part: down(e, 0, part))
                if more:
                    up(e + 1, 0, 1 - par, lambda part: down(e, 1, part))
                else:
                    down(e, 1, 0)
                    down(e, 1, 1)

            with eng.Fori(0, E // 2 - 1) as j:
                body(j * 2 + 1, 1, True)
                body(j * 2 + 2, 0, True)
            route(4)
            body(E - 1, 1, False)

        @block.sync
        def _(sp):
            rows_out = out.rearrange("(t p) d -> p t d", p=P)
            for h in range(2):
                sp.wait_ge(s["acc"], 2 * E + 1 + h)
                sp.dma_start(rows_out[:, 4 * h:4 * h + 4, :], acc[:, 4 * h:4 * h + 4, :]).then_inc(s["w"], 16)
            sp.wait_ge(s["w"], 2 * 16)

        @block.tensor
        def _(pe):
            def route(step):
                if step == 0:
                    for t in range(4):
                        last = pe.matmul(small[:, 0, E * t:E * t + E], tT[:, tok(4 + t)], cent[:],
                                         start=True, stop=True)
                    last.then_inc(s["nrm"], 1)
                if step == 3:
                    pe.wait_ge(s["sel"], 1)
                    for t in range(NT):
                        last = pe.transpose(small[0:E, t // 4, tok(t % 4)], we[:, t, :], ident[:])
                    last.then_inc(s["weT"], 1)
                if step == 4:
                    pe.wait_ge(s["wtc"], 2)
                    for t in range(NT):
                        last = pe.matmul(small[:, t // 4, tok(t % 4)], weT[:, t, :], b2[:], start=True, stop=True)
                    last.then_inc(s["b2"], 1)

            def finish(e, h, part):
                if part == 0:
                    pe.wait_ge(s["hid"], e * 6 + (3 * h + 3 + 2))
                    pe.wait_ge(s["acc"], e * 2 + (h + 1))
                for t in (2 * part, 2 * part + 1):
                    for n in range(NH):
                        last = pe.matmul(down[:, h, P * t:P * t + P], hid[:, h, n, P * t:P * t + P],
                                         keep.w2[:, bass.ds(e, 1), n, :].rearrange("p e c -> p (e c)"),
                                         start=(n == 0), stop=(n == NH - 1))
                if part:
                    last.then_inc(s["down"], 1)

            def up(e, h, par, between):
                if isinstance(e, int) and e == 0 and h == 1:
                    pe.wait_ge(s["sp"], 2)
                half = slice(512 * h, 512 * h + 512)
                for n in range(NH):
                    w = (3 * h + n) % 2
                    pe.wait_ge(s["hid"], e * 6 + (3 * h + n + 1))
                    for k in range(2):
                        o = gu[0:HT, w, k, :]
                        hi = w_hi[:, bass.ds(e, 1), k, HT * n:HT * n + HT].rearrange("p e c -> p (e c)")
                        lo = w_lo[:, bass.ds(e, 1), k, HT * n:HT * n + HT].rearrange("p e c -> p (e c)")
                        pe.matmul(o, hi, t_hi[:, half], start=True, stop=False)
                        pe.matmul(o, hi, t_lo[:, half], start=False, stop=False)
                        last = pe.matmul(o, lo, t_hi[:, half], start=False, stop=True)
                    last.then_inc(s["gu"], 1)
                    if between and n:
                        between(n - 1)

            per_expert(pe, up, finish, route)

        @block.scalar
        def _(act):
            def route(step):
                if step == 0:
                    act.wait_ge(s["top"], NT + 1)
                    nc.scalar.activation(far[:], far[:], ACT.Sqrt).then_inc(s["te"], 1)
                if step == 1:
                    act.wait_ge(s["rt"], 5)
                    nc.scalar.activation(gap[:], gap[:], ACT.Tanh, scale=0.5).then_inc(s["te"], 1)
                if step == 3:
                    act.wait_ge(s["weT"], 1)
                    for h in range(2):
                        nc.scalar.copy(weT[:, 4 * h:4 * h + 4, :].rearrange("p t c -> p (t c)"),
                                       small[0:E, h, :]).then_inc(s["wtc"], 1)

            def gates(e, h, par, between):
                if h == 0:
                    nc.scalar.copy(gate_bias[:, par, :], bgu[:, bass.ds(e, 1), 0, :].rearrange(
                        "p e c -> p (e c)")).then_inc(s["gb"], 1)
                    act.wait_ge(s["gb"], e + 1)
                for n in range(NH):
                    w = (3 * h + n) % 2
                    act.wait_ge(s["gu"], e * 6 + (3 * h + n + 1))
                    act.wait_ge(s["hid"], e * 6 + (3 * h + n + 1))
                    nc.scalar.activation(gate[:, w, :], gu[0:HT, w, 0, :], ACT.Silu,
                                         bias=gate_bias[:, par, n:n + 1]).then_inc(s["gate"], 1)

            per_expert(act, gates, lambda e, h, part: None, route)
        @block.vector
        def _(dve):
            dve.sem_inc(s["hid"], 2)
            dve.sem_inc(s["acc"], 2)
            second = slice(512, 1024)
            dve.tensor_copy(t_hi[:, second], tT[:, second]).then_inc(s["sp"], 1)
            dve.wait_ge(s["sp"], 1)
            dve.tensor_tensor(t_lo[:, second], tT[:, second], t_hi[:, second], ALU.subtract).then_inc(s["sp"], 1)
            n = [0]

            def step(ins):
                n[0] += 1
                ins.then_inc(s["rt"], 1)
                dve.wait_ge(s["rt"], n[0])

            def per_expert_of(ap):
                return ap.to_broadcast([P, NT, E])

            def route(part):
                if part == 0:
                    for h in range(2):
                        if h:
                            dve.wait_ge(s["nrm"], 1)
                        dots = small[:, 0, 0:4 * E] if h else keep.dots[:, E:5 * E]
                        step(dve.scalar_tensor_tensor(
                            out=dist2[:, 4 * h:4 * h + 4, :], in0=dots.rearrange("p (t e) -> p t e", e=E),
                            scalar=-2.0, in1=keep.dots[:, 0:E].unsqueeze(1).to_broadcast([P, 4, E]),
                            op0=ALU.mult, op1=ALU.add))
                    step(dve.tensor_tensor(dist2[:], dist2[:], per_expert_of(norms[:].unsqueeze(2)), ALU.add))
                    step(dve.tensor_scalar(dist2[:], dist2[:], 1e-12, None, ALU.max))
                    for t in range(NT):
                        dve.max(top[:, t, :], dist2[:, t, :]).then_inc(s["top"], 1)
                    dve.wait_ge(s["top"], NT)
                    dve.tensor_copy(far[:], top[:, :, 0:2]).then_inc(s["top"], 1)
                    for t in range(NT):
                        last = dve.max_index(top_i[:, t, :], top[:, t, :], dist2[:, t, :])
                    last.then_inc(s["top"], 1)
                    dve.wait_ge(s["te"], 1)
                    step(dve.tensor_tensor(gap[:], far[:, :, 1], far[:, :, 0], ALU.subtract))
                if part == 4:
                    dve.wait_ge(s["b2"], 1)
                    dve.wait_ge(s["acc"], 2 * E)
                    dve.tensor_tensor(acc[:], acc[:], small[:].rearrange("p h (t c) -> p (h t) c", c=P),
                                      ALU.add).then_inc(s["sel"], 1)
                    dve.wait_ge(s["sel"], 2)
                if part != 2:
                    return
                dve.wait_ge(s["top"], NT + 2)
                step(dve.tensor_copy(top_f[:], top_i[:, :, 0:2]))
                dve.wait_ge(s["te"], 2)
                step(dve.tensor_scalar(wts[:, :, 0], gap[:], -0.5, 0.5, ALU.mult, ALU.add))
                step(dve.tensor_scalar(wts[:, :, 1], gap[:], 0.5, 0.5, ALU.mult, ALU.add))
                for k, to in ((0, pick), (1, we)):
                    step(dve.tensor_tensor(to[:], per_expert_of(keep.iota[:].unsqueeze(1)),
                                           per_expert_of(top_f[:, :, k:k + 1]), ALU.is_equal))
                    step(dve.tensor_tensor(to[:], to[:], per_expert_of(wts[:, :, k:k + 1]), ALU.mult))
                dve.tensor_tensor(we[:], we[:], pick[:], ALU.add).then_inc(s["sel"], 1)
                dve.wait_ge(s["sel"], 1)

            def weigh(e, h, part):
                if part == 0:
                    return
                dve.wait_ge(s["down"], e * 2 + (h + 1))
                for t in range(4):
                    k = 4 * h + t
                    last = dve.scalar_tensor_tensor(
                        out=acc[:, k, :], in0=down[:, h, P * t:P * t + P],
                        scalar=we[:, k, bass.ds(e, 1)], in1=acc[:, k, :], op0=ALU.mult, op1=ALU.add)
                last.then_inc(s["acc"], 1)

            def hidden(e, h, par, between):
                for n in range(NH):
                    w = (3 * h + n) % 2
                    dve.wait_ge(s["gate"], e * 6 + (3 * h + n + 1))
                    dve.scalar_tensor_tensor(
                        out=hid[:, h, n, :], in0=gu[0:HT, w, 1, :],
                        scalar=bgu[:, bass.ds(e, 1), 1, n:n + 1].rearrange("p e c -> p (e c)"),
                        in1=gate[:, w, :], op0=ALU.add, op1=ALU.mult).then_inc(s["hid"], 1)
                if between:
                    between(1)

            per_expert(dve, hidden, weigh, route)


class Keep:
    pass


def program(nc, A, out):
    with ExitStack() as ctx:
        def sb(name, shape, dt=F32):
            return ctx.enter_context(nc.sbuf_tensor("keep_" + name, shape, dt))

        keep = Keep()
        keep.x = sb("x", [P, NT, P])
        keep.ident = sb("ident", [P, P])
        keep.marks = sb("marks", [P, GH + 2])
        keep.vecs = sb("vecs", [P, NV])
        keep.rows = sb("rows", [P, NR])
        keep.iota = sb("iota", [P, E])
        keep.sums = sb("sums", [P, GH, T])
        keep.wo = sb("wo", [P, P])
        keep.win = sb("win", [P, 644])
        keep.wout = sb("wout", [P, 2, P])
        keep.wfc = sb("wfc", [P, 4 * P])
        keep.wproj = sb("wproj", [P, 4, P])
        attention(nc, A, keep)
        keep.tT = sb("tT", [P, T])
        keep.w_hi = sb("w_hi", [P, E, 2, NH * HT], BF16)
        keep.w_lo = sb("w_lo", [P, E, 2, NH * HT], BF16)
        keep.bgu = sb("bgu", [HT, E, 2, NH])
        keep.b2 = sb("b2", [E, P])
        keep.cent = sb("cent", [P, E])
        keep.cent_sq = sb("cent_sq", [P, E])
        keep.ones = sb("ones", [P, P])
        keep.norms = sb("norms", [P, NT])
        keep.dots = sb("dots", [P, 5 * E])
        keep.t_hi = sb("t_hi", [P, T], BF16)
        keep.t_lo = sb("t_lo", [P, T], BF16)
        keep.w2 = sb("w2", [HT, E, NH, P])
        mamba_mlp(nc, A, keep)
        experts(nc, A, keep, out)


def lay_out(a):
    import numpy as np
    f = np.float32
    g = {k.replace("L0_", ""): np.asarray(v) for k, v in a.items()}
    wq = np.zeros((P, G, 4, GH, HD), f)
    bq = np.zeros((4, GH, HD, G), f)
    wq[:, :, :3] = g["xattn_Wq"].T.reshape(P, G, 1, GH, HD)
    bq[:3] = g["xattn_bq"].reshape(G, GH, HD).transpose(1, 2, 0)
    marks = np.zeros((4, GH, HD, GH + 2), f)
    for h in range(GH):
        marks[:3, h, :, h] = 1
    marks[1, :, :, GH] = -1
    marks[0, 1, :, GH + 1] = -1

    wk = g["xattn_Wk"].T.reshape(P, G, GH, HD).transpose(0, 2, 3, 1)
    bk = g["xattn_bk"].reshape(G, GH, HD).transpose(1, 2, 0)

    def cols(v):
        return v.reshape(-1, P).T

    conv = g["attn_conv_w"].reshape(3, P, 4).transpose(1, 0, 2).reshape(P, 12)
    vecs = np.concatenate([
        cols(bk.reshape(-1)), bq.reshape(P, G), cols(g["attn_ln1_w"]), cols(g["attn_ln1_b"]),
        cols(g["attn_ln2_w"]), cols(g["attn_ln2_b"]), conv, cols(g["attn_conv_b"]),
        cols(np.repeat(g["attn_D_param"], 64)), cols(g["attn_norm_w"]), cols(g["attn_fc_b"])], 1)
    rows = np.concatenate([g["xattn_bv"], g["xattn_bo"], g["attn_proj_b"], g["attn_A_log"],
                           g["attn_dt_bias"]])[None]
    c = np.ascontiguousarray
    return {
        "x": c(g["x"].reshape(T, P)),
        "ctx": c(g["ctx_1024"].transpose(2, 0, 1)),
        "ident": np.eye(P, dtype=f),
        "nident": -np.eye(P, dtype=f),
        "marks": marks.reshape(P, GH + 2),
        "vecs": c(vecs),
        "iota": np.tile(np.arange(E, dtype=f), (P, 1)),
        "sel": c(np.broadcast_to(np.tile(np.eye(MH, dtype=f), (3, 1))[:, :, None], (3 * MH, MH, P))),
        "rows": c(rows),
        "wkv": c(np.stack([wk.reshape(P, P), g["xattn_Wv"].T], 1)),
        "wq": wq.reshape(P, G, P),
        "wo": c(g["xattn_Wo"].T),
        "win": c(g["attn_in_proj_w"].T),
        "wout": c(g["attn_out_proj_w"].T.reshape(2, P, P).transpose(1, 0, 2)),
        "wfc": c(g["attn_fc_w"].T),
        "wproj": c(g["attn_proj_w"].T.reshape(4, P, P).transpose(1, 0, 2)),
        "cent": c(g["ffn_centroid"].T),
        "wgu": c(np.stack([g["ffn_Wg"], g["ffn_W1"]], 0).transpose(2, 1, 0, 3)),
        "bgu": c(np.stack([g["ffn_bg"], g["ffn_b1"]], 0).reshape(2, E, NH, HT).transpose(3, 1, 0, 2)),
        "w2": c(g["ffn_W2"].reshape(E, NH, HT, P).transpose(2, 0, 1, 3)),
        "b2": c(g["ffn_b2"]),
    }


def kernel(**inputs):
    import numpy as np
    import concourse.bacc as bacc
    from concourse.bass_utils import run_bass_kernel_spmd

    nc = bacc.Bacc("TRN2", target_bir_lowering=False, num_devices=1)
    arrays = lay_out(inputs)
    aps = {k: nc.dram_tensor(f"in_{k}", v.shape, F32, kind="ExternalInput").ap()
           for k, v in arrays.items()}
    out = nc.dram_tensor("out_0", (T, P), F32, kind="ExternalOutput").ap()
    program(nc, aps, out)
    r = run_bass_kernel_spmd(nc, [{f"in_{k}": v for k, v in arrays.items()}], core_ids=[0])
    return np.asarray(r.results[0]["out_0"]).reshape(B, LQ, P)
```
